# Optimizing a Trainium2 kernel written in Bass

```python
import numpy as np
import jax
import jax.numpy as jnp

def _softmax(x, axis=-1):
    return jax.nn.softmax(x, axis=axis)

def _gelu(x):
    return jax.nn.gelu(x, approximate=True)

def _silu(x):
    return jax.nn.silu(x)

def _sigmoid(x):
    return jax.nn.sigmoid(x)

def _layernorm(x, axis=-1, eps=1e-05):
    m = jnp.mean(x, axis=axis, keepdims=True)
    v = jnp.var(x, axis=axis, keepdims=True)
    return (x - m) / jnp.sqrt(v + eps)

def _scatter_add(tgt, idx, src, axis=0):
    return tgt.at[idx].add(src)

def _segment_sum(src, seg, n):
    return jax.ops.segment_sum(src, seg, n)
kernel_name = 'mk_seq_postln_d2_jaxref_r8_17a64d'

def setup_inputs(seed: int=0):
    np.random.seed(seed)
    _w = jnp.asarray

    def _L0_attn_setup():
        import jax, jax.numpy as jnp
        import numpy as np
        EMB = 128
        HEADS = 16
        HEADSIZE = EMB // HEADS
        EPS = 1e-05

        def _layernorm(x, g, b):
            m = jnp.mean(x, axis=-1, keepdims=True)
            v = jnp.mean((x - m) ** 2, axis=-1, keepdims=True)
            return (x - m) * jax.lax.rsqrt(v + EPS) * g + b
        key = jax.random.key(seed)
        ks = jax.random.split(key, 6)
        B, T = (4, 256)
        s = 1.0 / np.sqrt(EMB)
        return {'x': jax.random.normal(ks[0], (B, T, EMB), dtype=jnp.float32), 'Wk': jax.random.normal(ks[1], (EMB, EMB), dtype=jnp.float32) * s, 'Wq': jax.random.normal(ks[2], (EMB, EMB), dtype=jnp.float32) * s, 'Wv': jax.random.normal(ks[3], (EMB, EMB), dtype=jnp.float32) * s, 'Wo': jax.random.normal(ks[4], (EMB, EMB), dtype=jnp.float32) * s, 'bo': jnp.zeros((EMB,), dtype=jnp.float32), 'kln_g': jnp.ones((HEADSIZE,), dtype=jnp.float32), 'kln_b': jnp.zeros((HEADSIZE,), dtype=jnp.float32), 'qln_g': jnp.ones((HEADSIZE,), dtype=jnp.float32), 'qln_b': jnp.zeros((HEADSIZE,), dtype=jnp.float32)}
    _L0_attn_in = _L0_attn_setup()

    def _L0_ffn_setup():
        import jax, jax.numpy as jnp
        import numpy as np
        EPS = 1e-12

        def rms_norm(t, gamma):
            n = jnp.maximum(jnp.linalg.norm(t, axis=-1, keepdims=True), EPS)
            scale = jnp.sqrt(jnp.asarray(t.shape[-1], t.dtype))
            return t / n * scale * gamma
        key = jax.random.key(seed)
        ks = jax.random.split(key, 4)
        b, s, d = (4, 512, 128)
        e, t = (8, 64)
        hidden = 4 * d
        return {'x': jax.random.normal(ks[0], (b, s, d), dtype=jnp.float32), 'gamma_x': jnp.ones((d,), dtype=jnp.float32), 'gamma_slot': jnp.ones((d,), dtype=jnp.float32), 'slot_embeds': jax.random.normal(ks[1], (e, t, d), dtype=jnp.float32), 'w1': jax.random.normal(ks[2], (d, hidden), dtype=jnp.float32) * (1.0 / np.sqrt(d)), 'w2': jax.random.normal(ks[3], (hidden, d), dtype=jnp.float32) * (1.0 / np.sqrt(hidden))}
    _L0_ffn_in = _L0_ffn_setup()

    def _L1_attn_setup():
        import jax, jax.numpy as jnp
        import numpy as np
        EPS = 1e-06
        H = 16

        def rmsnorm(x, w):
            return x * jax.lax.rsqrt(jnp.mean(x * x, axis=-1, keepdims=True) + EPS) * w

        def l2norm(x):
            return x * jax.lax.rsqrt(jnp.sum(x * x, axis=-1, keepdims=True) + EPS)

        def delta_rule(q, k, v, beta):
            B, S, Hh, dk = q.shape
            dv = v.shape[-1]
            qt = jnp.moveaxis(q, 1, 0)
            kt = jnp.moveaxis(k, 1, 0)
            vt = jnp.moveaxis(v, 1, 0)
            bt = jnp.moveaxis(beta, 1, 0)

            def step(Sm, inp):
                qi, ki, vi, bi = inp
                Sk = jnp.einsum('bhkv,bhk->bhv', Sm, ki)
                upd = ki[..., :, None] * (vi - Sk)[..., None, :]
                Sm = Sm + bi[..., None, None] * upd
                oi = jnp.einsum('bhkv,bhk->bhv', Sm, qi)
                return (Sm, oi)
            S0 = jnp.zeros((B, Hh, dk, dv), q.dtype)
            _, out = jax.lax.scan(step, S0, (qt, kt, vt, bt))
            return jnp.moveaxis(out, 0, 1)
        key = jax.random.key(seed)
        ks = jax.random.split(key, 12)
        B, S, D, F = (2, 256, 128, 512)
        std = 0.02
        inp = {'hidden_states': jax.random.normal(ks[0], (B, S, D), jnp.float32), 'Wq': jax.random.normal(ks[1], (D, D), jnp.float32) * std, 'Wk': jax.random.normal(ks[2], (D, D), jnp.float32) * std, 'Wv': jax.random.normal(ks[3], (D, D), jnp.float32) * std, 'Wb': jax.random.normal(ks[4], (D, H), jnp.float32) * std, 'Wo': jax.random.normal(ks[5], (D, D), jnp.float32) * std, 'ln1': jnp.ones((D,), jnp.float32), 'ln2': jnp.ones((D,), jnp.float32), 'Wg': jax.random.normal(ks[6], (D, F), jnp.float32) * std, 'Wu': jax.random.normal(ks[7], (D, F), jnp.float32) * std, 'Wd': jax.random.normal(ks[8], (F, D), jnp.float32) * std}
        return inp
    _L1_attn_in = _L1_attn_setup()

    def _L1_ffn_setup():
        import jax, jax.numpy as jnp
        import numpy as np
        D_IN, D_HID = (128, 512)

        def _ternary(key, shape):
            return jax.random.randint(key, shape, -1, 2).astype(jnp.float32)

        def _tlin(x, w, s):
            return jnp.einsum('bsi,oi->bso', x, w) * s
        key = jax.random.key(seed)
        ks = jax.random.split(key, 12)
        inv = lambda fan: 1.0 / np.sqrt(fan).astype(np.float32)
        return {'x': jax.random.normal(ks[0], (4, 256, D_IN), dtype=jnp.float32), 'w1_w': _ternary(ks[1], (D_HID, D_IN)), 'w1_s': jax.random.uniform(ks[2], (D_HID,), dtype=jnp.float32) * inv(D_IN), 'w2_w': _ternary(ks[3], (D_HID, D_IN)), 'w2_s': jax.random.uniform(ks[4], (D_HID,), dtype=jnp.float32) * inv(D_IN), 'h1_w': _ternary(ks[5], (D_HID, D_HID)), 'h1_s': jax.random.uniform(ks[6], (D_HID,), dtype=jnp.float32) * inv(D_HID), 'h2_w': _ternary(ks[7], (D_HID, D_HID)), 'h2_s': jax.random.uniform(ks[8], (D_HID,), dtype=jnp.float32) * inv(D_HID), 'w3_w': _ternary(ks[9], (D_IN, D_HID)), 'w3_s': jax.random.uniform(ks[10], (D_IN,), dtype=jnp.float32) * inv(D_HID)}
    _L1_ffn_in = _L1_ffn_setup()
    _d = {'L0_attn_x': _L0_attn_in['x'], 'L0_attn_Wk': _L0_attn_in['Wk'], 'L0_attn_Wq': _L0_attn_in['Wq'], 'L0_attn_Wv': _L0_attn_in['Wv'], 'L0_attn_Wo': _L0_attn_in['Wo'], 'L0_attn_bo': _L0_attn_in['bo'], 'L0_attn_kln_g': _L0_attn_in['kln_g'], 'L0_attn_kln_b': _L0_attn_in['kln_b'], 'L0_attn_qln_g': _L0_attn_in['qln_g'], 'L0_attn_qln_b': _L0_attn_in['qln_b'], 'L0_ffn_gamma_x': _L0_ffn_in['gamma_x'], 'L0_ffn_gamma_slot': _L0_ffn_in['gamma_slot'], 'L0_ffn_slot_embeds': _L0_ffn_in['slot_embeds'], 'L0_ffn_w1': _L0_ffn_in['w1'], 'L0_ffn_w2': _L0_ffn_in['w2'], 'L1_attn_Wq': _L1_attn_in['Wq'], 'L1_attn_Wk': _L1_attn_in['Wk'], 'L1_attn_Wv': _L1_attn_in['Wv'], 'L1_attn_Wb': _L1_attn_in['Wb'], 'L1_attn_Wo': _L1_attn_in['Wo'], 'L1_attn_ln1': _L1_attn_in['ln1'], 'L1_attn_ln2': _L1_attn_in['ln2'], 'L1_attn_Wg': _L1_attn_in['Wg'], 'L1_attn_Wu': _L1_attn_in['Wu'], 'L1_attn_Wd': _L1_attn_in['Wd'], 'L1_ffn_w1_w': _L1_ffn_in['w1_w'], 'L1_ffn_w1_s': _L1_ffn_in['w1_s'], 'L1_ffn_w2_w': _L1_ffn_in['w2_w'], 'L1_ffn_w2_s': _L1_ffn_in['w2_s'], 'L1_ffn_h1_w': _L1_ffn_in['h1_w'], 'L1_ffn_h1_s': _L1_ffn_in['h1_s'], 'L1_ffn_h2_w': _L1_ffn_in['h2_w'], 'L1_ffn_h2_s': _L1_ffn_in['h2_s'], 'L1_ffn_w3_w': _L1_ffn_in['w3_w'], 'L1_ffn_w3_s': _L1_ffn_in['w3_s']}
    _x0 = _d['L0_attn_x']
    _d['L0_attn_x'] = jax.random.normal(jax.random.fold_in(jax.random.key(seed), 1), (8, 512, 128), dtype=_x0.dtype)
    del _x0
    return _d

def reference(L0_attn_x, L0_attn_Wk, L0_attn_Wq, L0_attn_Wv, L0_attn_Wo, L0_attn_bo, L0_attn_kln_g, L0_attn_kln_b, L0_attn_qln_g, L0_attn_qln_b, L0_ffn_gamma_x, L0_ffn_gamma_slot, L0_ffn_slot_embeds, L0_ffn_w1, L0_ffn_w2, L1_attn_Wq, L1_attn_Wk, L1_attn_Wv, L1_attn_Wb, L1_attn_Wo, L1_attn_ln1, L1_attn_ln2, L1_attn_Wg, L1_attn_Wu, L1_attn_Wd, L1_ffn_w1_w, L1_ffn_w1_s, L1_ffn_w2_w, L1_ffn_w2_s, L1_ffn_h1_w, L1_ffn_h1_s, L1_ffn_h2_w, L1_ffn_h2_s, L1_ffn_w3_w, L1_ffn_w3_s):

    def _L0_attn_ref(x, Wk, Wq, Wv, Wo, bo, kln_g, kln_b, qln_g, qln_b):
        import jax, jax.numpy as jnp
        import numpy as np
        EMB = 128
        HEADS = 16
        HEADSIZE = EMB // HEADS
        EPS = 1e-05

        def _layernorm(x, g, b):
            m = jnp.mean(x, axis=-1, keepdims=True)
            v = jnp.mean((x - m) ** 2, axis=-1, keepdims=True)
            return (x - m) * jax.lax.rsqrt(v + EPS) * g + b
        B, T, E = x.shape
        k = jnp.einsum('bte,fe->btf', x, Wk).reshape(B, T, HEADS, HEADSIZE)
        q = jnp.einsum('bte,fe->btf', x, Wq).reshape(B, T, HEADS, HEADSIZE)
        v = jnp.einsum('bte,fe->btf', x, Wv).reshape(B, T, HEADS, HEADSIZE)
        k = _layernorm(k, kln_g, kln_b)
        q = _layernorm(q, qln_g, qln_b)
        scale = E ** (-0.25)
        q = q * scale
        k = k * scale
        dot = jnp.einsum('bihd,bjhd->bhij', q, k)
        causal = jnp.triu(jnp.ones((T, T), dtype=bool), k=1)
        dot = jnp.where(causal, -jnp.inf, dot)
        att = jax.nn.softmax(dot, axis=-1)
        out = jnp.einsum('bhij,bjhd->bihd', att, v).reshape(B, T, E)
        return jnp.einsum('bte,fe->btf', out, Wo) + bo

    def _L0_ffn_ref(x, gamma_x, gamma_slot, slot_embeds, w1, w2):
        import jax, jax.numpy as jnp
        import numpy as np
        EPS = 1e-12

        def rms_norm(t, gamma):
            n = jnp.maximum(jnp.linalg.norm(t, axis=-1, keepdims=True), EPS)
            scale = jnp.sqrt(jnp.asarray(t.shape[-1], t.dtype))
            return t / n * scale * gamma
        b, s, d = x.shape
        e, t, _ = slot_embeds.shape
        xn = rms_norm(x, gamma_x)
        se = rms_norm(slot_embeds, gamma_slot)
        logits = jnp.einsum('bsd,etd->bset', xn, se)
        dispatch = jax.nn.softmax(logits, axis=1)
        slots = jnp.einsum('bsd,bset->betd', xn, dispatch)
        h = jax.nn.gelu(slots @ w1, approximate=False)
        processed = h @ w2
        combine = jax.nn.softmax(logits.reshape(b, s, e * t), axis=-1)
        out = jnp.einsum('bnd,bsn->bsd', processed.reshape(b, e * t, d), combine)
        return out

    def _L1_attn_ref(hidden_states, Wq, Wk, Wv, Wb, Wo, ln1, ln2, Wg, Wu, Wd):
        import jax, jax.numpy as jnp
        import numpy as np
        EPS = 1e-06
        H = 16

        def rmsnorm(x, w):
            return x * jax.lax.rsqrt(jnp.mean(x * x, axis=-1, keepdims=True) + EPS) * w

        def l2norm(x):
            return x * jax.lax.rsqrt(jnp.sum(x * x, axis=-1, keepdims=True) + EPS)

        def delta_rule(q, k, v, beta):
            B, S, Hh, dk = q.shape
            dv = v.shape[-1]
            qt = jnp.moveaxis(q, 1, 0)
            kt = jnp.moveaxis(k, 1, 0)
            vt = jnp.moveaxis(v, 1, 0)
            bt = jnp.moveaxis(beta, 1, 0)

            def step(Sm, inp):
                qi, ki, vi, bi = inp
                Sk = jnp.einsum('bhkv,bhk->bhv', Sm, ki)
                upd = ki[..., :, None] * (vi - Sk)[..., None, :]
                Sm = Sm + bi[..., None, None] * upd
                oi = jnp.einsum('bhkv,bhk->bhv', Sm, qi)
                return (Sm, oi)
            S0 = jnp.zeros((B, Hh, dk, dv), q.dtype)
            _, out = jax.lax.scan(step, S0, (qt, kt, vt, bt))
            return jnp.moveaxis(out, 0, 1)
        B, S, D = hidden_states.shape
        dk = D // H
        x = rmsnorm(hidden_states, ln1)
        q = l2norm(jax.nn.silu(x @ Wq).reshape(B, S, H, dk))
        k = l2norm(jax.nn.silu(x @ Wk).reshape(B, S, H, dk))
        v = jax.nn.silu(x @ Wv).reshape(B, S, H, dk)
        beta = jax.nn.sigmoid(x @ Wb)
        o = delta_rule(q, k, v, beta).reshape(B, S, D)
        h = hidden_states + o @ Wo
        y = rmsnorm(h, ln2)
        h = h + jax.nn.silu(y @ Wg) * (y @ Wu) @ Wd
        return h

    def _L1_ffn_ref(x, w1_w, w1_s, w2_w, w2_s, h1_w, h1_s, h2_w, h2_s, w3_w, w3_s):
        import jax, jax.numpy as jnp
        import numpy as np
        D_IN, D_HID = (128, 512)

        def _ternary(key, shape):
            return jax.random.randint(key, shape, -1, 2).astype(jnp.float32)

        def _tlin(x, w, s):
            return jnp.einsum('bsi,oi->bso', x, w) * s
        h = jax.nn.silu(_tlin(x, w1_w, w1_s)) * _tlin(x, w2_w, w2_s)
        h = jax.nn.gelu(_tlin(h, h1_w, h1_s), approximate=False)
        h = jax.nn.gelu(_tlin(h, h2_w, h2_s), approximate=False)
        return _tlin(h, w3_w, w3_s)
    x = L0_attn_x
    x = _layernorm(x + _L0_attn_ref(x, L0_attn_Wk, L0_attn_Wq, L0_attn_Wv, L0_attn_Wo, L0_attn_bo, L0_attn_kln_g, L0_attn_kln_b, L0_attn_qln_g, L0_attn_qln_b), axis=-1)
    x = _layernorm(x + _L0_ffn_ref(x, L0_ffn_gamma_x, L0_ffn_gamma_slot, L0_ffn_slot_embeds, L0_ffn_w1, L0_ffn_w2), axis=-1)
    x = _layernorm(x + _L1_attn_ref(x, L1_attn_Wq, L1_attn_Wk, L1_attn_Wv, L1_attn_Wb, L1_attn_Wo, L1_attn_ln1, L1_attn_ln2, L1_attn_Wg, L1_attn_Wu, L1_attn_Wd), axis=-1)
    x = _layernorm(x + _L1_ffn_ref(x, L1_ffn_w1_w, L1_ffn_w1_s, L1_ffn_w2_w, L1_ffn_w2_s, L1_ffn_h1_w, L1_ffn_h1_s, L1_ffn_h2_w, L1_ffn_h2_s, L1_ffn_w3_w, L1_ffn_w3_s), axis=-1)
    return x

_drawn_inputs = setup_inputs


def setup_inputs(seed=0):
    import zlib

    import numpy as np

    out = dict(_drawn_inputs(seed))
    spreads = {'L0_attn_bo': (0.0, 0.1),
     'L0_attn_kln_g': (1.0, 0.6),
     'L0_attn_kln_b': (0.0, 0.8),
     'L0_attn_qln_g': (1.0, 0.6),
     'L0_attn_qln_b': (0.0, 0.8),
     'L0_ffn_gamma_x': (1.0, 0.2),
     'L0_ffn_gamma_slot': (1.0, 0.2),
     'L1_attn_ln1': (1.0, 0.6),
     'L1_attn_ln2': (1.0, 0.6)}
    factors = {'L1_attn_Wq': 6.74,
     'L1_attn_Wk': 6.761,
     'L1_attn_Wv': 6.85,
     'L1_attn_Wb': 8.0,
     'L1_attn_Wo': 6.787,
     'L1_attn_Wg': 8.0,
     'L1_attn_Wu': 8.0,
     'L1_attn_Wd': 8.0,
     'L1_ffn_w1_w': 8.0,
     'L1_ffn_w1_s': 8.0,
     'L1_ffn_w2_w': 8.0,
     'L1_ffn_w2_s': 8.0,
     'L1_ffn_h1_w': 8.0,
     'L1_ffn_h1_s': 8.0,
     'L1_ffn_h2_w': 8.0,
     'L1_ffn_h2_s': 8.0,
     'L1_ffn_w3_w': 8.0,
     'L1_ffn_w3_s': 8.0}
    for name, (base, spread) in spreads.items():
        noise = np.random.default_rng([zlib.crc32(name.encode()), seed]).standard_normal(out[name].shape)
        drawn = base * np.exp(spread * noise) if base else spread * noise
        out[name] = jnp.asarray(drawn.astype(out[name].dtype))
    for name, factor in factors.items():
        out[name] = (out[name] * factor).astype(out[name].dtype)
    return out
```

```python
from contextlib import ExitStack

import numpy as np
import concourse.bass as bass
from concourse import mybir

F32 = mybir.dt.float32
F32R = mybir.dt.float32r
BF16 = mybir.dt.bfloat16
I32 = mybir.dt.int32
ALU = mybir.AluOpType
ACT = mybir.ActivationFunctionType
X = mybir.AxisListType.X

P = 128
B, S, D = 8, 512, 128
NT = S // P
NH, HD = 16, 8
NG = NH // 4
NE, NS = 8, 64
N = NE * NS
HID = 512
HC = HID // P
QW = 3 * D + NH
CH = 4
NC = P // CH
LN_EPS = 1e-5
MASK = -1e30
RSQRT_SEED = 1597463007.0
CREDIT = 1


class Handoff:

    def __init__(self, ready, taken, banks, uses):
        self.ready, self.taken, self.banks = ready, taken, banks
        self.order = [u for u, _ in uses]
        self.engine = dict(uses)
        self.total = {e: sum(x == e for _, x in uses) for e in taken}
        self.ordinal = {}
        seen = {e: 0 for e in taken}
        for u, e in uses:
            seen[e] += 1
            self.ordinal[u] = seen[e]

    def bank(self, use):
        return self.banks[self.order.index(use) % len(self.banks)]

    def filled(self, use, i):
        return i * len(self.order) + self.order.index(use) + 1

    def emptied(self, use, i):
        return i * self.total[self.engine[use]] + self.ordinal[use]

    def wait_free(self, pe, use, i):
        k = self.order.index(use) - len(self.banks)
        if k >= 0:
            before = self.order[k]
            pe.wait_ge(self.taken[self.engine[before]], CREDIT + self.emptied(before, i))
        else:
            for e, n in self.total.items():
                if n:
                    pe.wait_ge(self.taken[e], CREDIT + i * n)


class Order:

    def __init__(self, eng, done, per, i, first):
        self.eng, self.sem, self.base, self.n, self.first = eng, done, i * per, 0, first
        self.per = per

    def mark(self, ins):
        ins.then_inc(self.sem, 1)
        self.n += 1

    def settle(self):
        self.eng.wait_ge(self.sem, self.first + self.base + self.n)

    def step(self, ins):
        self.mark(ins)
        self.settle()

    def end(self, name):
        assert self.n == self.per, (name, self.n, self.per)


def build(nc, A, out, taps=None):
    ctx = ExitStack()
    with ctx:
        def sb(name, shape, dt=F32):
            return ctx.enter_context(nc.sbuf_tensor(name, shape, dt))

        def sem(name):
            return ctx.enter_context(nc.semaphore(name))

        ps = ctx.enter_context(nc.psum_tensor("ps", [P, 8, 512], F32))

        q_rep = nc.dram_tensor("q_rep", (NH, 4, HD, S), F32, kind="Internal").ap()
        k_rep = nc.dram_tensor("k_rep", (NH, 4, HD, S), F32, kind="Internal").ap()
        proj_d = nc.dram_tensor("proj_d", (B, NT, P, QW), F32, kind="Internal").ap()
        x2_d = nc.dram_tensor("x2_d", (B, NT, P, D), F32, kind="Internal").ap()

        ident = sb("ident", [P, P])
        ident_b = sb("ident_b", [P, P], BF16)
        mask_qk = sb("mask_qk", [P, P], BF16)
        mask_kq = sb("mask_kq", [P, P], BF16)
        w_qkv = sb("w_qkv", [P, 3 * D])
        w_out = sb("w_out", [P, D])
        bias_o = sb("bias_o", [P, D])
        qk_gb = sb("qk_gb", [P, 4])
        slot_T = sb("slot_T", [P, N])
        gamma_x = sb("gamma_x", [P, 1])
        gamma_s = sb("gamma_s", [P, 1])
        e_w1 = sb("e_w1", [P, HID])
        e_w2 = sb("e_w2", [P, HC, D])
        w_mix = sb("w_mix", [P, QW])
        w_o1 = sb("w_o1", [P, D])
        ln12 = sb("ln12", [P, 2])
        w_g = sb("w_g", [P, HID])
        w_u = sb("w_u", [P, HID])
        w_d = sb("w_d", [P, HC, D])
        f_w1 = sb("f_w1", [P, HID])
        f_w2 = sb("f_w2", [P, HID])
        f_h1 = sb("f_h1", [P, HC, HID])
        f_h2 = sb("f_h2", [P, HC, HID])
        f_w3 = sb("f_w3", [P, HC, D])
        f_s = sb("f_s", [P, 4, HC])
        f_s3 = sb("f_s3", [P, 1])

        ARENA = 34 * 1024
        arena = sb("arena", [P, ARENA])
        qr = sb("qr", [P, NG, S], F32R)
        kr = sb("kr", [P, NG, S], F32R)

        class Carve:
            def __init__(self):
                self.at = 0

            def take(self, *shape):
                n = int(np.prod(shape))
                ap = arena[:, self.at:self.at + n]
                self.at += n
                assert self.at <= ARENA, self.at
                if len(shape) == 2:
                    return ap.rearrange("p (a b) -> p a b", a=shape[0])
                if len(shape) == 3:
                    return ap.rearrange("p (a b c) -> p a b c", a=shape[0], b=shape[1])
                if len(shape) == 4:
                    return ap.rearrange("p (a b c d) -> p a b c d", a=shape[0], b=shape[1], c=shape[2])
                return ap

        c0 = Carve()
        raw_w = c0.take(4, P)
        raw_slot = c0.take(4, P)
        raw_f1 = c0.take(4, P)
        raw_f2 = c0.take(4, P)
        raw_h1 = c0.take(4, HID)
        raw_h2 = c0.take(4, HID)
        raw_w3 = c0.take(HID)
        centre = c0.take(2 * NH)
        slot_sq = c0.take(4, P)
        slot_n = c0.take(4)
        slot_r = c0.take(4)
        slot_t = c0.take(4)
        ones_zeros = c0.take(2, S)

        c1 = Carve()
        xb = c1.take(NT, D)
        xbo = c1.take(NT, D)
        act_T = c1.take(S)
        qk = c1.take(NT, 2 * D)
        qk_sq = c1.take(NT, 2 * D)
        qk_n = c1.take(NT, 2 * D)
        qk_var = c1.take(P)
        qk_r = c1.take(P)
        qk_t = c1.take(P)
        qk_T = c1.take(2, S)
        v_aug = c1.take(NT, NH, HD + 1)
        neg_max = c1.take(NT, NH)
        prob = c1.take(2, 4, 1280)
        rec = c1.take(NT, 4)
        att = c1.take(NT, D)
        y1 = c1.take(NT, D)
        y_sq = c1.take(NT, D)
        x1 = c1.take(NT, D)
        x2 = c1.take(NT, D)
        st = c1.take(8, NT)
        xr = c1.take(NT, D)
        neg_top = c1.take(2, 4)
        z_sum = c1.take(2, 4)
        z_inv = c1.take(2, 4)
        comb = c1.take(NT, N)
        comb_T = c1.take(4, S)
        disp_T = c1.take(4, S)
        disp = c1.take(NT, N)
        slots_n = c1.take(4, D)
        slots = c1.take(N)
        h_T = c1.take(HC, N)
        done_e = c1.take(4, D)
        proj = c1.take(NT, QW)
        hilo = sb("hilo", [P, 2, 2, S], F32R)
        nm_T = sb("nm_T", [NH, S], F32R)

        c2 = Carve()
        mix = c2.take(B, QW)
        x2t = c2.take(B, D)
        l_sq = c2.take(B, 2 * D)
        l_var = c2.take(B * 2 * NH)
        l_r = c2.take(B * 2 * NH)
        l_t = c2.take(B * 2 * NH)
        perm = c2.take(3, HD, B * NH)
        beta_p = c2.take(B * NH)
        q_c = c2.take(P, HD)
        k_c = c2.take(P, HD)
        v_c = c2.take(P, HD)
        beta = c2.take(P)
        wu = c2.take(P, 2 * HD)
        gram = c2.take(NC, CH * CH)
        qkd = c2.take(NC, CH * CH)
        tmp = c2.take(2048)
        state = c2.take(NC + 1, HD, HD)
        s_m = c2.take(CH, HD, HD)
        s_w = c2.take(CH, HD)
        s_n = c2.take(HD, HD, CH)
        s_d = c2.take(HD, HD)
        u_c = c2.take(P, HD)
        o_m = c2.take(NC, HD, HD + CH)
        o_c = c2.take(HD, P)
        o_tok = c2.take(B, D)
        o_T = c2.take(B, P)
        h1 = c2.take(B, D)
        hn = o_tok
        hn_T = c2.take(B, P)
        y3 = c2.take(4, D)
        y3_sq = c2.take(4, D)
        x3 = c2.take(4, D)
        x3_T = c2.take(S)
        y4 = y3
        x4 = c2.take(4, D)
        gate = c2.take(2, S)
        hid_a = l_sq.rearrange("p b w -> p (b w)").rearrange("p (c s) -> p c s", c=HC)
        hid_b = tmp.rearrange("p (c s) -> p c s", c=HC)
        st2 = c2.take(8, B)

        w_loaded = sem("w_loaded")
        consts = sem("consts")
        w_ready = sem("w_ready")
        w_taken = sem("w_taken")
        w_final = sem("w_final")
        rep_init = sem("rep_init")
        pool_done, act_done, dve_done = sem("pool_done"), sem("act_done"), sem("dve_done")
        x_loaded = sem("x_loaded")
        x_biased = sem("x_biased")
        t_ready, t_act, t_dve = sem("t_ready"), sem("t_act"), sem("t_dve")
        qk_squared, qk_normed = sem("qk_squared"), sem("qk_normed")
        split_done, split_stored, rep_loaded, max_placed = (
            sem("split_done"), sem("split_stored"), sem("rep_loaded"), sem("max_placed"))
        s_ready, s_taken = sem("s_ready"), sem("s_taken")
        p_ready, p_taken = sem("p_ready"), sem("p_taken")
        x1_ready, xr_ready, top_ready, inv_ready = sem("x1_ready"), sem("xr_ready"), sem("top_ready"), sem("inv_ready")
        x2_ready, proj_stored = sem("x2_ready"), sem("proj_stored")
        beta_ready = sem("beta_ready")
        att_ready = sem("att_ready")
        l_loaded, l_squared, l_perm, l_kb = (
            sem("l_loaded"), sem("l_squared"), sem("l_perm"), sem("l_kb"))
        u_ready, t2_ready, t2_act, t2_dve = sem("t2_ready_scan"), sem("t2_ready"), sem("t2_act"), sem("t2_dve")
        o_ready, h1_ready, hn_ready, x3_ready, hid_ready = (
            sem("o_ready"), sem("h1_ready"), sem("hn_ready"), sem("x3_ready"), sem("hid_ready"))
        x4_ready, stored = sem("x4_ready"), sem("stored")
        dve2_done, pool2_done, act2_done = sem("dve2_done"), sem("pool2_done"), sem("act2_done")
        setup_dve = sem("setup_dve")
        setup_pool = sem("setup_pool")
        gate_ready = sem("gate_ready")

        counted = [x_loaded, x_biased, t_ready, t_act, t_dve, qk_squared, qk_normed, split_done, split_stored, rep_loaded, max_placed, s_ready, s_taken, p_ready, p_taken, x1_ready, xr_ready, top_ready, inv_ready, x2_ready, proj_stored, beta_ready, l_loaded, l_squared, l_perm, l_kb, t2_ready, t2_act, t2_dve, o_ready, hn_ready, x3_ready, x4_ready, stored, dve_done, dve2_done, pool2_done]

        T = Handoff(t_ready, {"act": t_act, "dve": t_dve}, [6, 7],
                    [("xT", "act")] + [(f"qkv{t}", "act") for t in range(NT)]
                    + [("qT", "act"), ("kT", "act"), ("nmT", "dve")]
                    + [(f"pv{g}", "dve") for g in range(NG)]
                    + [("aT", "act"), ("ao", "dve"), ("x1T", "act")]
                    + [(f"L{t}", "act") for t in range(NT)] + [(f"M{t}", "act") for t in range(4)]
                    + [(f"cT{t}", "act") for t in range(NT)] + [(f"dT{t}", "dve") for t in range(4)]
                    + [("sn", "act"), ("slots", "act")] + [(f"h{c}", "act") for c in range(HC)]
                    + [("pr", "act"), ("mo", "dve"), ("x2T", "act")]
                    + [(f"c{t}", "act") for t in range(NT)])
        halves = (0, 1)
        uses2 = [(f"{n}{j}", "act") for n in "qkv" for j in halves] + [("beta", "act")]
        uses2 += [("o0", "act"), ("o1", "act"), ("oT0", "act"), ("oT1", "act"), ("wo0", "dve"), ("wo1", "dve"),
                  ("hT0", "act"), ("hT1", "act")]
        for f in halves:
            for c in range(HC):
                uses2 += [(f"g{f}{c}", "act"), (f"u{f}{c}", "dve")]
            uses2 += [(f"fo{f}", "dve"), (f"x3T{f}", "act")]
            for c in range(HC):
                uses2 += [(f"a{f}{c}", "act"), (f"b{f}{c}", "dve")]
            uses2 += [(f"m{f}{c}", "act") for c in range(HC)] + [(f"n{f}{c}", "act") for c in range(HC)]
            uses2 += [(f"y{f}", "dve")]
        T2 = Handoff(t2_ready, {"act": t2_act, "dve": t2_dve}, list(range(8)), uses2)

        s_units = []
        for it in range(NT):
            per = {0: 4, 1: 2}.get(it, 1)
            for g0 in range(0, NG, per):
                for q in range(4):
                    s_units.append((it, q, list(range(g0, g0 + per))))
        p_units = [(g, jt, pr) for g in range(NG) for jt in range(NT) for pr in range(2)]
        p_off = [0, 512, 896, 1152]
        PU = len(p_units) // NG

        s_jobs = [[(raw_w[:, j, :], None) for j in range(4)], [(raw_slot[:, j, :], None) for j in range(4)],
                  [(raw_f1[:, j, :], None) for j in range(4)], [(raw_f2[:, j, :], None) for j in range(4)]]
        for raw in (raw_h1, raw_h2):
            for ic in range(4):
                s_jobs.append([(raw[:, oc, ic * P:(ic + 1) * P], None) for oc in range(4)])
        s_jobs.append([(raw_w3[:, ic * P:(ic + 1) * P], None) for ic in range(4)])
        s_dst = [None, None, f_w1[:, :], f_w2[:, :]] + [f_h1[:, ic, :] for ic in range(4)] \
            + [f_h2[:, ic, :] for ic in range(4)] + [f_w3[:, :, :]]

        def arena_free(eng):
            eng.wait_ge(w_taken, len(s_jobs))
            eng.wait_ge(rep_init, 32)

        block = ctx.enter_context(nc.Block())

        @block.sync
        def _(sp):
            def load(dst, src):
                sp.dma_start(dst, src).then_inc(w_loaded, 16)

            for j, n in enumerate(("Wq", "Wk", "Wv", "Wo")):
                load(raw_w[:, j, :], A[f"L0_attn_{n}"])
            load(raw_slot, A["L0_ffn_slot_embeds"].rearrange("e t d -> (e t) d").rearrange("(c p) d -> p c d", p=P))
            load(raw_f1, A["L1_ffn_w1_w"].rearrange("(c p) d -> p c d", p=P))
            load(raw_f2, A["L1_ffn_w2_w"].rearrange("(c p) d -> p c d", p=P))
            load(raw_h1, A["L1_ffn_h1_w"].rearrange("(c p) d -> p c d", p=P))
            load(raw_h2, A["L1_ffn_h2_w"].rearrange("(c p) d -> p c d", p=P))
            load(raw_w3, A["L1_ffn_w3_w"])
            load(bias_o[:, :], A["L0_attn_bo"].partition_broadcast(P))
            for j, n in enumerate(("qln_g", "qln_b", "kln_g", "kln_b")):
                v = A[f"L0_attn_{n}"].rearrange("(d o) -> d o", o=1)
                for h in range(NH):
                    sp.dma_start(qk_gb[h * HD:(h + 1) * HD, j:j + 1], v).then_inc(w_loaded, 16)
            col = lambda n: A[n].rearrange("(d o) -> d o", o=1)
            load(gamma_x[:, :], col("L0_ffn_gamma_x"))
            load(gamma_s[:, :], col("L0_ffn_gamma_slot"))
            load(e_w1[:, :], A["L0_ffn_w1"])
            load(e_w2[:, :, :], A["L0_ffn_w2"].rearrange("(c p) d -> p c d", p=P))
            for j, n in enumerate(("Wq", "Wk", "Wv")):
                load(w_mix[:, j * D:(j + 1) * D], A[f"L1_attn_{n}"])
            load(w_mix[:, 3 * D:], A["L1_attn_Wb"])
            load(w_o1[:, :], A["L1_attn_Wo"])
            load(ln12[:, 0:1], col("L1_attn_ln1"))
            load(ln12[:, 1:2], col("L1_attn_ln2"))
            load(w_g[:, :], A["L1_attn_Wg"])
            load(w_u[:, :], A["L1_attn_Wu"])
            load(w_d[:, :, :], A["L1_attn_Wd"].rearrange("(c p) d -> p c d", p=P))
            for j, n in enumerate(("w1", "w2", "h1", "h2")):
                for c in range(HC):
                    load(f_s[:, j, c:c + 1], A[f"L1_ffn_{n}_s"][c * P:(c + 1) * P].rearrange("(p o) -> p o", o=1))
            load(f_s3[:, :], col("L1_ffn_w3_s"))
            sp.wait_ge(setup_pool, 2)
            sp.dma_start(q_rep[:, 3, :, :], ones_zeros[:, 0, :]).then_inc(rep_init, 16)
            sp.dma_start(k_rep[:, 3, :, :], ones_zeros[:, 1, :]).then_inc(rep_init, 16)
            sp.wait_ge(rep_init, 32)
            arena_free(sp)

            with sp.Fori(0, B) as i:
                sp.wait_ge(x1_ready, CREDIT + i)
                sp.dma_start(xb, A["L0_attn_x"][bass.ds(i, 1), :, :].rearrange("o (t p) d -> p (o t) d", p=P)) \
                    .then_inc(x_loaded, 16)
                sp.wait_ge(split_done, CREDIT + i + 1)
                for rep, j, parts in ((q_rep, 0, (0, 0, 1)), (k_rep, 1, (0, 1, 0))):
                    for c, part in enumerate(parts):
                        sp.dma_start(rep[:, c, :, :], hilo[:, j, part, :].bitcast(F32)).then_inc(split_stored, 16)
                sp.wait_ge(split_stored, CREDIT + (i + 1) * 96)
                for rep, dst in ((q_rep, qr), (k_rep, kr)):
                    sp.dma_start(dst[:, :, :].bitcast(F32), rep.rearrange("(g h) c d t -> (h c d) g t", g=NG)) \
                        .then_inc(rep_loaded, 16)
                sp.wait_ge(t_dve, CREDIT + T.emptied("nmT", i))
                for g in range(NG):
                    sp.dma_start(qr[24:P:32, g, :].bitcast(F32), nm_T[4 * g:4 * g + 4, :].bitcast(F32)) \
                        .then_inc(max_placed, 16)
                sp.wait_ge(beta_ready, CREDIT + i + 1)
                sp.dma_start(proj_d[bass.ds(i, 1), :, :, :].rearrange("o t p w -> p (o t) w"), proj) \
                    .then_inc(proj_stored, 16)
                sp.dma_start(x2_d[bass.ds(i, 1), :, :, :].rearrange("o t p w -> p (o t) w"), x2) \
                    .then_inc(proj_stored, 16)
            sp.wait_ge(proj_stored, CREDIT + B * 32)

            with sp.Fori(0, NT) as i:
                sp.wait_ge(x4_ready, CREDIT + i * 2)
                sp.dma_start(mix, proj_d[:, bass.ds(i, 1), :, :].rearrange("b o p w -> p (b o) w")).then_inc(l_loaded, 16)
                sp.dma_start(x2t, x2_d[:, bass.ds(i, 1), :, :].rearrange("b o p w -> p (b o) w")).then_inc(l_loaded, 16)
                for f in halves:
                    sp.wait_ge(x4_ready, CREDIT + i * 2 + f + 1)
                    sp.dma_start(out[4 * f:4 * f + 4, bass.ds(i * P, P), :].rearrange("b p d -> p b d"), x4) \
                        .then_inc(stored, 16)
            sp.wait_ge(stored, CREDIT + NT * 32)

        @block.gpsimd
        def _(g):
            for x in counted:
                g.sem_inc(x, CREDIT)
            g.memset(ones_zeros[:, 0, :], 0.0).then_inc(setup_pool, 1)
            g.memset(ones_zeros[:, 1, :], 1.0).then_inc(setup_pool, 1)
            g.memset(ident[:, :], 0.0).then_inc(setup_pool, 1)
            g.memset(mask_qk[:, :], 0.0).then_inc(setup_pool, 1)
            g.memset(mask_kq[:, :], 0.0).then_inc(setup_pool, 1)
            g.wait_ge(setup_pool, 5)
            g.affine_select(out=ident[:, :], in_=ident[:, :], compare_op=ALU.not_equal, fill=1.0,
                            base=0, pattern=[[-1, P]], channel_multiplier=1).then_inc(setup_pool, 1)
            g.affine_select(out=mask_qk[:, :], in_=mask_qk[:, :], compare_op=ALU.is_ge, fill=MASK,
                            base=0, pattern=[[-1, P]], channel_multiplier=1).then_inc(setup_pool, 1)
            g.affine_select(out=mask_kq[:, :], in_=mask_kq[:, :], compare_op=ALU.is_ge, fill=MASK,
                            base=0, pattern=[[1, P]], channel_multiplier=-1).then_inc(setup_pool, 1)
            g.wait_ge(setup_pool, 8)
            g.tensor_copy(ident_b[:, :], ident[:, :]).then_inc(setup_pool, 1)
            arena_free(g)
            g.memset(v_aug, 1.0).then_inc(setup_pool, 1)

            with g.Fori(0, B) as i:
                g.wait_ge(x_loaded, CREDIT + (i + 1) * 16)
                g.wait_ge(x1_ready, CREDIT + i)
                g.tensor_tensor(xbo, xb, bias_o[:, :].unsqueeze(1).broadcast_to([P, NT, D]), ALU.add) \
                    .then_inc(x_biased, 1)
                g.wait_ge(t_act, CREDIT + T.emptied(f"qkv{NT - 1}", i))
                g.wait_ge(qk_normed, CREDIT + i)
                g.tensor_tensor(qk_sq, qk, qk, ALU.mult).then_inc(qk_squared, 1)
                g.wait_ge(t_act, CREDIT + T.emptied("kT", i))
                g.tensor_tensor(hilo[:, :, 1, :], qk_T, hilo[:, :, 0, :].bitcast(F32), ALU.subtract) \
                    .then_inc(split_done, 1)

            g.wait_ge(proj_stored, CREDIT + B * 32)
            with g.Fori(0, NT) as i:
                g.wait_ge(l_loaded, CREDIT + (i + 1) * 32)
                g.tensor_tensor(l_sq, mix[:, :, 0:2 * D], mix[:, :, 0:2 * D], ALU.mult).then_inc(l_squared, 1)
                g.tensor_copy(perm[:, 2, :, :].rearrange("p d (b h) -> p b h d", b=B),
                              mix[:, :, 2 * D:3 * D].rearrange("p b (h d) -> p b h d", d=HD)).then_inc(l_perm, 1)
                g.tensor_copy(beta_p.rearrange("p (b h) -> p b h", b=B), mix[:, :, 3 * D:QW]).then_inc(l_perm, 1)
                g.wait_ge(t2_act, CREDIT + T2.emptied("beta", i))
                for j, src in enumerate((k_c, v_c)):
                    g.tensor_tensor(wu[:, :, j * HD:(j + 1) * HD], src,
                                    beta.unsqueeze(2).broadcast_to([P, P, HD]), ALU.mult).then_inc(l_kb, 1)
                g.wait_ge(hn_ready, CREDIT + i + 1)
                g.tensor_tensor(hn, h1, st2[:, 5, :].unsqueeze(2).broadcast_to([P, B, D]), ALU.mult) \
                    .then_inc(pool2_done, 1)

        @block.tensor
        def _(pe):
            pe.wait_ge(w_final, 1)
            pe.wait_ge(setup_pool, 9)
            for j, job in enumerate(s_jobs):
                if j >= 8:
                    pe.wait_ge(w_taken, j - 7)
                for k, (src, _) in enumerate(job):
                    last = pe.transpose(ps[:, j % 8, k * P:(k + 1) * P], src, ident[:, :])
                last.then_inc(w_ready, 1)
            arena_free(pe)

            with pe.Fori(0, B) as i:
                def fill(use):
                    T.wait_free(pe, use, i)
                    return ps[:, T.bank(use), :]

                def transposes(use, srcs):
                    bank = fill(use)
                    for k, src in enumerate(srcs):
                        last = pe.transpose(bank[0:src.shape[1], k * P:(k + 1) * P], src, ident[:, :])
                    last.then_inc(t_ready, 1)

                pe.wait_ge(x_loaded, CREDIT + (i + 1) * 16)
                transposes("xT", [xb[:, t, :] for t in range(NT)])
                pe.wait_ge(t_act, CREDIT + T.emptied("xT", i))
                for t in range(NT):
                    pe.matmul(fill(f"qkv{t}")[:, 0:3 * D], act_T[:, t * P:(t + 1) * P], w_qkv[:, :],
                              start=True, stop=True).then_inc(t_ready, 1)
                pe.wait_ge(qk_normed, CREDIT + i + 1)
                transposes("qT", [qk_n[:, t, 0:D] for t in range(NT)])
                transposes("kT", [qk_n[:, t, D:2 * D] for t in range(NT)])
                pe.wait_ge(rep_loaded, CREDIT + (i + 1) * 32)
                for k, (it, q, gs) in enumerate(s_units):
                    pe.wait_ge(s_taken, CREDIT + i * len(s_units) + max(k - 1, 0))
                    w = (it + 1) * P
                    for n, gg in enumerate(gs):
                        rows = slice(32 * q, 32 * q + 32)
                        bank = ps[:, 4 + k % 2, n * w:(n + 1) * w]
                        pe.matmul(bank, qr[rows, gg, it * P:(it + 1) * P], kr[rows, gg, 0:w], start=True, stop=False)
                        last = pe.matmul(bank[:, it * P:w], ident_b[:, :], mask_qk[:, :], start=False, stop=True)
                    last.then_inc(s_ready, 1)
                pe.wait_ge(s_taken, CREDIT + (i + 1) * len(s_units))
                transposes("nmT", [neg_max[:, t, :] for t in range(NT)])
                pe.wait_ge(max_placed, CREDIT + (i + 1) * 64)

                def products(gg):
                    pe.wait_ge(p_taken, CREDIT + i * len(p_units) + PU * (gg + 1))
                    bank = fill(f"pv{gg}")
                    for h4 in range(4):
                        for it in range(NT):
                            for jt in range(it + 1):
                                col = (it * 4 + h4) * (HD + 1)
                                at = p_off[jt] + (it - jt) * P
                                last = pe.matmul(bank[:, col:col + HD + 1], prob[:, gg % 2, h4, at:at + P],
                                                 v_aug[:, jt, 4 * gg + h4, :], start=(jt == 0), stop=(jt == it))
                    last.then_inc(t_ready, 1)

                for k, (gg, jt, pr) in enumerate(p_units):
                    pe.wait_ge(p_taken, CREDIT + i * len(p_units) + max(k - 1, 0))
                    for n in range(2):
                        rows = slice(32 * (2 * pr + n), 32 * (2 * pr + n) + 32)
                        bank = ps[:, 2 * (k % 2) + n, 0:S - jt * P]
                        pe.matmul(bank, kr[rows, gg, jt * P:(jt + 1) * P], qr[rows, gg, jt * P:S],
                                  start=True, stop=False)
                        last = pe.matmul(bank[:, 0:P], ident_b[:, :], mask_kq[:, :], start=False, stop=True)
                    last.then_inc(p_ready, 1)
                    if (k + 1) % PU == 0 and gg >= 1:
                        products(gg - 1)
                products(NG - 1)
                pe.wait_ge(t_dve, CREDIT + T.emptied(f"pv{NG - 1}", i))
                transposes("aT", [att[:, t, :] for t in range(NT)])
                pe.wait_ge(t_act, CREDIT + T.emptied("aT", i))
                bank = fill("ao")
                for t in range(NT):
                    last = pe.matmul(bank[:, t * P:(t + 1) * P], act_T[:, t * P:(t + 1) * P], w_out[:, :],
                                     start=True, stop=True)
                last.then_inc(t_ready, 1)
                pe.wait_ge(xr_ready, CREDIT + i + 1)
                transposes("x1T", [xr[:, t, :] for t in range(NT)])
                pe.wait_ge(t_act, CREDIT + T.emptied("x1T", i))
                for t in range(NT):
                    pe.matmul(fill(f"L{t}"), act_T[:, t * P:(t + 1) * P], slot_T[:, :], start=True, stop=True) \
                        .then_inc(t_ready, 1)
                for c in range(4):
                    pe.matmul(fill(f"M{c}"), slot_T[:, c * P:(c + 1) * P], act_T, start=True, stop=True) \
                        .then_inc(t_ready, 1)
                for t in range(NT):
                    pe.wait_ge(t_act, CREDIT + T.emptied(f"L{t}", i))
                    transposes(f"cT{t}", [comb[:, t, c * P:(c + 1) * P] for c in range(4)])
                for c in range(4):
                    pe.wait_ge(t_act, CREDIT + T.emptied(f"M{c}", i))
                    transposes(f"dT{c}", [disp_T[:, c, t * P:(t + 1) * P] for t in range(NT)])
                pe.wait_ge(t_dve, CREDIT + T.emptied("dT3", i))
                bank = fill("sn")
                for c in range(4):
                    for t in range(NT):
                        last = pe.matmul(bank[:, c * P:(c + 1) * P], disp[:, t, c * P:(c + 1) * P], xr[:, t, :],
                                         start=(t == 0), stop=(t == NT - 1))
                last.then_inc(t_ready, 1)
                pe.wait_ge(t_act, CREDIT + T.emptied("sn", i))
                transposes("slots", [slots_n[:, c, :] for c in range(4)])
                pe.wait_ge(t_act, CREDIT + T.emptied("slots", i))
                for c in range(HC):
                    pe.matmul(fill(f"h{c}"), e_w1[:, c * P:(c + 1) * P], slots, start=True, stop=True) \
                        .then_inc(t_ready, 1)
                pe.wait_ge(t_act, CREDIT + T.emptied(f"h{HC - 1}", i))
                bank = fill("pr")
                for n in range(4):
                    for c in range(HC):
                        last = pe.matmul(bank[:, n * P:(n + 1) * P], h_T[:, c, n * P:(n + 1) * P], e_w2[:, c, :],
                                         start=(c == 0), stop=(c == HC - 1))
                last.then_inc(t_ready, 1)
                pe.wait_ge(t_act, CREDIT + T.emptied("pr", i))
                bank = fill("mo")
                for t in range(NT):
                    for n in range(4):
                        last = pe.matmul(bank[:, t * P:(t + 1) * P], comb_T[:, n, t * P:(t + 1) * P], done_e[:, n, :],
                                         start=(n == 0), stop=(n == 3))
                last.then_inc(t_ready, 1)
                pe.wait_ge(x2_ready, CREDIT + i + 1)
                transposes("x2T", [x2[:, t, :] for t in range(NT)])
                pe.wait_ge(t_act, CREDIT + T.emptied("x2T", i))
                for t in range(NT):
                    pe.matmul(fill(f"c{t}")[:, 0:QW], act_T[:, t * P:(t + 1) * P], w_mix[:, :], start=True, stop=True) \
                        .then_inc(t_ready, 1)

            pe.wait_ge(t_act, CREDIT + B * T.total["act"])
            pe.wait_ge(t_dve, CREDIT + B * T.total["dve"])
            with pe.Fori(0, NT) as i:
                def fill2(use):
                    T2.wait_free(pe, use, i)
                    return ps[:, T2.bank(use), :]

                def transposes2(use, srcs):
                    bank = fill2(use)
                    for k, src in enumerate(srcs):
                        last = pe.transpose(bank[:, k * P:(k + 1) * P], src, ident[:, :])
                    last.then_inc(t2_ready, 1)

                pe.wait_ge(l_perm, CREDIT + (i + 1) * 4)
                for w, n in enumerate("qkv"):
                    for j in halves:
                        transposes2(f"{n}{j}", [perm[:, w, 4 * j + d, :] for d in range(4)])
                transposes2("beta", [beta_p])
                pe.wait_ge(o_ready, CREDIT + i + 1)
                for j in halves:
                    transposes2(f"o{j}", [o_c[:, 4 * j + d, :] for d in range(4)])
                pe.wait_ge(t2_act, CREDIT + T2.emptied("o1", i))
                for j in halves:
                    transposes2(f"oT{j}", [o_tok[:, 4 * j + b, :] for b in range(4)])
                for j in halves:
                    pe.wait_ge(t2_act, CREDIT + T2.emptied(f"oT{j}", i))
                    bank = fill2(f"wo{j}")
                    for b in range(4):
                        last = pe.matmul(bank[:, b * P:(b + 1) * P], o_T[:, 4 * j + b, :], w_o1[:, :],
                                         start=True, stop=True)
                    last.then_inc(t2_ready, 1)
                pe.wait_ge(pool2_done, CREDIT + i + 1)
                for j in halves:
                    transposes2(f"hT{j}", [hn[:, 4 * j + b, :] for b in range(4)])
                for f in halves:
                    def by_token(use, hid, w):
                        bank = fill2(use)
                        for b in range(4):
                            for c in range(HC):
                                last = pe.matmul(bank[:, b * P:(b + 1) * P], hid[:, c, b * P:(b + 1) * P],
                                                 w[:, c, :], start=(c == 0), stop=(c == HC - 1))
                        last.then_inc(t2_ready, 1)

                    def by_hidden(use, w, src):
                        pe.matmul(fill2(use), w, src, start=True, stop=True).then_inc(t2_ready, 1)

                    pe.wait_ge(t2_act, CREDIT + T2.emptied(f"hT{f}", i))
                    src = hn_T[:, 4 * f:4 * f + 4, :]
                    for c in range(HC):
                        by_hidden(f"g{f}{c}", w_g[:, c * P:(c + 1) * P], src)
                        by_hidden(f"u{f}{c}", w_u[:, c * P:(c + 1) * P], src)
                    pe.wait_ge(t2_dve, CREDIT + T2.emptied(f"u{f}{HC - 1}", i))
                    by_token(f"fo{f}", hid_a, w_d)
                    pe.wait_ge(x3_ready, CREDIT + i * 2 + f + 1)
                    transposes2(f"x3T{f}", [x3[:, b, :] for b in range(4)])
                    pe.wait_ge(t2_act, CREDIT + T2.emptied(f"x3T{f}", i))
                    for c in range(HC):
                        by_hidden(f"a{f}{c}", f_w1[:, c * P:(c + 1) * P], x3_T)
                        by_hidden(f"b{f}{c}", f_w2[:, c * P:(c + 1) * P], x3_T)
                    for use, w, src, who in (("m", f_h1, hid_a, f"b{f}{HC - 1}"), ("n", f_h2, hid_b, f"m{f}{HC - 1}")):
                        pe.wait_ge(t2_dve if who[0] == "b" else t2_act, CREDIT + T2.emptied(who, i))
                        for c in range(HC):
                            bank = fill2(f"{use}{f}{c}")
                            for k in range(HC):
                                last = pe.matmul(bank, w[:, k, c * P:(c + 1) * P], src[:, k, :],
                                                 start=(k == 0), stop=(k == HC - 1))
                            last.then_inc(t2_ready, 1)
                    pe.wait_ge(t2_act, CREDIT + T2.emptied(f"n{f}{HC - 1}", i))
                    by_token(f"y{f}", hid_a, f_w3)

        @block.scalar
        def _(act):
            for j, dst in enumerate(s_dst):
                if dst is not None:
                    act.wait_ge(w_ready, j + 1)
                    act.wait_ge(w_taken, j)
                    src = ps[:, j % 8, :]
                    if len(dst.shape) == 3:
                        src = src.rearrange("p (a b) -> p a b", a=4)
                    act.activation(dst, src, ACT.Copy).then_inc(w_taken, 1)
            arena_free(act)
            act.wait_ge(setup_pool, 10)

            with act.Fori(0, B) as i:
                def take(use, dst, src, func=ACT.Copy, **kw):
                    act.wait_ge(t_ready, CREDIT + T.filled(use, i))
                    return act.activation(dst, src(ps[:, T.bank(use), :]), func, **kw)

                act.wait_ge(t_ready, CREDIT + i * len(T.order))
                take("xT", act_T, lambda b: b).then_inc(t_act, 1)
                act.wait_ge(qk_normed, CREDIT + i)
                for t in range(NT):
                    take(f"qkv{t}", qk[:, t, :], lambda b: b[:, 0:2 * D])
                    act.activation(v_aug[:, t, :, 0:HD],
                                   ps[:, T.bank(f"qkv{t}"), 2 * D:3 * D].rearrange("p (h d) -> p h d", d=HD),
                                   ACT.Copy).then_inc(t_act, 1)
                act.wait_ge(split_done, CREDIT + i)
                act.wait_ge(split_stored, CREDIT + i * 96)
                for j, n in enumerate("qk"):
                    for dst in (qk_T[:, j, :], hilo[:, j, 0, :]):
                        r = take(f"{n}T", dst, lambda b: b, ACT.Identity, scale=qk_gb[:, 2 * j:2 * j + 1],
                                 bias=qk_gb[:, 2 * j + 1:2 * j + 2])
                    r.then_inc(t_act, 1)
                for k, (gg, jt, pr) in enumerate(p_units):
                    act.wait_ge(p_ready, CREDIT + i * len(p_units) + k + 1)
                    if k % PU == 0 and gg >= 2:
                        act.wait_ge(t_ready, CREDIT + T.filled(f"pv{gg - 2}", i))
                    w = S - jt * P
                    bank = 2 * (k % 2)
                    act.activation(prob[:, gg % 2, 2 * pr:2 * pr + 2, p_off[jt]:p_off[jt] + w],
                                   ps[:, bank:bank + 2, 0:w], ACT.Exp).then_inc(p_taken, 1)
                take("aT", act_T, lambda b: b).then_inc(t_act, 1)
                act.wait_ge(t_ready, CREDIT + T.filled("ao", i))
                take("x1T", act_T, lambda b: b).then_inc(t_act, 1)
                for j, (n, dst) in enumerate((("L", comb), ("M", disp_T))):
                    for t in range(4):
                        act.wait_ge(top_ready, CREDIT + i * 8 + 4 * j + t + 1)
                        take(f"{n}{t}", dst[:, t, :], lambda b: b, ACT.Exp, bias=neg_top[:, j, t:t + 1],
                             accum_out=z_sum[:, j, t:t + 1]).then_inc(t_act, 1)
                for t in range(NT):
                    take(f"cT{t}", comb_T[:, :, t * P:(t + 1) * P], lambda b: b.rearrange("p (c s) -> p c s", c=4)) \
                        .then_inc(t_act, 1)
                act.wait_ge(t_ready, CREDIT + T.filled("sn", i))
                act.wait_ge(inv_ready, CREDIT + i + 1)
                for c in range(4):
                    r = take("sn", slots_n[:, c, :], lambda b: b[:, c * P:(c + 1) * P], ACT.Identity,
                             scale=z_inv[:, 1, c:c + 1])
                r.then_inc(t_act, 1)
                take("slots", slots, lambda b: b, ACT.Identity, scale=gamma_x[:, 0:1]).then_inc(t_act, 1)
                for c in range(HC):
                    take(f"h{c}", h_T[:, c, :], lambda b: b, ACT.Gelu).then_inc(t_act, 1)
                take("pr", done_e, lambda b: b.rearrange("p (c s) -> p c s", c=4)).then_inc(t_act, 1)
                take("x2T", act_T, lambda b: b).then_inc(t_act, 1)
                act.wait_ge(proj_stored, CREDIT + i * 32)
                act.wait_ge(x2_ready, CREDIT + i + 1)
                for t in range(NT):
                    take(f"c{t}", proj[:, t, 0:3 * D], lambda b: b[:, 0:3 * D], ACT.Silu, scale=st[:, 5, t:t + 1])
                    act.activation(proj[:, t, 3 * D:QW], ps[:, T.bank(f"c{t}"), 3 * D:QW], ACT.Tanh,
                                   scale=st[:, 7, t:t + 1]).then_inc(t_act, 1)

            with act.Fori(0, NT) as i:
                def take2(use, dst, src=lambda b: b, func=ACT.Copy, **kw):
                    act.wait_ge(t2_ready, CREDIT + T2.filled(use, i))
                    return act.activation(dst, src(ps[:, T2.bank(use), :]), func, **kw)

                if True:
                    act.wait_ge(proj_stored, CREDIT + B * 32)
                for n, dst in (("q", q_c), ("k", k_c), ("v", v_c)):
                    for j in halves:
                        take2(f"{n}{j}", dst[:, :, 4 * j:4 * j + 4].rearrange("p t d -> p d t"),
                              lambda b: b.rearrange("p (d t) -> p d t", d=4)).then_inc(t2_act, 1)
                take2("beta", beta, lambda b: b[:, 0:P]).then_inc(t2_act, 1)
                for j in halves:
                    take2(f"o{j}", o_tok.rearrange("p b (h d) -> p d (b h)", d=HD)[:, 4 * j:4 * j + 4, :],
                          lambda b: b.rearrange("p (d t) -> p d t", d=4)).then_inc(t2_act, 1)
                for j in halves:
                    take2(f"oT{j}", o_T[:, 4 * j:4 * j + 4, :], lambda b: b.rearrange("p (d t) -> p d t", d=4)) \
                        .then_inc(t2_act, 1)
                for j in halves:
                    take2(f"hT{j}", hn_T[:, 4 * j:4 * j + 4, :], lambda b: b.rearrange("p (d t) -> p d t", d=4)) \
                        .then_inc(t2_act, 1)
                for f in halves:
                    for c in range(HC):
                        if c >= 2:
                            act.wait_ge(t2_dve, CREDIT + T2.emptied(f"u{f}{c - 2}", i))
                        elif f == 1:
                            act.wait_ge(t2_dve, CREDIT + T2.emptied(f"b{0}{HC - 1}", i))
                        else:
                            act.wait_ge(t2_dve, CREDIT + i * T2.total["dve"])
                        take2(f"g{f}{c}", gate[:, c % 2, :], func=ACT.Silu).then_inc(t2_act, 1)
                    take2(f"x3T{f}", x3_T).then_inc(t2_act, 1)
                    for c in range(HC):
                        act.wait_ge(t2_dve, CREDIT + T2.emptied(f"b{f}{c - 2}" if c >= 2 else f"u{f}{HC - 1}", i))
                        take2(f"a{f}{c}", gate[:, c % 2, :], func=ACT.Silu, scale=f_s[:, 0, c:c + 1]).then_inc(t2_act, 1)
                    for c in range(HC):
                        take2(f"m{f}{c}", hid_b[:, c, :], func=ACT.Gelu, scale=f_s[:, 2, c:c + 1]).then_inc(t2_act, 1)
                    for c in range(HC):
                        take2(f"n{f}{c}", hid_a[:, c, :], func=ACT.Gelu, scale=f_s[:, 3, c:c + 1]).then_inc(t2_act, 1)

        @block.vector
        def _(v):
            def rsqrt(o, y, x, t):
                o.step(v.tensor_scalar(y.bitcast(I32), x.bitcast(I32), -0.5, RSQRT_SEED, ALU.mult, ALU.add))
                for _ in range(3):
                    o.step(v.tensor_tensor(t, y, y, ALU.mult))
                    o.step(v.scalar_tensor_tensor(t, t, -0.5, x, ALU.mult, ALU.mult))
                    o.step(v.scalar_tensor_tensor(y, t, 1.5, y, ALU.add, ALU.mult))

            def centre_and_scale(o, y, sq, s, n):
                o.step(v.tensor_reduce(s[:, 0, 0:n], y, X, ALU.add))
                o.step(v.tensor_scalar(s[:, 0, 0:n], s[:, 0, 0:n], 1.0 / D, None, ALU.mult))
                o.step(v.tensor_tensor(y, y, s[:, 0, 0:n].unsqueeze(2).broadcast_to([P, n, D]), ALU.subtract))
                o.step(v.tensor_tensor(sq, y, y, ALU.mult))
                o.step(v.tensor_reduce(s[:, 1, 0:n], sq, X, ALU.add))
                o.step(v.tensor_scalar(s[:, 2, 0:n], s[:, 1, 0:n], 1.0 / D, LN_EPS, ALU.mult, ALU.add))
                rsqrt(o, s[:, 3, 0:n], s[:, 2, 0:n], s[:, 4, 0:n])

            def scaled(dst, y, s, n):
                return v.tensor_tensor(dst, y, s.unsqueeze(2).broadcast_to([P, n, D]), ALU.mult)

            o = Order(v, setup_dve, 0, 0, 0)
            v.wait_ge(w_loaded, (W_TOTAL) * 16)
            o.step(v.tensor_tensor(slot_sq, raw_slot, raw_slot, ALU.mult))
            o.step(v.tensor_reduce(slot_n, slot_sq, X, ALU.add))
            o.step(v.tensor_scalar(slot_n, slot_n, 1e-24, None, ALU.max))
            rsqrt(o, slot_r, slot_n, slot_t)
            o.step(v.tensor_scalar(slot_r, slot_r, float(D) ** 0.5, None, ALU.mult))
            o.step(scaled(raw_slot, raw_slot, slot_r, 4))
            o.step(v.tensor_tensor(gamma_s[:, :], gamma_s[:, :], gamma_x[:, :], ALU.mult))
            o.step(v.tensor_scalar(raw_w3, raw_w3, f_s3[:, 0:1], None, ALU.mult))
            o.step(v.tensor_scalar(qk_gb[:, :], qk_gb[:, :], float(D) ** -0.25, None, ALU.mult))
            o.step(v.tensor_scalar(w_mix[:, :], w_mix[:, :], ln12[:, 0:1], None, ALU.mult))
            o.step(v.tensor_scalar(w_g[:, :], w_g[:, :], ln12[:, 1:2], None, ALU.mult))
            v.tensor_scalar(w_u[:, :], w_u[:, :], ln12[:, 1:2], None, ALU.mult).then_inc(w_final, 1)
            v.wait_ge(w_ready, 1)
            v.wait_ge(w_final, 1)
            o.step(v.tensor_reduce(centre, ps[:, 0, 0:2 * D].rearrange("p (g d) -> p g d", d=HD), X, ALU.add))
            o.step(v.tensor_scalar(centre, centre, -1.0 / HD, None, ALU.mult))
            o.step(v.tensor_tensor(w_qkv[:, 0:2 * D].rearrange("p (g d) -> p g d", d=HD),
                                   ps[:, 0, 0:2 * D].rearrange("p (g d) -> p g d", d=HD),
                                   centre.unsqueeze(2).broadcast_to([P, 2 * NH, HD]), ALU.add))
            o.step(v.tensor_copy(w_qkv[:, 2 * D:3 * D], ps[:, 0, 2 * D:3 * D]))
            v.tensor_copy(w_out[:, :], ps[:, 0, 3 * D:4 * D]).then_inc(w_taken, 1)
            v.wait_ge(w_ready, 2)
            v.tensor_scalar(slot_T[:, :], ps[:, 1, :], gamma_s[:, 0:1], None, ALU.mult).then_inc(w_taken, 1)
            assert o.n == SETUP_DVE, ('SETUP_DVE', o.n, 0)
            arena_free(v)

            with v.Fori(0, B) as i:
                o = Order(v, dve_done, DVE1, i, CREDIT)
                s = st

                def arrived(use):
                    v.wait_ge(t_ready, CREDIT + T.filled(use, i))
                    return ps[:, T.bank(use), :]

                v.wait_ge(qk_squared, CREDIT + i + 1)
                o.step(v.tensor_reduce(qk_var, qk_sq.rearrange("p t (g d) -> p (t g) d", d=HD), X, ALU.add))
                o.step(v.tensor_scalar(qk_var, qk_var, 1.0 / HD, LN_EPS, ALU.mult, ALU.add))
                rsqrt(o, qk_r, qk_var, qk_t)
                v.tensor_tensor(qk_n.rearrange("p t (g d) -> p (t g) d", d=HD),
                                qk.rearrange("p t (g d) -> p (t g) d", d=HD),
                                qk_r.unsqueeze(2).broadcast_to([P, P, HD]), ALU.mult).then_inc(qk_normed, 1)
                for k, (it, q, gs) in enumerate(s_units):
                    v.wait_ge(s_ready, CREDIT + i * len(s_units) + k + 1)
                    w = (it + 1) * P
                    v.tensor_reduce(neg_max[:, it, 4 * gs[0] + q:4 * gs[-1] + q + 1:4],
                                    ps[:, 4 + k % 2, 0:len(gs) * w].rearrange("p (n w) -> p n w", w=w),
                                    X, ALU.max, negate=True).then_inc(s_taken, 1)
                v.wait_ge(max_placed, CREDIT + i * 64)
                v.tensor_copy(nm_T[:, :], arrived("nmT")[0:NH, :]).then_inc(t_dve, 1)
                for g in range(NG):
                    pv = arrived(f"pv{g}")[:, 0:NT * 4 * (HD + 1)].rearrange("p (t h d) -> p t h d", t=NT, h=4)
                    o.step(v.reciprocal(rec, pv[:, :, :, HD]))
                    for t in range(NT):
                        r = v.tensor_tensor(att[:, t, g * 32:(g + 1) * 32].rearrange("p (h d) -> p h d", d=HD),
                                            pv[:, t, :, 0:HD], rec[:, t, :].unsqueeze(2).broadcast_to([P, 4, HD]),
                                            ALU.mult)
                        if t < NT - 1:
                            o.mark(r)
                        else:
                            r.then_inc(t_dve, 1)
                    v.wait_ge(t_dve, CREDIT + T.emptied(f"pv{g}", i))
                v.wait_ge(x_biased, CREDIT + i + 1)
                v.tensor_tensor(y1, arrived("ao").rearrange("p (t d) -> p t d", d=D), xbo, ALU.add).then_inc(t_dve, 1)
                v.wait_ge(t_dve, CREDIT + T.emptied("ao", i))
                centre_and_scale(o, y1, y_sq, s, NT)
                scaled(x1, y1, s[:, 3, 0:NT], NT).then_inc(x1_ready, 1)
                v.wait_ge(x1_ready, CREDIT + i + 1)
                o.step(v.tensor_tensor(y_sq, x1, x1, ALU.mult))
                o.step(v.tensor_reduce(s[:, 1, :], y_sq, X, ALU.add))
                o.step(v.tensor_scalar(s[:, 1, :], s[:, 1, :], 1e-24, None, ALU.max))
                rsqrt(o, s[:, 3, :], s[:, 1, :], s[:, 4, :])
                o.step(v.tensor_scalar(s[:, 6, :], s[:, 3, :], float(D) ** 0.5, None, ALU.mult))
                scaled(xr, x1, s[:, 6, :], NT).then_inc(xr_ready, 1)
                for j, n in enumerate("LM"):
                    for t in range(4):
                        v.tensor_reduce(neg_top[:, j, t:t + 1], arrived(f"{n}{t}"), X, ALU.max, negate=True) \
                            .then_inc(top_ready, 1)
                v.wait_ge(t_act, CREDIT + T.emptied("M3", i))
                v.reciprocal(z_inv, z_sum).then_inc(inv_ready, 1)
                for c in range(4):
                    v.tensor_copy(disp[:, :, c * P:(c + 1) * P],
                                  arrived(f"dT{c}").rearrange("p (t n) -> p t n", t=NT)).then_inc(t_dve, 1)
                v.wait_ge(proj_stored, CREDIT + i * 32)
                v.wait_ge(inv_ready, CREDIT + i + 1)
                v.tensor_tensor(y1, arrived("mo").rearrange("p (t d) -> p t d", d=D),
                                z_inv[:, 0, :].unsqueeze(2).broadcast_to([P, NT, D]), ALU.mult).then_inc(t_dve, 1)
                v.wait_ge(t_dve, CREDIT + T.emptied("mo", i))
                o.step(v.tensor_tensor(y1, y1, x1, ALU.add))
                centre_and_scale(o, y1, y_sq, s, NT)
                o.step(scaled(x2, y1, s[:, 3, 0:NT], NT))
                o.step(v.tensor_tensor(y_sq, x2, x2, ALU.mult))
                o.step(v.tensor_reduce(s[:, 1, :], y_sq, X, ALU.add))
                o.step(v.tensor_scalar(s[:, 2, :], s[:, 1, :], 1.0 / D, 1e-6, ALU.mult, ALU.add))
                rsqrt(o, s[:, 5, :], s[:, 2, :], s[:, 4, :])
                v.tensor_scalar(s[:, 7, :], s[:, 5, :], 0.5, None, ALU.mult).then_inc(x2_ready, 1)
                v.wait_ge(t_act, CREDIT + (i + 1) * T.total["act"])
                v.tensor_scalar(proj[:, :, 3 * D:QW], proj[:, :, 3 * D:QW], 0.5, 0.5, ALU.mult, ALU.add) \
                    .then_inc(beta_ready, 1)
                o.end('DVE1')

            v.wait_ge(proj_stored, CREDIT + B * 32)
            v.memset(state[:, NC, :, :], 0.0).then_inc(setup_dve, 1)
            v.wait_ge(setup_dve, SETUP_DVE + 1)
            with v.Fori(0, NT) as i:
                o = Order(v, dve2_done, DVE2, i, CREDIT)
                s = st2

                def arrived2(use):
                    v.wait_ge(t2_ready, CREDIT + T2.filled(use, i))
                    return ps[:, T2.bank(use), :]

                o.step(v.tensor_copy(state[:, 0, :, :], state[:, NC, :, :]))
                v.wait_ge(l_squared, CREDIT + i + 1)
                o.step(v.tensor_reduce(l_var, l_sq.rearrange("p b (g d) -> p (b g) d", d=HD), X, ALU.add))
                o.step(v.tensor_scalar(l_var, l_var, 1e-6, None, ALU.add))
                rsqrt(o, l_r, l_var, l_t)
                rr = l_r.rearrange("p (b w h) -> p b w h", b=B, w=2)
                for w in range(2):
                    for b in range(B):
                        r = v.tensor_tensor(perm[:, w, :, b * NH:(b + 1) * NH].rearrange("p d h -> p h d"),
                                            mix[:, b, w * D:(w + 1) * D].rearrange("p (h d) -> p h d", d=HD),
                                            rr[:, b, w, :].unsqueeze(2).broadcast_to([P, NH, HD]), ALU.mult)
                        if b < B - 1:
                            o.mark(r)
                        else:
                            r.then_inc(l_perm, 1)
                v.wait_ge(l_perm, CREDIT + (i + 1) * 4)
                v.wait_ge(l_kb, CREDIT + (i + 1) * 2)
                kc = k_c.rearrange("p (c j) d -> p c j d", j=CH)
                qc = q_c.rearrange("p (c j) d -> p c j d", j=CH)
                wc = wu.rearrange("p (c j) w -> p c j w", j=CH)
                uc = u_c.rearrange("p (c j) d -> p c j d", j=CH)
                for dst, left, first in ((gram, wc[:, :, :, 0:HD], 1), (qkd, qc, 0)):
                    for lag in range(first, CH):
                        n = CH - lag
                        tv = tmp[:, 0:NC * n * HD].rearrange("p (c j d) -> p c j d", c=NC, j=n)
                        if first:
                            pass
                        o.step(v.tensor_tensor(tv, left[:, :, lag:CH, :], kc[:, :, 0:n, :], ALU.mult))
                        o.step(v.tensor_reduce(dst[:, :, lag * CH:lag * CH + (n - 1) * (CH + 1) + 1:CH + 1], tv, X, ALU.add))
                for r_ in range(1, CH):
                    tv = tmp[:, 0:NC * 2 * HD * r_].rearrange("p (c w j) -> p c w j", c=NC, j=r_)
                    o.step(v.tensor_tensor(tv, wc[:, :, 0:r_, :].rearrange("p c j w -> p c w j"),
                                           gram[:, :, r_ * CH:r_ * CH + r_].unsqueeze(2).broadcast_to([P, NC, 2 * HD, r_]),
                                           ALU.mult))
                    t2 = l_sq.rearrange("p b w -> p (b w)")[:, 0:NC * 2 * HD].rearrange("p (c w) -> p c w", c=NC)
                    o.step(v.tensor_reduce(t2, tv, X, ALU.add))
                    o.step(v.tensor_tensor(wc[:, :, r_, :], wc[:, :, r_, :], t2, ALU.subtract))
                for c in range(NC):
                    o.step(v.tensor_tensor(s_m, wc[:, c, :, 0:HD].unsqueeze(2).broadcast_to([P, CH, HD, HD]),
                                           state[:, c, :, :].unsqueeze(1).broadcast_to([P, CH, HD, HD]), ALU.mult))
                    o.step(v.tensor_reduce(s_w, s_m, X, ALU.add))
                    o.step(v.tensor_tensor(uc[:, c, :, :], wc[:, c, :, HD:2 * HD], s_w, ALU.subtract))
                    o.step(v.tensor_tensor(s_n, uc[:, c, :, :].rearrange("p j v -> p v j").unsqueeze(2)
                                           .broadcast_to([P, HD, HD, CH]),
                                           kc[:, c, :, :].rearrange("p j k -> p k j").unsqueeze(1)
                                           .broadcast_to([P, HD, HD, CH]), ALU.mult))
                    o.step(v.tensor_reduce(s_d, s_n, X, ALU.add))
                    o.step(v.tensor_tensor(state[:, c + 1, :, :], state[:, c, :, :], s_d, ALU.add))
                oc = o_c.rearrange("p v (c j) -> p c j v", j=CH)
                for r_ in range(CH):
                    o.step(v.tensor_tensor(o_m[:, :, :, 0:HD], state[:, 0:NC, :, :],
                                           qc[:, :, r_, :].unsqueeze(2).broadcast_to([P, NC, HD, HD]), ALU.mult))
                    o.step(v.tensor_tensor(o_m[:, :, :, HD:HD + r_ + 1], uc[:, :, 0:r_ + 1, :].rearrange("p c j v -> p c v j"),
                                           qkd[:, :, r_ * CH:r_ * CH + r_ + 1].unsqueeze(2)
                                           .broadcast_to([P, NC, HD, r_ + 1]), ALU.mult))
                    r = v.tensor_reduce(oc[:, :, r_, :], o_m[:, :, :, 0:HD + r_ + 1], X, ALU.add)
                    if r_ < CH - 1:
                        o.step(r)
                    else:
                        r.then_inc(o_ready, 1)
                for j in halves:
                    v.tensor_tensor(h1[:, 4 * j:4 * j + 4, :], arrived2(f"wo{j}").rearrange("p (b d) -> p b d", d=D),
                                    x2t[:, 4 * j:4 * j + 4, :], ALU.add).then_inc(t2_dve, 1)
                v.wait_ge(t2_dve, CREDIT + T2.emptied("wo1", i))
                o.step(v.tensor_tensor(hn, h1, h1, ALU.mult))
                o.step(v.tensor_reduce(s[:, 1, :], hn, X, ALU.add))
                o.step(v.tensor_scalar(s[:, 2, :], s[:, 1, :], 1.0 / D, 1e-6, ALU.mult, ALU.add))
                rsqrt(o, s[:, 5, :], s[:, 2, :], s[:, 4, :])
                v.tensor_tensor(x2t, x2t, h1, ALU.add).then_inc(hn_ready, 1)
                for f in halves:
                    for c in range(HC):
                        v.wait_ge(t2_act, CREDIT + T2.emptied(f"g{f}{c}", i))
                        v.tensor_tensor(hid_a[:, c, :], arrived2(f"u{f}{c}"), gate[:, c % 2, :], ALU.mult) \
                            .then_inc(t2_dve, 1)
                    v.wait_ge(hn_ready, CREDIT + i + 1)
                    v.tensor_tensor(y3, arrived2(f"fo{f}").rearrange("p (b d) -> p b d", d=D),
                                    x2t[:, 4 * f:4 * f + 4, :], ALU.add).then_inc(t2_dve, 1)
                    v.wait_ge(t2_dve, CREDIT + T2.emptied(f"fo{f}", i))
                    centre_and_scale(o, y3, y3_sq, s, 4)
                    scaled(x3, y3, s[:, 3, 0:4], 4).then_inc(x3_ready, 1)
                    v.wait_ge(x3_ready, CREDIT + i * 2 + f + 1)
                    for c in range(HC):
                        v.wait_ge(t2_act, CREDIT + T2.emptied(f"a{f}{c}", i))
                        v.scalar_tensor_tensor(hid_a[:, c, :], arrived2(f"b{f}{c}"), f_s[:, 1, c:c + 1],
                                               gate[:, c % 2, :], ALU.mult, ALU.mult).then_inc(t2_dve, 1)
                    v.tensor_tensor(y4, arrived2(f"y{f}").rearrange("p (b d) -> p b d", d=D), x3, ALU.add) \
                        .then_inc(t2_dve, 1)
                    v.wait_ge(t2_dve, CREDIT + T2.emptied(f"y{f}", i))
                    centre_and_scale(o, y4, y3_sq, s, 4)
                    v.wait_ge(stored, CREDIT + i * 32 + f * 16)
                    scaled(x4, y4, s[:, 3, 0:4], 4).then_inc(x4_ready, 1)
                    v.wait_ge(x4_ready, CREDIT + i * 2 + f + 1)
                o.end('DVE2')


W_TOTAL = 11 + 64 + 2 + 2 + 3 + 1 + 1 + 2 + 2 + 1 + 4 * HC + 1
SETUP_DVE = 24
DVE1 = 89
DVE2 = 330

_OUTS = [((B, S, D), "float32")]


def kernel(**inputs):
    import concourse.bacc as bacc
    from concourse.bass_utils import run_bass_kernel_spmd

    nc = bacc.Bacc("TRN2", target_bir_lowering=False, num_devices=1)
    arrays, args = {}, {}
    for name, value in inputs.items():
        a = np.ascontiguousarray(value)
        arrays[f"in_{name}"] = a
        args[name] = nc.dram_tensor(f"in_{name}", a.shape, mybir.dt.from_np(a.dtype), kind="ExternalInput").ap()
    shape, dtype = _OUTS[0]
    out = nc.dram_tensor("out_0", shape, mybir.dt.from_np(np.dtype(dtype)), kind="ExternalOutput").ap()
    build(nc, args, out)
    r = run_bass_kernel_spmd(nc, [arrays], core_ids=[0])
    return r.results[0]["out_0"]
```

```python
from contextlib import ExitStack

import numpy as np
import concourse.bass as bass
from concourse import mybir

F32 = mybir.dt.float32
F32R = mybir.dt.float32r
BF16 = mybir.dt.bfloat16
I32 = mybir.dt.int32
ALU = mybir.AluOpType
ACT = mybir.ActivationFunctionType
X = mybir.AxisListType.X

P = 128
B, S, D = 8, 512, 128
NT = S // P
NH, HD = 16, 8
NG = NH // 4
NE, NS = 8, 64
N = NE * NS
HID = 512
HC = HID // P
QW = 3 * D + NH
CH = 4
NC = P // CH
LN_EPS = 1e-5
MASK = -1e30
RSQRT_SEED = 1597463007.0
RSQRT_SCALE = 64.0 / 9
CREDIT = 1


class Handoff:

    def __init__(self, ready, taken, banks, uses):
        self.ready, self.taken, self.banks = ready, taken, banks
        self.order = [u for u, _ in uses]
        self.engine = dict(uses)
        self.total = {e: sum(x == e for _, x in uses) for e in taken}
        self.ordinal = {}
        seen = {e: 0 for e in taken}
        for u, e in uses:
            seen[e] += 1
            self.ordinal[u] = seen[e]

    def bank(self, use):
        return self.banks[self.order.index(use) % len(self.banks)]

    def filled(self, use, i):
        return i * len(self.order) + self.order.index(use) + 1

    def emptied(self, use, i):
        return i * self.total[self.engine[use]] + self.ordinal[use]

    def wait_free(self, pe, use, i):
        k = self.order.index(use) - len(self.banks)
        if k >= 0:
            before = self.order[k]
            pe.wait_ge(self.taken[self.engine[before]], CREDIT + self.emptied(before, i))
        else:
            for e, n in self.total.items():
                if n:
                    pe.wait_ge(self.taken[e], CREDIT + i * n)


class Order:

    def __init__(self, eng, done, per, i, first):
        self.eng, self.sem, self.base, self.n, self.first, self.per = eng, done, i * per, 0, first, per
        self.between = None

    def mark(self, ins):
        ins.then_inc(self.sem, 1)
        self.n += 1

    def settle(self):
        self.eng.wait_ge(self.sem, self.first + self.base + self.n)

    def complete(self):
        if self.between:
            self.between()
        self.settle()

    def step(self, ins):
        self.mark(ins)
        self.complete()

    def end(self, name):
        assert self.n == self.per, (name, self.n, self.per)


def build(nc, A, out, taps=None):
    ctx = ExitStack()
    with ctx:
        def sb(name, shape, dt=F32):
            return ctx.enter_context(nc.sbuf_tensor(name, shape, dt))

        def sem(name):
            return ctx.enter_context(nc.semaphore(name))

        ps = ctx.enter_context(nc.psum_tensor("ps", [P, 8, 512], F32))

        q_rep = nc.dram_tensor("q_rep", (NH, 4, HD, S), F32, kind="Internal").ap()
        k_rep = nc.dram_tensor("k_rep", (NH, 4, HD, S), F32, kind="Internal").ap()
        proj_d = nc.dram_tensor("proj_d", (B, NT, P, QW), F32, kind="Internal").ap()
        gb_d = nc.dram_tensor("gb_d", (4, NH, HD), F32, kind="Internal").ap()
        x2_d = nc.dram_tensor("x2_d", (B, NT, P, D), F32, kind="Internal").ap()

        ident = sb("ident", [P, P])
        ident_b = sb("ident_b", [P, P], BF16)
        mask_qk = sb("mask_qk", [P, P], BF16)
        mask_kq = sb("mask_kq", [P, P], BF16)
        w_qkv = sb("w_qkv", [P, 3 * D])
        w_out = sb("w_out", [P, D])
        bias_o = sb("bias_o", [P, D])
        qk_gb = sb("qk_gb", [P, 4])
        slot_T = sb("slot_T", [P, N])
        gamma_x = sb("gamma_x", [P, 1])
        gamma_s = sb("gamma_s", [P, 1])
        e_w1 = sb("e_w1", [P, HID])
        e_w2 = sb("e_w2", [P, HC, D])
        w_mix = sb("w_mix", [P, QW])
        w_o1 = sb("w_o1", [P, D])
        ln12 = sb("ln12", [P, 2])
        w_g = sb("w_g", [P, HID])
        w_u = sb("w_u", [P, HID])
        w_d = sb("w_d", [P, HC, D])
        f_w1 = sb("f_w1", [P, HID])
        f_w2 = sb("f_w2", [P, HID])
        f_h1 = sb("f_h1", [P, HC, HID])
        f_h2 = sb("f_h2", [P, HC, HID])
        f_w3 = sb("f_w3", [P, HC, D])
        f_s = sb("f_s", [P, 4, HC])
        f_s3 = sb("f_s3", [P, 1])

        ARENA = 34 * 1024
        arena = sb("arena", [P, ARENA])
        qr = sb("qr", [P, NG, S], F32R)
        kr = sb("kr", [P, NG, S], F32R)

        class Carve:
            def __init__(self):
                self.at = 0

            def take(self, *shape):
                n = int(np.prod(shape))
                ap = arena[:, self.at:self.at + n]
                self.at += n
                assert self.at <= ARENA, self.at
                if len(shape) == 2:
                    return ap.rearrange("p (a b) -> p a b", a=shape[0])
                if len(shape) == 3:
                    return ap.rearrange("p (a b c) -> p a b c", a=shape[0], b=shape[1])
                if len(shape) == 4:
                    return ap.rearrange("p (a b c d) -> p a b c d", a=shape[0], b=shape[1], c=shape[2])
                return ap

        c0 = Carve()
        raw_w = c0.take(4, P)
        raw_slot = c0.take(4, P)
        raw_f1 = c0.take(4, P)
        raw_f2 = c0.take(4, P)
        raw_h1 = c0.take(4, HID)
        raw_h2 = c0.take(4, HID)
        raw_w3 = c0.take(HID)
        centre = c0.take(2 * NH)
        slot_sq = c0.take(4, P)
        slot_n = c0.take(4)
        slot_r = c0.take(4)
        slot_t = c0.take(4)
        ones_zeros = c0.take(2, S)

        c1 = Carve()
        xb = c1.take(NT, D)
        xbo = c1.take(NT, D)
        xT = c1.take(S)
        act_T = c1.take(S)
        qk = c1.take(NT, 2 * D)
        qk_sq = c1.take(NT, 2 * D)
        qk_n = qk_sq
        qk_var = c1.take(P)
        qk_r = c1.take(P)
        qk_t = c1.take(P)
        qk_T = c1.take(2, S)
        v_new = c1.take(NT, D)
        v_aug = c1.take(NT, NH, 32)
        pv_T = c1.take(2, S)
        neg_max = c1.take(NT, NH)
        prob = c1.take(2, 4, 1280)
        rec = c1.take(NT, 4)
        att = c1.take(NT, D)
        y1 = c1.take(NT, D)
        y_sq = c1.take(NT, D)
        x1 = c1.take(NT, D)
        x2 = c1.take(NT, D)
        st = c1.take(8, NT)
        bn1 = c1.take(NT, 6)
        xr = c1.take(NT, D)
        neg_top = c1.take(2, 4)
        z_sum = c1.take(2, 4)
        z_inv = c1.take(2, 4)
        comb = c1.take(NT, N)
        comb_T = c1.take(4, S)
        disp_T = c1.take(4, S)
        disp = c1.take(NT, N)
        slots_n = c1.take(4, D)
        slots = c1.take(N)
        h_T = comb
        done_e = c1.take(4, D)
        proj = c1.take(NT, QW)
        hilo = sb("hilo", [P, 2, 2, S], F32R)
        nm_T = sb("nm_T", [NH, S], F32R)

        c2 = Carve()
        mix = c2.take(B, QW)
        x2t = c2.take(B, D)
        l_sq = c2.take(B, 2 * D)
        scan_part = l_sq.rearrange("p b w -> p (b w)")
        u_c = scan_part[:, 0:P * HD].rearrange("p (t d) -> p t d", d=HD)
        fold = scan_part[:, P * HD:P * HD + NC * 2 * HD].rearrange("p (c w) -> p c w", c=NC)
        l_var = c2.take(B * 2 * NH)
        l_r = c2.take(B * 2 * NH)
        l_t = c2.take(B * 2 * NH)
        perm = c2.take(3, HD, B * NH)
        beta_p = c2.take(B * NH)
        q_c = c2.take(P, HD)
        k_c = c2.take(P, HD)
        v_c = c2.take(P, HD)
        beta = c2.take(P)
        wu = c2.take(P, 2 * HD)
        gram = c2.take(NC, CH * CH)
        qkd = c2.take(NC, CH * CH)
        state = c2.take(NC, HD, HD)
        w_s = c2.take(2, CH, HD, HD + 1)
        k_u = c2.take(2, HD, HD, CH + 1)
        o_m = c2.take(NC, HD, HD + CH)
        tmp = o_m.rearrange("p c v k -> p (c v k)")
        o_c = v_c.rearrange("p t d -> p (t d)").rearrange("p (d t) -> p d t", t=P)
        o_tok = c2.take(B, D)
        o_T = c2.take(B, P)
        h1 = c2.take(B, D)
        hn = o_tok
        hn_T = o_T
        y3 = c2.take(4, D)
        bn2 = c2.take(4, 6)
        x3 = c2.take(B, D)
        x3_T = c2.take(2, S)
        y4 = y3
        x4 = c2.take(4, D)
        gate = c2.take(2, S)
        up = c2.take(2, S)
        hid_a = c2.take(HC, S)
        hid_b = perm.rearrange("p w d b -> p (w d b)")[:, 0:HC * S].rearrange("p (c s) -> p c s", c=HC)
        st2 = c2.take(8, B)

        w_loaded = sem("w_loaded")
        consts = sem("consts")
        w_ready = sem("w_ready")
        w_taken = sem("w_taken")
        w_final = sem("w_final")
        rep_init = sem("rep_init")
        pool_done, act_done, dve_done = sem("pool_done"), sem("act_done"), sem("dve_done")
        x_loaded = sem("x_loaded")
        x_biased = sem("x_biased")
        f_ready, f_act, f_dve = sem("f_ready"), sem("f_act"), sem("f_dve")
        pv_ready, pv_act, pv_dve = sem("pv_ready"), sem("pv_act"), sem("pv_dve")
        t_ready, t_act, t_dve = sem("t_ready"), sem("t_act"), sem("t_dve")
        qk_squared, qk_normed = sem("qk_squared"), sem("qk_normed")
        split_done, split_stored, rep_loaded, max_placed = (
            sem("split_done"), sem("split_stored"), sem("rep_loaded"), sem("max_placed"))
        s_ready, s_taken = sem("s_ready"), sem("s_taken")
        p_ready, p_taken = sem("p_ready"), sem("p_taken")
        x1_ready, xr_ready, top_ready, inv_ready = sem("x1_ready"), sem("xr_ready"), sem("top_ready"), sem("inv_ready")
        x2_ready, proj_stored = sem("x2_ready"), sem("proj_stored")
        beta_ready = sem("beta_ready")
        v_placed, front_done = sem("v_placed"), sem("front_done")
        att_ready = sem("att_ready")
        x2_loaded = sem("x2_loaded")
        l_loaded, l_squared, l_perm, l_kb = (
            sem("l_loaded"), sem("l_squared"), sem("l_perm"), sem("l_kb"))
        r_ready, r_act, scan_done = sem("r_ready"), sem("r_act"), sem("scan_done")
        u_ready, t2_ready, t2_act, t2_dve = sem("t2_ready_scan"), sem("t2_ready"), sem("t2_act"), sem("t2_dve")
        o_ready, h1_ready, hn_ready, x3_ready, hid_ready = (
            sem("o_ready"), sem("h1_ready"), sem("hn_ready"), sem("x3_ready"), sem("hid_ready"))
        x4_ready, stored = sem("x4_ready"), sem("stored")
        dve2_done, pool2_done, act2_done = sem("dve2_done"), sem("pool2_done"), sem("act2_done")
        setup_dve = sem("setup_dve")
        setup_pool = sem("setup_pool")
        gated = sem("gated")

        counted = [gated, r_ready, r_act, scan_done, x2_loaded, f_ready, f_act, f_dve, pv_ready, pv_act, pv_dve, v_placed, front_done, x_loaded, x_biased, t_ready, t_act, t_dve, qk_squared, qk_normed, split_done, split_stored, rep_loaded, max_placed, s_ready, s_taken, p_ready, p_taken, x1_ready, xr_ready, top_ready, inv_ready, x2_ready, proj_stored, beta_ready, l_loaded, l_squared, l_perm, l_kb, t2_ready, t2_act, t2_dve, o_ready, hn_ready, x3_ready, x4_ready, stored, dve_done, dve2_done, pool2_done]

        F = Handoff(f_ready, {"act": f_act, "dve": f_dve}, [4, 5],
                    [("xT", "act")] + [(f"qkv{t}", "act") for t in range(NT)]
                    + [("qT", "act"), ("kT", "act"), ("nmT", "dve")])
        V = Handoff(pv_ready, {"act": pv_act, "dve": pv_dve}, [6, 7],
                    [u for g in range(NG) for u in ((f"pvT{g}", "act"), (f"pv{g}", "dve"))])
        T = Handoff(t_ready, {"act": t_act, "dve": t_dve}, [0, 1, 2, 3, 6, 7],
                    [("aT", "act"), ("ao", "dve"), ("x1T", "act")]
                    + [(f"L{t}", "act") for t in range(NT)] + [(f"M{t}", "act") for t in range(4)]
                    + [(f"cT{t}", "act") for t in range(NT)] + [(f"dT{t}", "dve") for t in range(4)]
                    + [("sn", "act"), ("slots", "act")] + [(f"h{c}", "act") for c in range(HC)]
                    + [("pr", "act"), ("mo", "dve"), ("x2T", "act")]
                    + [(f"c{t}", "act") for t in range(NT)])
        halves = (0, 1)
        R = Handoff(r_ready, {"act": r_act}, [6, 7],
                    [(f"{n}{j}", "act") for n in "qkv" for j in halves] + [("beta", "act")])
        uses2 = [("o0", "act"), ("o1", "act"), ("oT0", "act"), ("oT1", "act"), ("wo0", "dve"), ("wo1", "dve"),
                  ("hT0", "act"), ("hT1", "act")]
        for f in halves:
            for c in range(HC):
                uses2 += [(f"g{f}{c}", "act"), (f"u{f}{c}", "act")]
            uses2 += [(f"fo{f}", "dve")]
        for f in halves:
            if f == 0:
                uses2 += [("x3T0", "act")]
            for c in range(HC):
                uses2 += [(f"a{f}{c}", "act"), (f"b{f}{c}", "act")]
            uses2 += [(f"m{f}{c}", "act") for c in range(HC)]
            if f == 0:
                uses2 += [("x3T1", "act")]
            uses2 += [(f"n{f}{c}", "act") for c in range(HC)] + [(f"y{f}", "dve")]
        T2 = Handoff(t2_ready, {"act": t2_act, "dve": t2_dve}, list(range(6)), uses2)

        s_units = []
        for it in range(NT):
            per = {0: 4, 1: 2}.get(it, 1)
            for g0 in range(0, NG, per):
                for q in range(4):
                    s_units.append((it, q, list(range(g0, g0 + per))))
        p_units = [(g, jt, pr) for g in range(NG) for jt in range(NT) for pr in range(2)]
        p_off = [0, 512, 896, 1152]
        PU = len(p_units) // NG
        S1, S2, S3 = 26, 36, len(s_units)

        s_jobs = [[(raw_w[:, j, :], None) for j in range(4)], [(raw_slot[:, j, :], None) for j in range(4)],
                  [(raw_f1[:, j, :], None) for j in range(4)], [(raw_f2[:, j, :], None) for j in range(4)]]
        for raw in (raw_h1, raw_h2):
            for ic in range(4):
                s_jobs.append([(raw[:, oc, ic * P:(ic + 1) * P], None) for oc in range(4)])
        s_jobs.append([(raw_w3[:, ic * P:(ic + 1) * P], None) for ic in range(4)])
        s_dst = [None, None, f_w1[:, :], f_w2[:, :]] + [f_h1[:, ic, :] for ic in range(4)] \
            + [f_h2[:, ic, :] for ic in range(4)] + [f_w3[:, :, :]]

        def arena_free(eng):
            eng.wait_ge(w_taken, len(s_jobs))
            eng.wait_ge(rep_init, 32)

        block = ctx.enter_context(nc.Block())

        @block.sync
        def _(sp):
            def load(dst, src, **kw):
                sp.dma_start(dst, src, **kw).then_inc(w_loaded, 16)

            for j, n in enumerate(("Wq", "Wk", "Wv", "Wo")):
                load(raw_w[:, j, :], A[f"L0_attn_{n}"])
            load(raw_slot, A["L0_ffn_slot_embeds"].rearrange("e t d -> (e t) d").rearrange("(c p) d -> p c d", p=P))
            load(raw_f1, A["L1_ffn_w1_w"].rearrange("(c p) d -> p c d", p=P))
            load(raw_f2, A["L1_ffn_w2_w"].rearrange("(c p) d -> p c d", p=P))
            load(raw_h1, A["L1_ffn_h1_w"].rearrange("(c p) d -> p c d", p=P))
            load(raw_h2, A["L1_ffn_h2_w"].rearrange("(c p) d -> p c d", p=P))
            load(raw_w3, A["L1_ffn_w3_w"])
            load(bias_o[:, :], A["L0_attn_bo"].partition_broadcast(P))
            for j, n in enumerate(("qln_g", "qln_b", "kln_g", "kln_b")):
                load(gb_d[j, :, :], A[f"L0_attn_{n}"].partition_broadcast(NH))
            sp.wait_ge(w_loaded, 15 * 16)
            load(qk_gb[:, :], gb_d.rearrange("j h d -> (h d) j"), allow_slow_non_contiguous=True)
            col = lambda n: A[n].rearrange("(d o) -> d o", o=1)
            load(gamma_x[:, :], col("L0_ffn_gamma_x"))
            load(gamma_s[:, :], col("L0_ffn_gamma_slot"))
            load(e_w1[:, :], A["L0_ffn_w1"])
            load(e_w2[:, :, :], A["L0_ffn_w2"].rearrange("(c p) d -> p c d", p=P))
            for j, n in enumerate(("Wq", "Wk", "Wv")):
                load(w_mix[:, j * D:(j + 1) * D], A[f"L1_attn_{n}"])
            load(w_mix[:, 3 * D:], A["L1_attn_Wb"])
            load(w_o1[:, :], A["L1_attn_Wo"])
            load(ln12[:, 0:1], col("L1_attn_ln1"))
            load(ln12[:, 1:2], col("L1_attn_ln2"))
            load(w_g[:, :], A["L1_attn_Wg"])
            load(w_u[:, :], A["L1_attn_Wu"])
            load(w_d[:, :, :], A["L1_attn_Wd"].rearrange("(c p) d -> p c d", p=P))
            for j, n in enumerate(("w1", "w2", "h1", "h2")):
                load(f_s[:, j, :], A[f"L1_ffn_{n}_s"].rearrange("(c p) -> p c", p=P), allow_slow_non_contiguous=True)
            load(f_s3[:, :], col("L1_ffn_w3_s"))
            sp.wait_ge(setup_pool, 2)
            sp.dma_start(q_rep[:, 3, :, :], ones_zeros[:, 0, :]).then_inc(rep_init, 16)
            sp.dma_start(k_rep[:, 3, :, :], ones_zeros[:, 1, :]).then_inc(rep_init, 16)
            sp.wait_ge(rep_init, 32)
            arena_free(sp)

            def load_x(b):
                sp.wait_ge(x_biased, CREDIT + b)
                sp.wait_ge(f_ready, CREDIT + b * len(F.order))
                sp.dma_start(xb, A["L0_attn_x"][bass.ds(b, 1), :, :].rearrange("o (t p) d -> p (o t) d", p=P)) \
                    .then_inc(x_loaded, 16)

            def replicate(b):
                sp.wait_ge(split_done, CREDIT + b + 1)
                for rep, j, parts in ((q_rep, 0, (0, 0, 1)), (k_rep, 1, (0, 1, 0))):
                    for c, part in enumerate(parts):
                        sp.dma_start(rep[:, c, :, :], hilo[:, j, part, :].bitcast(F32)).then_inc(split_stored, 16)
                sp.wait_ge(split_stored, CREDIT + (b + 1) * 96)
                sp.wait_ge(p_ready, CREDIT + b * len(p_units))
                for rep, dst in ((q_rep, qr), (k_rep, kr)):
                    sp.dma_start(dst[:, :, :].bitcast(F32), rep.rearrange("(g h) c d t -> (h c d) g t", g=NG)) \
                        .then_inc(rep_loaded, 16)

            def place_maxima(b):
                sp.wait_ge(f_dve, CREDIT + F.emptied("nmT", b))
                for g in range(NG):
                    sp.dma_start(qr[24:P:32, g, :].bitcast(F32), nm_T[4 * g:4 * g + 4, :].bitcast(F32)) \
                        .then_inc(max_placed, 16)

            def store(b):
                sp.wait_ge(beta_ready, CREDIT + b + 1)
                sp.dma_start(proj_d[bass.ds(b, 1), :, :, :].rearrange("o t p w -> p (o t) w"), proj) \
                    .then_inc(proj_stored, 16)
                sp.dma_start(x2_d[bass.ds(b, 1), :, :, :].rearrange("o t p w -> p (o t) w"), x2) \
                    .then_inc(proj_stored, 16)

            load_x(0)
            replicate(0)
            load_x(1)
            place_maxima(0)
            with sp.Fori(0, B - 2) as i:
                replicate(i + 1)
                place_maxima(i + 1)
                load_x(i + 2)
                store(i)
            replicate(B - 1)
            place_maxima(B - 1)
            store(B - 2)
            store(B - 1)
            sp.wait_ge(proj_stored, CREDIT + B * 32)

            def load_mix(tt):
                sp.wait_ge(l_perm, CREDIT + tt * 4)
                sp.dma_start(mix, proj_d[:, bass.ds(tt, 1), :, :].rearrange("b o p w -> p (b o) w")).then_inc(l_loaded, 16)

            def load_x2(tt, last):
                sp.wait_ge(t2_dve, CREDIT + T2.emptied("fo1", last))
                sp.dma_start(x2t, x2_d[:, bass.ds(tt, 1), :, :].rearrange("b o p w -> p (b o) w")).then_inc(x2_loaded, 16)

            def store_x4(tt, f):
                sp.wait_ge(x4_ready, CREDIT + tt * 2 + f + 1)
                sp.dma_start(out[4 * f:4 * f + 4, bass.ds(tt * P, P), :].rearrange("b p d -> p b d"), x4) \
                    .then_inc(stored, 16)

            load_mix(0)
            sp.dma_start(x2t, x2_d[:, 0:1, :, :].rearrange("b o p w -> p (b o) w")).then_inc(x2_loaded, 16)
            load_mix(1)
            with sp.Fori(0, NT - 2) as i:
                load_mix(i + 2)
                load_x2(i + 1, i)
                store_x4(i, 0)
                store_x4(i, 1)
            load_x2(NT - 1, NT - 2)
            store_x4(NT - 2, 0)
            store_x4(NT - 2, 1)
            store_x4(NT - 1, 0)
            store_x4(NT - 1, 1)
            sp.wait_ge(stored, CREDIT + NT * 32)

        @block.gpsimd
        def _(g):
            for x in counted:
                g.sem_inc(x, CREDIT)
            g.memset(ones_zeros[:, 0, :], 0.0).then_inc(setup_pool, 1)
            g.memset(ones_zeros[:, 1, :], 1.0).then_inc(setup_pool, 1)
            g.memset(ident[:, :], 0.0).then_inc(setup_pool, 1)
            g.memset(mask_qk[:, :], 0.0).then_inc(setup_pool, 1)
            g.memset(mask_kq[:, :], 0.0).then_inc(setup_pool, 1)
            g.wait_ge(setup_pool, 5)
            g.affine_select(out=ident[:, :], in_=ident[:, :], compare_op=ALU.not_equal, fill=1.0,
                            base=0, pattern=[[-1, P]], channel_multiplier=1).then_inc(setup_pool, 1)
            g.affine_select(out=mask_qk[:, :], in_=mask_qk[:, :], compare_op=ALU.is_ge, fill=MASK,
                            base=0, pattern=[[-1, P]], channel_multiplier=1).then_inc(setup_pool, 1)
            g.affine_select(out=mask_kq[:, :], in_=mask_kq[:, :], compare_op=ALU.is_ge, fill=MASK,
                            base=0, pattern=[[1, P]], channel_multiplier=-1).then_inc(setup_pool, 1)
            g.wait_ge(setup_pool, 8)
            g.tensor_copy(ident_b[:, :], ident[:, :]).then_inc(setup_pool, 1)
            arena_free(g)
            g.memset(v_aug, 1.0).then_inc(setup_pool, 1)

            def squares(b):
                g.wait_ge(f_act, CREDIT + F.emptied(f"qkv{NT - 1}", b))
                g.wait_ge(qk_normed, CREDIT + b)
                g.tensor_tensor(qk_sq, qk, qk, ALU.mult).then_inc(qk_squared, 1)

            def low_parts(b):
                g.wait_ge(f_act, CREDIT + F.emptied("kT", b))
                g.tensor_tensor(hilo[:, :, 1, :], qk_T, hilo[:, :, 0, :].bitcast(F32), ALU.subtract) \
                    .then_inc(split_done, 1)

            def place_v(b):
                g.wait_ge(pv_ready, CREDIT + b * len(V.order))
                g.tensor_tensor(v_aug[:, :, :, 0:HD], v_new.rearrange("p t (h d) -> p t h d", d=HD),
                                v_aug[:, :, :, HD:HD + 1].broadcast_to([P, NT, NH, HD]), ALU.mult).then_inc(v_placed, 1)

            def add_bias(b):
                g.wait_ge(x_loaded, CREDIT + (b + 1) * 16)
                g.wait_ge(x1_ready, CREDIT + b)
                g.tensor_tensor(xbo, xb, bias_o[:, :].unsqueeze(1).broadcast_to([P, NT, D]), ALU.add) \
                    .then_inc(x_biased, 1)

            g.wait_ge(setup_pool, 10)
            squares(0)
            low_parts(0)
            place_v(0)
            add_bias(0)
            with g.Fori(0, B - 1) as i:
                squares(i + 1)
                low_parts(i + 1)
                place_v(i + 1)
                add_bias(i + 1)

            g.wait_ge(proj_stored, CREDIT + B * 32)
            def prepare(tt, last):
                g.wait_ge(l_loaded, CREDIT + (tt + 1) * 16)
                g.wait_ge(o_ready, CREDIT + tt)
                if last is not None:
                    g.wait_ge(t2_ready, CREDIT + last * len(T2.order))
                g.wait_ge(l_perm, CREDIT + tt * 4)
                g.wait_ge(r_ready, CREDIT + tt * len(R.order))
                g.tensor_tensor(l_sq, mix[:, :, 0:2 * D], mix[:, :, 0:2 * D], ALU.mult).then_inc(l_squared, 1)
                g.tensor_copy(perm[:, 2, :, :].rearrange("p d (b h) -> p b h d", b=B),
                              mix[:, :, 2 * D:3 * D].rearrange("p b (h d) -> p b h d", d=HD)).then_inc(l_perm, 1)
                g.tensor_copy(beta_p.rearrange("p (b h) -> p b h", b=B), mix[:, :, 3 * D:QW]).then_inc(l_perm, 1)

            def scale_rows(tt):
                g.wait_ge(r_act, CREDIT + R.emptied("beta", tt))
                for j, src in enumerate((k_c, v_c)):
                    g.tensor_tensor(wu[:, :, j * HD:(j + 1) * HD], src,
                                    beta.unsqueeze(2).broadcast_to([P, P, HD]), ALU.mult).then_inc(l_kb, 1)

            def normalise_h(tt):
                g.wait_ge(hn_ready, CREDIT + tt + 1)
                g.tensor_tensor(hn, h1, st2[:, 5, :].unsqueeze(2).broadcast_to([P, B, D]), ALU.mult) \
                    .then_inc(pool2_done, 1)

            def multiply_gates(tt):
                for n, f, before in (("u", 0, None), ("u", 1, "fo0"), ("b", 0, "fo1"), ("b", 1, "y0")):
                    g.wait_ge(t2_ready, CREDIT + (T2.filled(before, tt) if before else tt * len(T2.order)))
                    for c in range(HC):
                        g.wait_ge(t2_act, CREDIT + T2.emptied(f"{n}{f}{c}", tt))
                        g.tensor_tensor(hid_a[:, c, :], up[:, c % 2, :], gate[:, c % 2, :], ALU.mult) \
                            .then_inc(gated, 1)

            prepare(0, None)
            scale_rows(0)
            with g.Fori(0, NT - 1) as i:
                prepare(i + 1, i)
                normalise_h(i)
                scale_rows(i + 1)
                multiply_gates(i)
            normalise_h(NT - 1)
            multiply_gates(NT - 1)

        @block.tensor
        def _(pe):
            pe.wait_ge(w_final, 1)
            pe.wait_ge(setup_pool, 9)
            for j, job in enumerate(s_jobs):
                if j >= 8:
                    pe.wait_ge(w_taken, j - 7)
                for k, (src, _) in enumerate(job):
                    last = pe.transpose(ps[:, j % 8, k * P:(k + 1) * P], src, ident[:, :])
                last.then_inc(w_ready, 1)
            arena_free(pe)

            def fill(R, use, b):
                R.wait_free(pe, use, b)
                return ps[:, R.bank(use), :]

            def transposes(R, use, b, srcs):
                bank = fill(R, use, b)
                for k, src in enumerate(srcs):
                    last = pe.transpose(bank[0:src.shape[1], k * P:(k + 1) * P], src, ident[:, :])
                last.then_inc(R.ready, 1)

            def transpose_x(b):
                pe.wait_ge(x_loaded, CREDIT + (b + 1) * 16)
                transposes(F, "xT", b, [xb[:, t, :] for t in range(NT)])

            def project_qkv(b):
                pe.wait_ge(f_act, CREDIT + F.emptied("xT", b))
                for t in range(NT):
                    pe.matmul(fill(F, f"qkv{t}", b)[:, 0:3 * D], xT[:, t * P:(t + 1) * P], w_qkv[:, :],
                              start=True, stop=True).then_inc(f_ready, 1)

            def transpose_qk(b):
                pe.wait_ge(qk_normed, CREDIT + b + 1)
                transposes(F, "qT", b, [qk_n[:, t, 0:D] for t in range(NT)])
                transposes(F, "kT", b, [qk_n[:, t, D:2 * D] for t in range(NT)])

            def scores_for_maxima(b, first, end):
                if first == 0:
                    pe.wait_ge(rep_loaded, CREDIT + (b + 1) * 32)
                    pe.wait_ge(f_act, CREDIT + F.emptied("kT", b))
                for k in range(first, end):
                    it, q, gs = s_units[k]
                    pe.wait_ge(s_taken, CREDIT + b * len(s_units) + max(k - 1, 0))
                    w = (it + 1) * P
                    for n, gg in enumerate(gs):
                        rows = slice(32 * q, 32 * q + 32)
                        bank = ps[:, 4 + k % 2, n * w:(n + 1) * w]
                        pe.matmul(bank, qr[rows, gg, it * P:(it + 1) * P], kr[rows, gg, 0:w], start=True, stop=False)
                        last = pe.matmul(bank[:, it * P:w], ident_b[:, :], mask_qk[:, :], start=False, stop=True)
                    last.then_inc(s_ready, 1)

            def transpose_maxima(b):
                pe.wait_ge(s_taken, CREDIT + (b + 1) * len(s_units))
                transposes(F, "nmT", b, [neg_max[:, t, :] for t in range(NT)])

            def scores(b, gg, h4):
                for k in range(gg * PU + 2 * h4, gg * PU + 2 * h4 + 2):
                    _, jt, pr = p_units[k]
                    pe.wait_ge(p_taken, CREDIT + b * len(p_units) + max(k - 1, 0))
                    for n in range(2):
                        rows = slice(32 * (2 * pr + n), 32 * (2 * pr + n) + 32)
                        bank = ps[:, 2 * (k % 2) + n, 0:S - jt * P]
                        pe.matmul(bank, kr[rows, gg, jt * P:(jt + 1) * P], qr[rows, gg, jt * P:S],
                                  start=True, stop=False)
                        last = pe.matmul(bank[:, 0:P], ident_b[:, :], mask_kq[:, :], start=False, stop=True)
                    last.then_inc(p_ready, 1)

            def products(b, gg, h4):
                if h4 == 0:
                    pe.wait_ge(p_taken, CREDIT + b * len(p_units) + PU * (gg + 1))
                    fill(V, f"pvT{gg}", b)
                bank = ps[:, V.bank(f"pvT{gg}"), :]
                for jt in range(NT):
                    last = pe.matmul(bank[32 * h4:32 * h4 + 32, jt * P:S], v_aug[:, jt, 4 * gg + h4, :],
                                     prob[:, gg % 2, h4, p_off[jt]:p_off[jt] + S - jt * P],
                                     start=(jt == 0), stop=(jt == NT - 1))
                if h4 == 3:
                    last.then_inc(pv_ready, 1)

            def turn_products(b, gg):
                pe.wait_ge(pv_act, CREDIT + V.emptied(f"pvT{gg}", b))
                transposes(V, f"pv{gg}", b, [pv_T[:, gg % 2, t * P:(t + 1) * P] for t in range(NT)])

            def batch(i, front):
                pe.wait_ge(t_act, CREDIT + i * T.total["act"])
                pe.wait_ge(t_dve, CREDIT + i * T.total["dve"])
                pe.wait_ge(max_placed, CREDIT + (i + 1) * 64)
                if front is not None:
                    transpose_x(front)
                for gg in range(NG + 1):
                    for h4 in range(4):
                        if gg < NG:
                            scores(i, gg, h4)
                        if (gg, h4) == (0, 0):
                            pe.wait_ge(v_placed, CREDIT + i + 1)
                            if front is not None:
                                project_qkv(front)
                        if gg >= 1:
                            products(i, gg - 1, h4)
                        if gg >= 2 and h4 == 1:
                            turn_products(i, gg - 2)
                        if (gg, h4) == QK_TURNED and front is not None:
                            transpose_qk(front)
                turn_products(i, NG - 1)
                pe.wait_ge(pv_dve, CREDIT + V.emptied(f"pv{NG - 1}", i))
                transposes(T, "aT", i, [att[:, t, :] for t in range(NT)])
                pe.wait_ge(t_act, CREDIT + T.emptied("aT", i))
                bank = fill(T, "ao", i)
                for t in range(NT):
                    last = pe.matmul(bank[:, t * P:(t + 1) * P], act_T[:, t * P:(t + 1) * P], w_out[:, :],
                                     start=True, stop=True)
                last.then_inc(t_ready, 1)
                if front is not None:
                    scores_for_maxima(front, 0, S1)
                pe.wait_ge(xr_ready, CREDIT + i + 1)
                transposes(T, "x1T", i, [xr[:, t, :] for t in range(NT)])
                pe.wait_ge(t_act, CREDIT + T.emptied("x1T", i))
                for t in range(NT):
                    pe.matmul(fill(T, f"L{t}", i), act_T[:, t * P:(t + 1) * P], slot_T[:, :], start=True, stop=True) \
                        .then_inc(t_ready, 1)
                for c in range(4):
                    pe.matmul(fill(T, f"M{c}", i), slot_T[:, c * P:(c + 1) * P], act_T, start=True, stop=True) \
                        .then_inc(t_ready, 1)
                if front is not None:
                    scores_for_maxima(front, S1, S2)
                for t in range(NT):
                    pe.wait_ge(t_act, CREDIT + T.emptied(f"L{t}", i))
                    transposes(T, f"cT{t}", i, [comb[:, t, c * P:(c + 1) * P] for c in range(4)])
                for c in range(4):
                    pe.wait_ge(t_act, CREDIT + T.emptied(f"M{c}", i))
                    transposes(T, f"dT{c}", i, [disp_T[:, c, t * P:(t + 1) * P] for t in range(NT)])
                pe.wait_ge(t_dve, CREDIT + T.emptied("dT3", i))
                bank = fill(T, "sn", i)
                for c in range(4):
                    for t in range(NT):
                        last = pe.matmul(bank[:, c * P:(c + 1) * P], disp[:, t, c * P:(c + 1) * P], xr[:, t, :],
                                         start=(t == 0), stop=(t == NT - 1))
                last.then_inc(t_ready, 1)
                pe.wait_ge(t_act, CREDIT + T.emptied("sn", i))
                transposes(T, "slots", i, [slots_n[:, c, :] for c in range(4)])
                pe.wait_ge(t_act, CREDIT + T.emptied("slots", i))
                for c in range(HC):
                    pe.matmul(fill(T, f"h{c}", i), e_w1[:, c * P:(c + 1) * P], slots, start=True, stop=True) \
                        .then_inc(t_ready, 1)
                if front is not None:
                    scores_for_maxima(front, S2, S3)
                    transpose_maxima(front)
                pe.wait_ge(t_act, CREDIT + T.emptied(f"h{HC - 1}", i))
                bank = fill(T, "pr", i)
                for n in range(4):
                    for c in range(HC):
                        last = pe.matmul(bank[:, n * P:(n + 1) * P], h_T[:, c, n * P:(n + 1) * P], e_w2[:, c, :],
                                         start=(c == 0), stop=(c == HC - 1))
                last.then_inc(t_ready, 1)
                pe.wait_ge(t_act, CREDIT + T.emptied("pr", i))
                bank = fill(T, "mo", i)
                for t in range(NT):
                    for n in range(4):
                        last = pe.matmul(bank[:, t * P:(t + 1) * P], comb_T[:, n, t * P:(t + 1) * P], done_e[:, n, :],
                                         start=(n == 0), stop=(n == 3))
                last.then_inc(t_ready, 1)
                pe.wait_ge(x2_ready, CREDIT + i + 1)
                transposes(T, "x2T", i, [x2[:, t, :] for t in range(NT)])
                pe.wait_ge(t_act, CREDIT + T.emptied("x2T", i))
                for t in range(NT):
                    pe.matmul(fill(T, f"c{t}", i)[:, 0:QW], act_T[:, t * P:(t + 1) * P], w_mix[:, :],
                              start=True, stop=True).then_inc(t_ready, 1)

            transpose_x(0)
            project_qkv(0)
            transpose_qk(0)
            scores_for_maxima(0, 0, len(s_units))
            transpose_maxima(0)
            with pe.Fori(0, B - 1) as i:
                batch(i, i + 1)
            batch(B - 1, None)

            pe.wait_ge(t_act, CREDIT + B * T.total["act"])
            pe.wait_ge(t_dve, CREDIT + B * T.total["dve"])
            def transpose_qkv(tt):
                pe.wait_ge(l_perm, CREDIT + (tt + 1) * 4)
                for w, n in enumerate("qkv"):
                    for j in halves:
                        transposes(R, f"{n}{j}", tt, [perm[:, w, 4 * j + d, :] for d in range(4)])
                R.wait_free(pe, "beta", tt)
                pe.transpose(ps[:, R.bank("beta"), 0:P], beta_p, ident[:, :]).then_inc(r_ready, 1)

            def tile(i, ahead):
                def fill2(use):
                    T2.wait_free(pe, use, i)
                    return ps[:, T2.bank(use), :]

                def transposes2(use, srcs):
                    bank = fill2(use)
                    for k, src in enumerate(srcs):
                        last = pe.transpose(bank[:, k * P:(k + 1) * P], src, ident[:, :])
                    last.then_inc(t2_ready, 1)

                pe.wait_ge(o_ready, CREDIT + i + 1)
                for j in halves:
                    transposes2(f"o{j}", [o_c[:, 4 * j + d, :] for d in range(4)])
                pe.wait_ge(t2_act, CREDIT + T2.emptied("o1", i))
                for j in halves:
                    transposes2(f"oT{j}", [o_tok[:, 4 * j + b, :] for b in range(4)])
                for j in halves:
                    pe.wait_ge(t2_act, CREDIT + T2.emptied(f"oT{j}", i))
                    bank = fill2(f"wo{j}")
                    for b in range(4):
                        last = pe.matmul(bank[:, b * P:(b + 1) * P], o_T[:, 4 * j + b, :], w_o1[:, :],
                                         start=True, stop=True)
                    last.then_inc(t2_ready, 1)
                pe.wait_ge(pool2_done, CREDIT + i + 1)
                for j in halves:
                    transposes2(f"hT{j}", [hn[:, 4 * j + b, :] for b in range(4)])
                if ahead is not None:
                    transpose_qkv(ahead)

                def by_token(use, hid, w):
                    bank = fill2(use)
                    for b in range(4):
                        for c in range(HC):
                            last = pe.matmul(bank[:, b * P:(b + 1) * P], hid[:, c, b * P:(b + 1) * P],
                                             w[:, c, :], start=(c == 0), stop=(c == HC - 1))
                    last.then_inc(t2_ready, 1)

                def by_hidden(use, w, src):
                    pe.matmul(fill2(use), w, src, start=True, stop=True).then_inc(t2_ready, 1)

                def square_layer(use, f, w, src):
                    for c in range(HC):
                        bank = fill2(f"{use}{f}{c}")
                        for k in range(HC):
                            last = pe.matmul(bank, w[:, k, c * P:(c + 1) * P], src[:, k, :],
                                             start=(k == 0), stop=(k == HC - 1))
                        last.then_inc(t2_ready, 1)

                def transpose_x3(f):
                    pe.wait_ge(x3_ready, CREDIT + i * 2 + f + 1)
                    transposes2(f"x3T{f}", [x3[:, 4 * f + b, :] for b in range(4)])

                for f in halves:
                    pe.wait_ge(t2_act, CREDIT + T2.emptied(f"hT{f}", i))
                    src = hn_T[:, 4 * f:4 * f + 4, :]
                    for c in range(HC):
                        by_hidden(f"g{f}{c}", w_g[:, c * P:(c + 1) * P], src)
                        by_hidden(f"u{f}{c}", w_u[:, c * P:(c + 1) * P], src)
                    pe.wait_ge(gated, CREDIT + i * 16 + 4 * (f + 1))
                    by_token(f"fo{f}", hid_a, w_d)
                for f in halves:
                    if f == 0:
                        transpose_x3(0)
                    pe.wait_ge(t2_act, CREDIT + T2.emptied(f"x3T{f}", i))
                    for c in range(HC):
                        by_hidden(f"a{f}{c}", f_w1[:, c * P:(c + 1) * P], x3_T[:, f, :])
                        by_hidden(f"b{f}{c}", f_w2[:, c * P:(c + 1) * P], x3_T[:, f, :])
                    pe.wait_ge(gated, CREDIT + i * 16 + 8 + 4 * (f + 1))
                    square_layer("m", f, f_h1, hid_a)
                    if f == 0:
                        transpose_x3(1)
                    pe.wait_ge(t2_act, CREDIT + T2.emptied(f"m{f}{HC - 1}", i))
                    square_layer("n", f, f_h2, hid_b)
                    pe.wait_ge(t2_act, CREDIT + T2.emptied(f"n{f}{HC - 1}", i))
                    by_token(f"y{f}", hid_a, f_w3)

            transpose_qkv(0)
            with pe.Fori(0, NT - 1) as i:
                tile(i, i + 1)
            tile(NT - 1, None)

        @block.scalar
        def _(act):
            for j, dst in enumerate(s_dst):
                if dst is not None:
                    act.wait_ge(w_ready, j + 1)
                    act.wait_ge(w_taken, j)
                    src = ps[:, j % 8, :]
                    if len(dst.shape) == 3:
                        src = src.rearrange("p (a b) -> p a b", a=4)
                    act.activation(dst, src, ACT.Copy).then_inc(w_taken, 1)
            arena_free(act)
            act.wait_ge(setup_pool, 10)

            def take(R, use, b, dst, src, func=ACT.Copy, **kw):
                act.wait_ge(R.ready, CREDIT + R.filled(use, b))
                return act.activation(dst, src(ps[:, R.bank(use), :]), func, **kw)

            def take_xT(b):
                act.wait_ge(qk_normed, CREDIT + b)
                take(F, "xT", b, xT, lambda p: p).then_inc(f_act, 1)

            def take_qkv(b):
                act.wait_ge(qk_normed, CREDIT + b)
                act.wait_ge(v_placed, CREDIT + b)
                for t in range(NT):
                    take(F, f"qkv{t}", b, qk[:, t, :], lambda p: p[:, 0:2 * D])
                    act.activation(v_new[:, t, :], ps[:, F.bank(f"qkv{t}"), 2 * D:3 * D], ACT.Copy).then_inc(f_act, 1)

            def take_qk_T(b):
                act.wait_ge(split_done, CREDIT + b)
                act.wait_ge(split_stored, CREDIT + b * 96)
                for j, n in enumerate("qk"):
                    for dst in (qk_T[:, j, :], hilo[:, j, 0, :]):
                        r = take(F, f"{n}T", b, dst, lambda p: p, ACT.Identity, scale=qk_gb[:, 2 * j:2 * j + 1],
                                 bias=qk_gb[:, 2 * j + 1:2 * j + 2])
                    r.then_inc(f_act, 1)

            def exponentials(b, gg, first, end):
                for k in range(gg * PU + first, gg * PU + end):
                    _, jt, pr = p_units[k]
                    act.wait_ge(p_ready, CREDIT + b * len(p_units) + k + 1)
                    if k % PU == 0:
                        if gg >= 2:
                            act.wait_ge(pv_ready, CREDIT + V.filled(f"pvT{gg - 2}", b))
                        else:
                            act.wait_ge(pv_ready, CREDIT + b * len(V.order))
                    w = S - jt * P
                    bank = 2 * (k % 2)
                    act.activation(prob[:, gg % 2, 2 * pr:2 * pr + 2, p_off[jt]:p_off[jt] + w],
                                   ps[:, bank:bank + 2, 0:w], ACT.Exp).then_inc(p_taken, 1)

            def take_products(b, gg):
                if gg >= 2:
                    act.wait_ge(pv_ready, CREDIT + V.filled(f"pv{gg - 2}", b))
                else:
                    act.wait_ge(pv_ready, CREDIT + b * len(V.order))
                take(V, f"pvT{gg}", b, pv_T[:, gg % 2, :], lambda p: p).then_inc(pv_act, 1)

            def batch(i, front):
                if front is not None:
                    take_xT(front)
                for gg in range(NG):
                    for h4 in range(4):
                        exponentials(i, gg, 2 * h4, 2 * h4 + 1)
                        if gg >= 2 and h4 == 0:
                            take_products(i, gg - 2)
                        exponentials(i, gg, 2 * h4 + 1, 2 * h4 + 2)
                        if (gg, h4) == (0, 0) and front is not None:
                            take_qkv(front)
                        if (gg, h4) == QK_TURNED and front is not None:
                            take_qk_T(front)
                take_products(i, NG - 2)
                take_products(i, NG - 1)
                act.wait_ge(t_ready, CREDIT + i * len(T.order))
                take(T, "aT", i, act_T, lambda p: p).then_inc(t_act, 1)
                act.wait_ge(t_ready, CREDIT + T.filled("ao", i))
                take(T, "x1T", i, act_T, lambda p: p).then_inc(t_act, 1)
                for j, (n, dst) in enumerate((("L", comb), ("M", disp_T))):
                    for t in range(4):
                        act.wait_ge(top_ready, CREDIT + i * 8 + 4 * j + t + 1)
                        take(T, f"{n}{t}", i, dst[:, t, :], lambda p: p, ACT.Exp, bias=neg_top[:, j, t:t + 1],
                             accum_out=z_sum[:, j, t:t + 1]).then_inc(t_act, 1)
                for t in range(NT):
                    take(T, f"cT{t}", i, comb_T[:, :, t * P:(t + 1) * P],
                         lambda p: p.rearrange("p (c s) -> p c s", c=4)).then_inc(t_act, 1)
                act.wait_ge(inv_ready, CREDIT + i + 1)
                for c in range(4):
                    r = take(T, "sn", i, slots_n[:, c, :], lambda p: p[:, c * P:(c + 1) * P], ACT.Identity,
                             scale=z_inv[:, 1, c:c + 1])
                r.then_inc(t_act, 1)
                take(T, "slots", i, slots, lambda p: p, ACT.Identity, scale=gamma_x[:, 0:1]).then_inc(t_act, 1)
                for c in range(HC):
                    take(T, f"h{c}", i, h_T[:, c, :], lambda p: p, ACT.Gelu).then_inc(t_act, 1)
                take(T, "pr", i, done_e, lambda p: p.rearrange("p (c s) -> p c s", c=4)).then_inc(t_act, 1)
                take(T, "x2T", i, act_T, lambda p: p).then_inc(t_act, 1)
                act.wait_ge(proj_stored, CREDIT + i * 32)
                act.wait_ge(x2_ready, CREDIT + i + 1)
                for t in range(NT):
                    take(T, f"c{t}", i, proj[:, t, 0:3 * D], lambda p: p[:, 0:3 * D], ACT.Silu, scale=st[:, 5, t:t + 1])
                    act.activation(proj[:, t, 3 * D:QW], ps[:, T.bank(f"c{t}"), 3 * D:QW], ACT.Tanh,
                                   scale=st[:, 7, t:t + 1]).then_inc(t_act, 1)

            take_xT(0)
            take_qkv(0)
            take_qk_T(0)
            with act.Fori(0, B - 1) as i:
                batch(i, i + 1)
            batch(B - 1, None)

            def take_qkv2(tt):
                act.wait_ge(o_ready, CREDIT + tt)
                for n, dst in (("q", q_c), ("k", k_c), ("v", v_c)):
                    for j in halves:
                        take(R, f"{n}{j}", tt, dst[:, :, 4 * j:4 * j + 4].rearrange("p t d -> p d t"),
                             lambda b: b.rearrange("p (d t) -> p d t", d=4)).then_inc(r_act, 1)
                take(R, "beta", tt, beta, lambda b: b[:, 0:P]).then_inc(r_act, 1)

            def tile(i, ahead):
                def take2(use, dst, src=lambda b: b, func=ACT.Copy, **kw):
                    act.wait_ge(t2_ready, CREDIT + T2.filled(use, i))
                    return act.activation(dst, src(ps[:, T2.bank(use), :]), func, **kw)

                for j in halves:
                    take2(f"o{j}", o_tok.rearrange("p b (h d) -> p d (b h)", d=HD)[:, 4 * j:4 * j + 4, :],
                          lambda b: b.rearrange("p (d t) -> p d t", d=4)).then_inc(t2_act, 1)
                for j in halves:
                    take2(f"oT{j}", o_T[:, 4 * j:4 * j + 4, :], lambda b: b.rearrange("p (d t) -> p d t", d=4)) \
                        .then_inc(t2_act, 1)
                for j in halves:
                    take2(f"hT{j}", hn_T[:, 4 * j:4 * j + 4, :], lambda b: b.rearrange("p (d t) -> p d t", d=4)) \
                        .then_inc(t2_act, 1)
                if ahead is not None:
                    take_qkv2(ahead)

                def gates(n, m, f, k0, scales):
                    for c in range(HC):
                        act.wait_ge(gated, CREDIT + i * 16 + max(k0 + c - 1, 0))
                        kw = [{"scale": f_s[:, j, c:c + 1]} if scales else {} for j in (0, 1)]
                        take2(f"{n}{f}{c}", gate[:, c % 2, :], func=ACT.Silu, **kw[0]).then_inc(t2_act, 1)
                        take2(f"{m}{f}{c}", up[:, c % 2, :], func=ACT.Identity, **kw[1]).then_inc(t2_act, 1)

                def gelus(use, f, j, dst):
                    for c in range(HC):
                        take2(f"{use}{f}{c}", dst[:, c, :], func=ACT.Gelu, scale=f_s[:, j, c:c + 1]).then_inc(t2_act, 1)

                for f in halves:
                    gates("g", "u", f, 4 * f, False)
                for f in halves:
                    if f == 0:
                        take2("x3T0", x3_T[:, 0, :]).then_inc(t2_act, 1)
                    gates("a", "b", f, 8 + 4 * f, True)
                    gelus("m", f, 2, hid_b)
                    if f == 0:
                        take2("x3T1", x3_T[:, 1, :]).then_inc(t2_act, 1)
                    gelus("n", f, 3, hid_a)

            act.wait_ge(proj_stored, CREDIT + B * 32)
            take_qkv2(0)
            with act.Fori(0, NT - 1) as i:
                tile(i, i + 1)
            tile(NT - 1, None)

        @block.vector
        def _(v):
            def rsqrt_steps(o, y, x, t):
                yield o.mark(v.tensor_scalar(y.bitcast(I32), x.bitcast(I32), -0.5, RSQRT_SEED, ALU.mult, ALU.add))
                yield o.mark(v.tensor_tensor(t, y, y, ALU.mult))
                yield o.mark(v.scalar_tensor_tensor(t, t, -0.5, x, ALU.mult, ALU.mult))
                yield o.mark(v.scalar_tensor_tensor(y, t, 1.5, y, ALU.add, ALU.mult))
                yield o.mark(v.tensor_tensor(t, y, y, ALU.mult))
                yield o.mark(v.tensor_tensor(t, t, x, ALU.mult))
                yield o.mark(v.scalar_tensor_tensor(t, t, -10.0 / 3, t, ALU.add, ALU.mult))
                yield o.mark(v.scalar_tensor_tensor(y, t, 5.0, y, ALU.add, ALU.mult))

            def rsqrt(o, y, x, t):
                for _ in rsqrt_steps(o, y, x, t):
                    o.complete()

            def layer_norm(o, dst, y, stats, s, n):
                for t in range(n):
                    o.mark(v.bn_stats(stats[:, t, :], y[:, t, :]))
                o.complete()
                mean_e, mean_o = stats[:, 0:n, 1], stats[:, 0:n, 4]
                o.mark(v.tensor_tensor(s[:, 0, 0:n], mean_e, mean_o, ALU.add))
                o.mark(v.tensor_tensor(s[:, 1, 0:n], mean_e, mean_o, ALU.subtract))
                o.step(v.tensor_tensor(s[:, 2, 0:n], stats[:, 0:n, 2], stats[:, 0:n, 5], ALU.add))
                o.mark(v.tensor_scalar(s[:, 0, 0:n], s[:, 0, 0:n], 0.5, None, ALU.mult))
                o.mark(v.scalar_tensor_tensor(s[:, 1, 0:n], s[:, 1, 0:n], 0.25 * RSQRT_SCALE, s[:, 1, 0:n],
                                              ALU.mult, ALU.mult))
                o.step(v.tensor_scalar(s[:, 2, 0:n], s[:, 2, 0:n], RSQRT_SCALE / D, RSQRT_SCALE * LN_EPS,
                                       ALU.mult, ALU.add))
                o.step(v.tensor_tensor(s[:, 2, 0:n], s[:, 2, 0:n], s[:, 1, 0:n], ALU.add))
                rsqrt(o, s[:, 3, 0:n], s[:, 2, 0:n], s[:, 4, 0:n])
                for t in range(n):
                    r = v.tensor_scalar(dst[:, t, :], y[:, t, :], s[:, 0, t:t + 1], s[:, 3, t:t + 1],
                                        ALU.subtract, ALU.mult)
                    if t < n - 1:
                        o.mark(r)
                return r

            def scaled(dst, y, s, n):
                return v.tensor_tensor(dst, y, s.unsqueeze(2).broadcast_to([P, n, D]), ALU.mult)

            o = Order(v, setup_dve, 0, 0, 0)
            v.wait_ge(w_loaded, (W_TOTAL) * 16)
            o.step(v.tensor_tensor(slot_sq, raw_slot, raw_slot, ALU.mult))
            o.step(v.tensor_reduce(slot_n, slot_sq, X, ALU.add))
            o.step(v.tensor_scalar(slot_n, slot_n, 1e-24, RSQRT_SCALE, ALU.max, ALU.mult))
            rsqrt(o, slot_r, slot_n, slot_t)
            o.step(v.tensor_scalar(slot_r, slot_r, float(D) ** 0.5, None, ALU.mult))
            o.step(scaled(raw_slot, raw_slot, slot_r, 4))
            o.step(v.tensor_tensor(gamma_s[:, :], gamma_s[:, :], gamma_x[:, :], ALU.mult))
            o.step(v.tensor_scalar(raw_w3, raw_w3, f_s3[:, 0:1], None, ALU.mult))
            o.step(v.tensor_scalar(qk_gb[:, :], qk_gb[:, :], float(D) ** -0.25, None, ALU.mult))
            o.step(v.tensor_scalar(w_mix[:, :], w_mix[:, :], ln12[:, 0:1], None, ALU.mult))
            o.step(v.tensor_scalar(w_g[:, :], w_g[:, :], ln12[:, 1:2], None, ALU.mult))
            v.tensor_scalar(w_u[:, :], w_u[:, :], ln12[:, 1:2], None, ALU.mult).then_inc(w_final, 1)
            v.wait_ge(w_ready, 1)
            v.wait_ge(w_final, 1)
            o.step(v.tensor_reduce(centre, ps[:, 0, 0:2 * D].rearrange("p (g d) -> p g d", d=HD), X, ALU.add))
            o.step(v.tensor_scalar(centre, centre, -1.0 / HD, None, ALU.mult))
            o.step(v.tensor_tensor(w_qkv[:, 0:2 * D].rearrange("p (g d) -> p g d", d=HD),
                                   ps[:, 0, 0:2 * D].rearrange("p (g d) -> p g d", d=HD),
                                   centre.unsqueeze(2).broadcast_to([P, 2 * NH, HD]), ALU.add))
            o.step(v.tensor_copy(w_qkv[:, 2 * D:3 * D], ps[:, 0, 2 * D:3 * D]))
            v.tensor_copy(w_out[:, :], ps[:, 0, 3 * D:4 * D]).then_inc(w_taken, 1)
            v.wait_ge(w_ready, 2)
            v.tensor_scalar(slot_T[:, :], ps[:, 1, :], gamma_s[:, 0:1], None, ALU.mult).then_inc(w_taken, 1)
            assert o.n == DVE_SETUP, ('DVE_SETUP', o.n, 0)
            arena_free(v)

            def arrived(R, use, b):
                v.wait_ge(R.ready, CREDIT + R.filled(use, b))
                return ps[:, R.bank(use), :]

            def norms(b):
                o = Order(v, front_done, DVE_FRONT, b, CREDIT)
                v.wait_ge(qk_squared, CREDIT + b + 1)
                o.step(v.tensor_reduce(qk_var, qk_sq.rearrange("p t (g d) -> p (t g) d", d=HD), X, ALU.add))
                o.step(v.tensor_scalar(qk_var, qk_var, RSQRT_SCALE / HD, RSQRT_SCALE * LN_EPS, ALU.mult, ALU.add))
                rsqrt(o, qk_r, qk_var, qk_t)
                v.tensor_tensor(qk_n.rearrange("p t (g d) -> p (t g) d", d=HD),
                                qk.rearrange("p t (g d) -> p (t g) d", d=HD),
                                qk_r.unsqueeze(2).broadcast_to([P, P, HD]), ALU.mult).then_inc(qk_normed, 1)
                o.end('DVE_FRONT')

            def maximum(b, k):
                it, q, gs = s_units[k]
                v.wait_ge(s_ready, CREDIT + b * len(s_units) + k + 1)
                w = (it + 1) * P
                v.tensor_reduce(neg_max[:, it, 4 * gs[0] + q:4 * gs[-1] + q + 1:4],
                                ps[:, 4 + k % 2, 0:len(gs) * w].rearrange("p (n w) -> p n w", w=w),
                                X, ALU.max, negate=True).then_inc(s_taken, 1)

            def take_maxima(b):
                v.wait_ge(max_placed, CREDIT + b * 64)
                v.tensor_copy(nm_T[:, :], arrived(F, "nmT", b)[0:NH, :]).then_inc(f_dve, 1)

            def batch(i, front):
                o = Order(v, dve_done, DVE1, i, CREDIT)
                s = st
                reduced = 0

                def reduce_to(end):
                    nonlocal reduced
                    if front is not None:
                        for k in range(reduced, end):
                            maximum(front, k)
                        reduced = max(end, reduced)

                if front is not None:
                    norms(front)
                for g in range(NG):
                    pv = arrived(V, f"pv{g}", i).rearrange("p (t h d) -> p t h d", t=NT, h=4)
                    o.step(v.reciprocal(rec, pv[:, :, :, HD]))
                    if g == 0:
                        v.wait_ge(t_ready, CREDIT + i * len(T.order))
                    v.tensor_tensor(att[:, :, g * 32:(g + 1) * 32].rearrange("p t (h d) -> p t h d", d=HD),
                                    pv[:, :, :, 0:HD], rec.unsqueeze(3).broadcast_to([P, NT, 4, HD]),
                                    ALU.mult).then_inc(pv_dve, 1)
                    v.wait_ge(pv_dve, CREDIT + V.emptied(f"pv{g}", i))
                v.wait_ge(x_biased, CREDIT + i + 1)
                v.tensor_tensor(y1, arrived(T, "ao", i).rearrange("p (t d) -> p t d", d=D), xbo, ALU.add).then_inc(t_dve, 1)
                v.wait_ge(t_dve, CREDIT + T.emptied("ao", i))
                o.between = lambda: reduce_to(min(reduced + 1, S1))
                layer_norm(o, x1, y1, bn1, s, NT).then_inc(x1_ready, 1)
                v.wait_ge(x1_ready, CREDIT + i + 1)
                o.step(v.tensor_tensor(y_sq, x1, x1, ALU.mult))
                o.step(v.tensor_reduce(s[:, 1, :], y_sq, X, ALU.add))
                o.step(v.tensor_scalar(s[:, 1, :], s[:, 1, :], 1e-24, RSQRT_SCALE, ALU.max, ALU.mult))
                rsqrt(o, s[:, 3, :], s[:, 1, :], s[:, 4, :])
                o.step(v.tensor_scalar(s[:, 6, :], s[:, 3, :], float(D) ** 0.5, None, ALU.mult))
                o.between = None
                reduce_to(S1)
                scaled(xr, x1, s[:, 6, :], NT).then_inc(xr_ready, 1)
                for j, n in enumerate("LM"):
                    for t in range(4):
                        v.tensor_reduce(neg_top[:, j, t:t + 1], arrived(T, f"{n}{t}", i), X, ALU.max, negate=True) \
                            .then_inc(top_ready, 1)
                reduce_to(S2)
                v.wait_ge(t_act, CREDIT + T.emptied("M3", i))
                v.reciprocal(z_inv, z_sum).then_inc(inv_ready, 1)
                for c in range(4):
                    v.tensor_copy(disp[:, :, c * P:(c + 1) * P],
                                  arrived(T, f"dT{c}", i).rearrange("p (t n) -> p t n", t=NT)).then_inc(t_dve, 1)
                if front is not None:
                    reduce_to(S3)
                    take_maxima(front)
                v.wait_ge(proj_stored, CREDIT + i * 32)
                v.wait_ge(inv_ready, CREDIT + i + 1)
                v.tensor_tensor(y1, arrived(T, "mo", i).rearrange("p (t d) -> p t d", d=D),
                                z_inv[:, 0, :].unsqueeze(2).broadcast_to([P, NT, D]), ALU.mult).then_inc(t_dve, 1)
                v.wait_ge(t_dve, CREDIT + T.emptied("mo", i))
                o.step(v.tensor_tensor(y1, y1, x1, ALU.add))
                o.step(layer_norm(o, x2, y1, bn1, s, NT))
                o.step(v.tensor_tensor(y_sq, x2, x2, ALU.mult))
                o.step(v.tensor_reduce(s[:, 1, :], y_sq, X, ALU.add))
                o.step(v.tensor_scalar(s[:, 2, :], s[:, 1, :], RSQRT_SCALE / D, RSQRT_SCALE * 1e-6, ALU.mult, ALU.add))
                rsqrt(o, s[:, 5, :], s[:, 2, :], s[:, 4, :])
                v.tensor_scalar(s[:, 7, :], s[:, 5, :], 0.5, None, ALU.mult).then_inc(x2_ready, 1)
                v.wait_ge(t_act, CREDIT + (i + 1) * T.total["act"])
                v.tensor_scalar(proj[:, :, 3 * D:QW], proj[:, :, 3 * D:QW], 0.5, 0.5, ALU.mult, ALU.add) \
                    .then_inc(beta_ready, 1)
                o.end('DVE1')

            norms(0)
            for k in range(len(s_units)):
                maximum(0, k)
            take_maxima(0)
            with v.Fori(0, B - 1) as i:
                batch(i, i + 1)
            batch(B - 1, None)

            v.wait_ge(proj_stored, CREDIT + B * 32)
            v.memset(k_u[:, 0, :, :, CH], 0.0).then_inc(setup_dve, 1)
            v.wait_ge(setup_dve, DVE_SETUP + 1)
            def normalise_qk(tt, o, last):
                v.wait_ge(l_squared, CREDIT + tt + 1)
                yield o.mark(v.tensor_reduce(l_var, l_sq.rearrange("p b (g d) -> p (b g) d", d=HD), X, ALU.add))
                yield o.mark(v.tensor_scalar(l_var, l_var, 1e-6, RSQRT_SCALE, ALU.add, ALU.mult))
                yield from rsqrt_steps(o, l_r, l_var, l_t)
                v.wait_ge(r_ready, CREDIT + tt * len(R.order))
                if last is not None:
                    v.wait_ge(t2_ready, CREDIT + last * len(T2.order))
                rr = l_r.rearrange("p (b w h) -> p b w h", b=B, w=2)
                for w in range(2):
                    yield v.tensor_tensor(perm[:, w, :, :].rearrange("p d (b h) -> p b h d", b=B),
                                          mix[:, :, w * D:(w + 1) * D].rearrange("p b (h d) -> p b h d", d=HD),
                                          rr[:, :, w, :].unsqueeze(3).broadcast_to([P, B, NH, HD]), ALU.mult) \
                        .then_inc(l_perm, 1)

            def scan(tt, o, wait_o):
                v.wait_ge(r_act, CREDIT + (tt + 1) * len(R.order))
                kc = k_c.rearrange("p (c j) d -> p c j d", j=CH)
                qc = q_c.rearrange("p (c j) d -> p c j d", j=CH)
                wc = wu.rearrange("p (c j) w -> p c j w", j=CH)
                uc = u_c.rearrange("p (c j) d -> p c j d", j=CH)
                for dst, left, first in ((qkd, qc, 0), (gram, wc[:, :, :, 0:HD], 1)):
                    if first:
                        v.wait_ge(l_kb, CREDIT + (tt + 1) * 2)
                    for lag in range(first, CH):
                        n = CH - lag
                        tv = tmp[:, 0:NC * n * HD].rearrange("p (c j d) -> p c j d", c=NC, j=n)
                        yield o.mark(v.tensor_tensor(tv, left[:, :, lag:CH, :], kc[:, :, 0:n, :], ALU.mult))
                        yield o.mark(v.tensor_reduce(dst[:, :, lag * CH:lag * CH + (n - 1) * (CH + 1) + 1:CH + 1], tv, X, ALU.add))
                for r_ in range(1, CH):
                    tv = tmp[:, 0:NC * 2 * HD * r_].rearrange("p (c w j) -> p c w j", c=NC, j=r_)
                    yield o.mark(v.tensor_tensor(tv, wc[:, :, 0:r_, :].rearrange("p c j w -> p c w j"),
                                           gram[:, :, r_ * CH:r_ * CH + r_].unsqueeze(2).broadcast_to([P, NC, 2 * HD, r_]),
                                           ALU.mult))
                    yield o.mark(v.tensor_reduce(fold, tv, X, ALU.add))
                    yield o.mark(v.tensor_tensor(wc[:, :, r_, :], wc[:, :, r_, :], fold, ALU.subtract))
                def minus_u(c):
                    return o.mark(v.tensor_scalar(w_s[:, c % 2, :, :, HD], wc[:, c, :, HD:2 * HD], -1.0, None, ALU.mult))

                minus_u(0)
                for c in range(NC):
                    now = k_u[:, c % 2, :, :, CH]
                    o.mark(v.tensor_tensor(w_s[:, c % 2, :, :, 0:HD],
                                           wc[:, c, :, 0:HD].unsqueeze(2).broadcast_to([P, CH, HD, HD]),
                                           now.unsqueeze(1).broadcast_to([P, CH, HD, HD]), ALU.mult))
                    yield o.mark(v.tensor_copy(state[:, c, :, :], now))
                    o.mark(v.tensor_reduce(uc[:, c, :, :], w_s[:, c % 2, :, :, :], X, ALU.add, negate=True))
                    yield minus_u(c + 1) if c < NC - 1 else None
                    yield o.mark(v.tensor_tensor(k_u[:, c % 2, :, :, 0:CH],
                                                 uc[:, c, :, :].rearrange("p j v -> p v j").unsqueeze(2)
                                                 .broadcast_to([P, HD, HD, CH]),
                                                 kc[:, c, :, :].rearrange("p j k -> p k j").unsqueeze(1)
                                                 .broadcast_to([P, HD, HD, CH]), ALU.mult))
                    yield o.mark(v.tensor_reduce(k_u[:, (c + 1) % 2, :, :, CH], k_u[:, c % 2, :, :, :], X, ALU.add))
                oc = o_c.rearrange("p v (c j) -> p c j v", j=CH)
                for r_ in range(CH):
                    yield o.mark(v.tensor_tensor(o_m[:, :, :, 0:HD], state,
                                           qc[:, :, r_, :].unsqueeze(2).broadcast_to([P, NC, HD, HD]), ALU.mult))
                    yield o.mark(v.tensor_tensor(o_m[:, :, :, HD:HD + r_ + 1], uc[:, :, 0:r_ + 1, :].rearrange("p c j v -> p c v j"),
                                           qkd[:, :, r_ * CH:r_ * CH + r_ + 1].unsqueeze(2)
                                           .broadcast_to([P, NC, HD, r_ + 1]), ALU.mult))
                    if r_ == 0:
                        if wait_o is not None:
                            v.wait_ge(t2_ready, CREDIT + T2.filled("o1", wait_o))
                    r = v.tensor_reduce(oc[:, :, r_, :], o_m[:, :, :, 0:HD + r_ + 1], X, ALU.add)
                    if r_ < CH - 1:
                        yield o.mark(r)
                    else:
                        yield r.then_inc(o_ready, 1)
                o.end('DVE_SCAN')

            def advance(o, steps, n):
                for _ in range(n):
                    o.settle()
                    if next(steps, o) is o:
                        return

            def tile(i, ahead):
                o = Order(v, dve2_done, DVE2, i, CREDIT)
                s = st2
                if ahead is not None:
                    o_scan = Order(v, scan_done, DVE_SCAN, ahead, CREDIT)
                    first_steps, steps = normalise_qk(ahead, o_scan, i), scan(ahead, o_scan, i)

                def prepare(n):
                    if ahead is not None:
                        advance(o_scan, first_steps, n)

                def further(n):
                    if ahead is not None:
                        advance(o_scan, steps, n)

                def arrived2(use):
                    return arrived(T2, use, i)

                v.wait_ge(x2_loaded, CREDIT + (i + 1) * 16)
                o.between = lambda: prepare(2)
                for j in halves:
                    v.tensor_tensor(h1[:, 4 * j:4 * j + 4, :], arrived2(f"wo{j}").rearrange("p (b d) -> p b d", d=D),
                                    x2t[:, 4 * j:4 * j + 4, :], ALU.add).then_inc(t2_dve, 1)
                v.wait_ge(t2_dve, CREDIT + T2.emptied("wo1", i))
                o.step(v.tensor_tensor(hn, h1, h1, ALU.mult))
                o.step(v.tensor_reduce(s[:, 1, :], hn, X, ALU.add))
                o.step(v.tensor_scalar(s[:, 2, :], s[:, 1, :], RSQRT_SCALE / D, RSQRT_SCALE * 1e-6, ALU.mult, ALU.add))
                rsqrt(o, s[:, 5, :], s[:, 2, :], s[:, 4, :])
                v.tensor_tensor(x2t, x2t, h1, ALU.add).then_inc(hn_ready, 1)
                prepare(DVE_SCAN)
                further(W_G)
                o.between = None
                for f in halves:
                    v.wait_ge(hn_ready, CREDIT + i + 1)
                    v.tensor_tensor(y3, arrived2(f"fo{f}").rearrange("p (b d) -> p b d", d=D),
                                    x2t[:, 4 * f:4 * f + 4, :], ALU.add).then_inc(t2_dve, 1)
                    v.wait_ge(t2_dve, CREDIT + T2.emptied(f"fo{f}", i))
                    layer_norm(o, x3[:, 4 * f:4 * f + 4, :], y3, bn2, s, 4).then_inc(x3_ready, 1)
                    v.wait_ge(x3_ready, CREDIT + i * 2 + f + 1)
                    if f == 0:
                        further(W_F)
                    o.between = lambda: further(1)
                for f in halves:
                    further(W_H)
                    v.tensor_tensor(y4, arrived2(f"y{f}").rearrange("p (b d) -> p b d", d=D),
                                    x3[:, 4 * f:4 * f + 4, :], ALU.add).then_inc(t2_dve, 1)
                    v.wait_ge(t2_dve, CREDIT + T2.emptied(f"y{f}", i))
                    v.wait_ge(stored, CREDIT + i * 32 + f * 16)
                    layer_norm(o, x4, y4, bn2, s, 4).then_inc(x4_ready, 1)
                    v.wait_ge(x4_ready, CREDIT + i * 2 + f + 1)
                further(DVE_SCAN)
                o.end('DVE2')

            o = Order(v, scan_done, DVE_SCAN, 0, CREDIT)
            advance(o, normalise_qk(0, o, None), DVE_SCAN)
            advance(o, scan(0, o, None), DVE_SCAN + 10)
            with v.Fori(0, NT - 1) as i:
                tile(i, i + 1)
            tile(NT - 1, None)


QK_TURNED = (1, 3)
W_G, W_F, W_H = 20, 8, 70
W_TOTAL = 11 + 5 + 2 + 2 + 3 + 1 + 1 + 2 + 2 + 1 + 4 + 1
DVE_SETUP = 22
DVE_FRONT = 10
DVE1 = 73
DVE_SCAN = 236
DVE2 = 99

_OUTS = [((B, S, D), "float32")]


def kernel(**inputs):
    import concourse.bacc as bacc
    from concourse.bass_utils import run_bass_kernel_spmd

    nc = bacc.Bacc("TRN2", target_bir_lowering=False, num_devices=1)
    arrays, args = {}, {}
    for name, value in inputs.items():
        a = np.ascontiguousarray(value)
        arrays[f"in_{name}"] = a
        args[name] = nc.dram_tensor(f"in_{name}", a.shape, mybir.dt.from_np(a.dtype), kind="ExternalInput").ap()
    shape, dtype = _OUTS[0]
    out = nc.dram_tensor("out_0", shape, mybir.dt.from_np(np.dtype(dtype)), kind="ExternalOutput").ap()
    build(nc, args, out)
    r = run_bass_kernel_spmd(nc, [arrays], core_ids=[0])
    return r.results[0]["out_0"]
```

```python
from contextlib import ExitStack

import numpy as np
import concourse.bass as bass
from concourse import mybir

F32 = mybir.dt.float32
F32R = mybir.dt.float32r
BF16 = mybir.dt.bfloat16
I32 = mybir.dt.int32
ALU = mybir.AluOpType
ACT = mybir.ActivationFunctionType
X = mybir.AxisListType.X

P = 128
B, S, D = 8, 512, 128
NT = S // P
NH, HD = 16, 8
NG = NH // 4
NE, NS = 8, 64
N = NE * NS
HID = 512
HC = HID // P
QW = 3 * D + NH
CH = 4
NC = P // CH
LN_EPS = 1e-5
MASK = -1e30
RSQRT_SEED = 1597463007.0
RSQRT_SCALE = 64.0 / 9
CREDIT = 1


class Handoff:

    def __init__(self, ready, taken, banks, uses):
        self.ready, self.taken, self.banks = ready, taken, banks
        self.order = [u for u, _ in uses]
        self.engine = dict(uses)
        self.total = {e: sum(x == e for _, x in uses) for e in taken}
        self.ordinal = {}
        seen = {e: 0 for e in taken}
        for u, e in uses:
            seen[e] += 1
            self.ordinal[u] = seen[e]

    def bank(self, use):
        return self.banks[self.order.index(use) % len(self.banks)]

    def filled(self, use, i):
        return i * len(self.order) + self.order.index(use) + 1

    def emptied(self, use, i):
        return i * self.total[self.engine[use]] + self.ordinal[use]

    def wait_free(self, pe, use, i):
        k = self.order.index(use) - len(self.banks)
        if k >= 0:
            before = self.order[k]
            pe.wait_ge(self.taken[self.engine[before]], CREDIT + self.emptied(before, i))
        else:
            for e, n in self.total.items():
                if n:
                    pe.wait_ge(self.taken[e], CREDIT + i * n)


class Order:

    def __init__(self, eng, done, per, i, first):
        self.eng, self.sem, self.base, self.n, self.first, self.per = eng, done, i * per, 0, first, per
        self.between = None

    def mark(self, ins):
        ins.then_inc(self.sem, 1)
        self.n += 1

    def settle(self):
        self.eng.wait_ge(self.sem, self.first + self.base + self.n)

    def complete(self):
        if self.between:
            self.between()
        self.settle()

    def step(self, ins):
        self.mark(ins)
        self.complete()

    def end(self, name):
        assert self.n == self.per, (name, self.n, self.per)


def build(nc, A, out, taps=None):
    ctx = ExitStack()
    with ctx:
        def sb(name, shape, dt=F32):
            return ctx.enter_context(nc.sbuf_tensor(name, shape, dt))

        def sem(name):
            return ctx.enter_context(nc.semaphore(name))

        ps = ctx.enter_context(nc.psum_tensor("ps", [P, 8, 512], F32))

        q_rep = nc.dram_tensor("q_rep", (NH, 4, HD, S), F32, kind="Internal").ap()
        k_rep = nc.dram_tensor("k_rep", (NH, 4, HD, S), F32, kind="Internal").ap()
        proj_d = nc.dram_tensor("proj_d", (B, NT, P, QW), F32, kind="Internal").ap()
        gb_d = nc.dram_tensor("gb_d", (4, NH, HD), F32, kind="Internal").ap()
        x2_d = nc.dram_tensor("x2_d", (B, NT, P, D), F32, kind="Internal").ap()

        ident = sb("ident", [P, P])
        ident_b = sb("ident_b", [P, P], BF16)
        mask_qk = sb("mask_qk", [P, P], BF16)
        mask_kq = sb("mask_kq", [P, P], BF16)
        w_qkv = sb("w_qkv", [P, 3 * D])
        w_out = sb("w_out", [P, D])
        bias_o = sb("bias_o", [P, D])
        qk_gb = sb("qk_gb", [P, 4])
        slot_T = sb("slot_T", [P, N])
        gamma_x = sb("gamma_x", [P, 1])
        gamma_s = sb("gamma_s", [P, 1])
        e_w = sb("e_w", [P, HID + HC * D])
        e_w1 = e_w[:, 0:HID]
        e_w2 = e_w[:, HID:HID + HC * D].rearrange("p (c d) -> p c d", c=HC)
        w_mix = sb("w_mix", [P, QW])
        w_o1 = sb("w_o1", [P, D])
        ln12 = sb("ln12", [P, 2])
        w_g = sb("w_g", [P, HID])
        w_u = sb("w_u", [P, HID])
        w_d = sb("w_d", [P, HC, D])
        f_w1 = sb("f_w1", [P, HID])
        f_w2 = sb("f_w2", [P, HID])
        f_h1 = sb("f_h1", [P, HC, HID])
        f_h2 = sb("f_h2", [P, HC, HID])
        f_w3 = sb("f_w3", [P, HC, D])
        f_s = sb("f_s", [P, 4, HC])
        f_s3 = sb("f_s3", [P, 1])

        ARENA = 34 * 1024
        arena = sb("arena", [P, ARENA])
        qr = sb("qr", [P, NG, S], F32R)
        kr = sb("kr", [P, NG, S], F32R)

        class Carve:
            def __init__(self):
                self.at = 0

            def take(self, *shape):
                n = int(np.prod(shape))
                ap = arena[:, self.at:self.at + n]
                self.at += n
                assert self.at <= ARENA, self.at
                if len(shape) == 2:
                    return ap.rearrange("p (a b) -> p a b", a=shape[0])
                if len(shape) == 3:
                    return ap.rearrange("p (a b c) -> p a b c", a=shape[0], b=shape[1])
                if len(shape) == 4:
                    return ap.rearrange("p (a b c d) -> p a b c d", a=shape[0], b=shape[1], c=shape[2])
                return ap

        c0 = Carve()
        raw_w = c0.take(4, P)
        raw_slot = c0.take(4, P)
        raw_f1 = c0.take(4, P)
        raw_f2 = c0.take(4, P)
        raw_h1 = c0.take(4, HID)
        raw_h2 = c0.take(4, HID)
        raw_w3 = c0.take(HID)
        centre = c0.take(2 * NH)
        slot_sq = c0.take(4, P)
        slot_n = c0.take(4)
        slot_r = c0.take(4)
        slot_t = c0.take(4)
        ones_zeros = c0.take(2, S)

        c1 = Carve()
        xb = c1.take(NT, D)
        xbo = c1.take(NT, D)
        xT = c1.take(S)
        act_T = c1.take(S)
        qk = c1.take(NT, 2 * D)
        qk_sq = c1.take(NT, 2 * D)
        qk_n = qk_sq
        qk_var = c1.take(P)
        qk_r = c1.take(P)
        qk_t = c1.take(P)
        qk_T = c1.take(2, S)
        v_new = c1.take(NT, D)
        v_aug = c1.take(NT, NH, 32)
        pv_T = c1.take(2, S)
        neg_max = c1.take(NT, NH)
        prob = c1.take(2, 4, 1280)
        rec = c1.take(NT, 4)
        att = c1.take(NT, D)
        y1 = c1.take(NT, D)
        y_sq = c1.take(NT, D)
        x1 = c1.take(NT, D)
        x2 = c1.take(NT, D)
        st = c1.take(8, NT)
        bn1 = c1.take(NT, 6)
        xr = c1.take(NT, D)
        neg_top = c1.take(2, 4)
        z_sum = c1.take(2, 4)
        z_inv = c1.take(2, 4)
        comb = c1.take(NT, N)
        comb_T = c1.take(4, S)
        disp_T = c1.take(4, S)
        disp = c1.take(NT, N)
        slots_n = c1.take(4, D)
        slots = c1.take(N)
        h_T = comb
        done_e = c1.take(4, D)
        proj = c1.take(NT, QW)
        hilo = sb("hilo", [P, 2, 2, S], F32R)
        nm_T = sb("nm_T", [NH, S], F32R)

        c2 = Carve()
        mix = c2.take(B, QW)
        x2t = c2.take(B, D)
        l_sq = c2.take(B, 2 * D)
        u_c = e_w[:, :].rearrange("p (t d) -> p t d", d=HD)
        fold = slot_T[:, :].rearrange("p (c w) -> p c w", c=NC)
        l_var = c2.take(B * 2 * NH)
        l_r = c2.take(B * 2 * NH)
        l_t = c2.take(B * 2 * NH)
        perm = c2.take(3, HD, B * NH)
        beta_p = c2.take(B * NH)
        q_c = c2.take(P, HD)
        k_c = c2.take(P, HD)
        v_c = c2.take(P, HD)
        beta = c2.take(P)
        wu = c2.take(P, 2 * HD)
        gram = c2.take(NC, CH * CH)
        qkd = c2.take(NC, CH * CH)
        state = c2.take(NC, HD, HD)
        w_s = c2.take(2, CH, HD, HD + 1)
        k_u = c2.take(2, HD, HD, CH + 1)
        o_m = c2.take(NC, HD, HD + CH)
        tmp = o_m.rearrange("p c v k -> p (c v k)")
        o_c = v_c.rearrange("p t d -> p (t d)").rearrange("p (d t) -> p d t", t=P)
        o_tok = c2.take(B, D)
        o_T = c2.take(B, P)
        h1 = c2.take(B, D)
        hn = o_tok
        hn_T = o_T
        y3 = c2.take(4, D)
        bn2 = c2.take(4, 6)
        x3 = c2.take(B, D)
        x3_T = c2.take(2, S)
        y4 = y3
        x4 = c2.take(4, D)
        gate = c2.take(2, S)
        up = c2.take(2, S)
        hid_a = c2.take(HC, S)
        hid_b = perm.rearrange("p w d b -> p (w d b)")[:, 0:HC * S].rearrange("p (c s) -> p c s", c=HC)
        st2 = c2.take(8, B)

        w_first = sem("w_first")
        w_loaded = sem("w_loaded")
        w_ready = sem("w_ready")
        w_taken = sem("w_taken")
        w_final = sem("w_final")
        rep_init = sem("rep_init")
        dve_done = sem("dve_done")
        x_loaded = sem("x_loaded")
        x_biased = sem("x_biased")
        f_ready, f_act, f_dve = sem("f_ready"), sem("f_act"), sem("f_dve")
        g_ready, g_act, tail_done = sem("g_ready"), sem("g_act"), sem("tail_done")
        pv_ready, pv_act, pv_dve = sem("pv_ready"), sem("pv_act"), sem("pv_dve")
        t_ready, t_act, t_dve = sem("t_ready"), sem("t_act"), sem("t_dve")
        qk_squared, qk_normed = sem("qk_squared"), sem("qk_normed")
        split_done, split_stored, rep_loaded, max_placed = (
            sem("split_done"), sem("split_stored"), sem("rep_loaded"), sem("max_placed"))
        s_ready, s_taken = sem("s_ready"), sem("s_taken")
        p_ready, p_taken = sem("p_ready"), sem("p_taken")
        x1_ready, xr_ready, top_ready, inv_ready = sem("x1_ready"), sem("xr_ready"), sem("top_ready"), sem("inv_ready")
        x2_ready, proj_stored = sem("x2_ready"), sem("proj_stored")
        beta_ready = sem("beta_ready")
        v_placed, front_done = sem("v_placed"), sem("front_done")
        x2_loaded = sem("x2_loaded")
        norms_done, x2_added = sem("norms_done"), sem("x2_added")
        h_ready, h_act, h_dve, h_done = sem("h_ready"), sem("h_act"), sem("h_dve"), sem("h_done")
        l_loaded, l_squared, l_perm, l_kb = (
            sem("l_loaded"), sem("l_squared"), sem("l_perm"), sem("l_kb"))
        r_ready, r_act, scan_done = sem("r_ready"), sem("r_act"), sem("scan_done")
        t2_ready, t2_act, t2_dve = sem("t2_ready"), sem("t2_act"), sem("t2_dve")
        o_ready, x3_ready = sem("o_ready"), sem("x3_ready")
        x4_ready, stored = sem("x4_ready"), sem("stored")
        dve2_done, hn_ready = sem("dve2_done"), sem("hn_ready")
        setup_dve = sem("setup_dve")
        setup_pool = sem("setup_pool")
        gated = sem("gated")

        counted = [h_ready, h_act, h_dve, h_done, norms_done, x2_added, g_ready, g_act, tail_done, gated,
                   r_ready, r_act, scan_done, x2_loaded, f_ready, f_act, f_dve, pv_ready, pv_act, pv_dve,
                   v_placed, front_done, x_loaded, x_biased, t_ready, t_act, t_dve, qk_squared, qk_normed,
                   split_done, split_stored, rep_loaded, max_placed, s_ready, s_taken, p_ready, p_taken,
                   x1_ready, xr_ready, top_ready, inv_ready, x2_ready, proj_stored, beta_ready, l_loaded,
                   l_squared, l_perm, l_kb, t2_ready, t2_act, t2_dve, o_ready, x3_ready, x4_ready, stored,
                   dve_done, dve2_done, hn_ready]

        F = Handoff(f_ready, {"act": f_act, "dve": f_dve}, [4, 5],
                    [("xT", "act")] + [(f"qkv{t}", "act") for t in range(NT)]
                    + [("qT", "act"), ("kT", "act"), ("nmT", "dve")])
        V = Handoff(pv_ready, {"act": pv_act, "dve": pv_dve}, [6, 7],
                    [u for g in range(NG) for u in ((f"pvT{g}", "act"), (f"pv{g}", "dve"))])
        T = Handoff(t_ready, {"act": t_act, "dve": t_dve}, [0, 1, 2, 3, 6, 7],
                    [("aT", "act"), ("ao", "dve"), ("x1T", "act")]
                    + [(f"L{t}", "act") for t in range(NT)] + [(f"M{t}", "act") for t in range(4)]
                    + [(f"cT{t}", "act") for t in range(NT)] + [(f"dT{t}", "dve") for t in range(4)]
                    + [("sn", "act"), ("slots", "act")] + [(f"h{c}", "act") for c in range(HC)]
                    + [("pr", "act"), ("mo", "dve")])
        G = Handoff(g_ready, {"act": g_act}, [4, 5], [("x2T", "act")] + [(f"c{t}", "act") for t in range(NT)])
        halves = (0, 1)
        R = Handoff(r_ready, {"act": r_act}, [4, 5],
                    [(f"{n}{j}", "act") for n in "qkv" for j in halves] + [("beta", "act")])
        H = Handoff(h_ready, {"act": h_act, "dve": h_dve}, [6, 7],
                    [("o0", "act"), ("o1", "act"), ("oT0", "act"), ("oT1", "act"), ("wo0", "dve"), ("wo1", "dve"),
                     ("hT0", "act"), ("hT1", "act")])
        uses2 = []
        for f in halves:
            for c in range(HC):
                uses2 += [(f"g{f}{c}", "act"), (f"u{f}{c}", "act")]
            uses2 += [(f"fo{f}", "dve")]
        for f in halves:
            if f == 0:
                uses2 += [("x3T0", "act")]
            for c in range(HC):
                uses2 += [(f"a{f}{c}", "act"), (f"b{f}{c}", "act")]
            uses2 += [(f"m{f}{c}", "act") for c in range(HC)]
            if f == 0:
                uses2 += [("x3T1", "act")]
            uses2 += [(f"n{f}{c}", "act") for c in range(HC)] + [(f"y{f}", "dve")]
        T2 = Handoff(t2_ready, {"act": t2_act, "dve": t2_dve}, list(range(4)), uses2)

        s_units = []
        for it in range(NT):
            per = {0: 4, 1: 2}.get(it, 1)
            for g0 in range(0, NG, per):
                for q in range(4):
                    s_units.append((it, q, list(range(g0, g0 + per))))
        p_units = [(g, jt, pr) for g in range(NG) for jt in range(NT) for pr in range(2)]
        p_off = [0, 512, 896, 1152]
        PU = len(p_units) // NG
        S1, S2, S3 = 26, 40, len(s_units)

        s_jobs = [[(raw_w[:, j, :], None) for j in range(4)], [(raw_slot[:, j, :], None) for j in range(4)],
                  [(raw_f1[:, j, :], None) for j in range(4)], [(raw_f2[:, j, :], None) for j in range(4)]]
        for raw in (raw_h1, raw_h2):
            for ic in range(4):
                s_jobs.append([(raw[:, oc, ic * P:(ic + 1) * P], None) for oc in range(4)])
        s_jobs.append([(raw_w3[:, ic * P:(ic + 1) * P], None) for ic in range(4)])
        s_dst = [None, None, f_w1[:, :], f_w2[:, :]] + [f_h1[:, ic, :] for ic in range(4)] \
            + [f_h2[:, ic, :] for ic in range(4)] + [f_w3[:, :, :]]

        def arena_free(eng):
            eng.wait_ge(w_taken, len(s_jobs))
            eng.wait_ge(rep_init, 32)

        block = ctx.enter_context(nc.Block())

        @block.sync
        def _(sp):
            def load(dst, src, loaded=w_loaded, **kw):
                sp.dma_start(dst, src, **kw).then_inc(loaded, 16)

            col = lambda n: A[n].rearrange("(d o) -> d o", o=1)
            for j, n in enumerate(("qln_g", "qln_b", "kln_g", "kln_b")):
                load(gb_d[j, :, :], A[f"L0_attn_{n}"].partition_broadcast(NH), w_first)
            for j, n in enumerate(("Wq", "Wk", "Wv", "Wo")):
                load(raw_w[:, j, :], A[f"L0_attn_{n}"], w_first)
            load(raw_slot, A["L0_ffn_slot_embeds"].rearrange("e t d -> (e t) d").rearrange("(c p) d -> p c d", p=P), w_first)
            load(gamma_x[:, :], col("L0_ffn_gamma_x"), w_first)
            load(gamma_s[:, :], col("L0_ffn_gamma_slot"), w_first)
            load(bias_o[:, :], A["L0_attn_bo"].partition_broadcast(P), w_first)
            load(raw_f1, A["L1_ffn_w1_w"].rearrange("(c p) d -> p c d", p=P))
            load(raw_f2, A["L1_ffn_w2_w"].rearrange("(c p) d -> p c d", p=P))
            load(raw_h1, A["L1_ffn_h1_w"].rearrange("(c p) d -> p c d", p=P))
            load(raw_h2, A["L1_ffn_h2_w"].rearrange("(c p) d -> p c d", p=P))
            load(raw_w3, A["L1_ffn_w3_w"])
            sp.wait_ge(w_first, (W_FIRST - 1) * 16)
            load(qk_gb[:, :], gb_d.rearrange("j h d -> (h d) j"), w_first, allow_slow_non_contiguous=True)
            load(f_s3[:, :], col("L1_ffn_w3_s"))
            for j, n in enumerate(("Wq", "Wk", "Wv")):
                load(w_mix[:, j * D:(j + 1) * D], A[f"L1_attn_{n}"])
            load(w_mix[:, 3 * D:], A["L1_attn_Wb"])
            load(ln12[:, 0:1], col("L1_attn_ln1"))
            load(ln12[:, 1:2], col("L1_attn_ln2"))
            load(w_g[:, :], A["L1_attn_Wg"])
            load(w_u[:, :], A["L1_attn_Wu"])
            load(e_w1, A["L0_ffn_w1"])
            load(e_w2, A["L0_ffn_w2"].rearrange("(c p) d -> p c d", p=P))
            load(w_o1[:, :], A["L1_attn_Wo"])
            load(w_d[:, :, :], A["L1_attn_Wd"].rearrange("(c p) d -> p c d", p=P))
            for j, n in enumerate(("w1", "w2", "h1", "h2")):
                load(f_s[:, j, :], A[f"L1_ffn_{n}_s"].rearrange("(c p) -> p c", p=P), allow_slow_non_contiguous=True)
            sp.wait_ge(setup_pool, 2)
            sp.dma_start(q_rep[:, 3, :, :], ones_zeros[:, 0, :]).then_inc(rep_init, 16)
            sp.dma_start(k_rep[:, 3, :, :], ones_zeros[:, 1, :]).then_inc(rep_init, 16)
            sp.wait_ge(rep_init, 32)
            arena_free(sp)

            def load_x(b):
                sp.wait_ge(x_biased, CREDIT + b)
                sp.wait_ge(f_ready, CREDIT + b * len(F.order))
                sp.dma_start(xb, A["L0_attn_x"][bass.ds(b, 1), :, :].rearrange("o (t p) d -> p (o t) d", p=P)) \
                    .then_inc(x_loaded, 16)

            def replicate(b):
                sp.wait_ge(split_done, CREDIT + b + 1)
                for rep, j, parts in ((q_rep, 0, (0, 0, 1)), (k_rep, 1, (0, 1, 0))):
                    for c, part in enumerate(parts):
                        sp.dma_start(rep[:, c, :, :], hilo[:, j, part, :].bitcast(F32)).then_inc(split_stored, 16)
                sp.wait_ge(split_stored, CREDIT + (b + 1) * 96)
                sp.wait_ge(p_ready, CREDIT + b * len(p_units))
                for rep, dst in ((q_rep, qr), (k_rep, kr)):
                    sp.dma_start(dst[:, :, :].bitcast(F32), rep.rearrange("(g h) c d t -> (h c d) g t", g=NG)) \
                        .then_inc(rep_loaded, 16)

            def place_maxima(b):
                sp.wait_ge(f_dve, CREDIT + F.emptied("nmT", b))
                for g in range(NG):
                    sp.dma_start(qr[24:P:32, g, :].bitcast(F32), nm_T[4 * g:4 * g + 4, :].bitcast(F32)) \
                        .then_inc(max_placed, 16)

            def store(b):
                sp.wait_ge(beta_ready, CREDIT + b + 1)
                sp.dma_start(proj_d[bass.ds(b, 1), :, :, :].rearrange("o t p w -> p (o t) w"), proj) \
                    .then_inc(proj_stored, 16)
                sp.dma_start(x2_d[bass.ds(b, 1), :, :, :].rearrange("o t p w -> p (o t) w"), x2) \
                    .then_inc(proj_stored, 16)

            load_x(0)
            replicate(0)
            load_x(1)
            place_maxima(0)
            replicate(1)
            place_maxima(1)
            load_x(2)
            with sp.Fori(0, B - 3) as i:
                replicate(i + 2)
                store(i)
                place_maxima(i + 2)
                load_x(i + 3)
            replicate(B - 1)
            store(B - 3)
            place_maxima(B - 1)
            store(B - 2)
            store(B - 1)
            sp.wait_ge(proj_stored, CREDIT + B * 32)

            def load_mix(tt):
                sp.wait_ge(l_perm, CREDIT + tt * 4)
                sp.dma_start(mix, proj_d[:, bass.ds(tt, 1), :, :].rearrange("b o p w -> p (b o) w")).then_inc(l_loaded, 16)

            def load_x2(tt, last):
                sp.wait_ge(t2_dve, CREDIT + T2.emptied("fo1", last))
                sp.dma_start(x2t, x2_d[:, bass.ds(tt, 1), :, :].rearrange("b o p w -> p (b o) w")).then_inc(x2_loaded, 16)

            def store_x4(tt, f):
                sp.wait_ge(x4_ready, CREDIT + tt * 2 + f + 1)
                sp.dma_start(out[4 * f:4 * f + 4, bass.ds(tt * P, P), :].rearrange("b p d -> p b d"), x4) \
                    .then_inc(stored, 16)

            load_mix(0)
            sp.dma_start(x2t, x2_d[:, 0:1, :, :].rearrange("b o p w -> p (b o) w")).then_inc(x2_loaded, 16)
            load_mix(1)
            with sp.Fori(0, NT - 2) as i:
                load_mix(i + 2)
                load_x2(i + 1, i)
                store_x4(i, 0)
                store_x4(i, 1)
            load_x2(NT - 1, NT - 2)
            store_x4(NT - 2, 0)
            store_x4(NT - 2, 1)
            store_x4(NT - 1, 0)
            store_x4(NT - 1, 1)
            sp.wait_ge(stored, CREDIT + NT * 32)

        @block.gpsimd
        def _(g):
            for x in counted:
                g.sem_inc(x, CREDIT)
            g.memset(ones_zeros[:, 0, :], 0.0).then_inc(setup_pool, 1)
            g.memset(ones_zeros[:, 1, :], 1.0).then_inc(setup_pool, 1)
            g.memset(ident[:, :], 0.0).then_inc(setup_pool, 1)
            g.memset(mask_qk[:, :], 0.0).then_inc(setup_pool, 1)
            g.memset(mask_kq[:, :], 0.0).then_inc(setup_pool, 1)
            g.wait_ge(setup_pool, 5)
            g.affine_select(out=ident[:, :], in_=ident[:, :], compare_op=ALU.not_equal, fill=1.0,
                            base=0, pattern=[[-1, P]], channel_multiplier=1).then_inc(setup_pool, 1)
            g.affine_select(out=mask_qk[:, :], in_=mask_qk[:, :], compare_op=ALU.is_ge, fill=MASK,
                            base=0, pattern=[[-1, P]], channel_multiplier=1).then_inc(setup_pool, 1)
            g.affine_select(out=mask_kq[:, :], in_=mask_kq[:, :], compare_op=ALU.is_ge, fill=MASK,
                            base=0, pattern=[[1, P]], channel_multiplier=-1).then_inc(setup_pool, 1)
            g.wait_ge(setup_pool, 8)
            g.tensor_copy(ident_b[:, :], ident[:, :]).then_inc(setup_pool, 1)
            arena_free(g)
            g.memset(v_aug, 1.0).then_inc(setup_pool, 1)

            def squares(b):
                g.wait_ge(f_act, CREDIT + F.emptied(f"qkv{NT - 1}", b))
                g.wait_ge(qk_normed, CREDIT + b)
                g.tensor_tensor(qk_sq, qk, qk, ALU.mult).then_inc(qk_squared, 1)

            def low_parts(b):
                g.wait_ge(f_act, CREDIT + F.emptied("kT", b))
                g.tensor_tensor(hilo[:, :, 1, :], qk_T, hilo[:, :, 0, :].bitcast(F32), ALU.subtract) \
                    .then_inc(split_done, 1)

            def place_v(b):
                g.wait_ge(pv_ready, CREDIT + b * len(V.order))
                g.tensor_tensor(v_aug[:, :, :, 0:HD], v_new.rearrange("p t (h d) -> p t h d", d=HD),
                                v_aug[:, :, :, HD:HD + 1].broadcast_to([P, NT, NH, HD]), ALU.mult).then_inc(v_placed, 1)

            def add_bias(b):
                g.wait_ge(x_loaded, CREDIT + (b + 1) * 16)
                g.wait_ge(x1_ready, CREDIT + b)
                g.tensor_tensor(xbo, xb, bias_o[:, :].unsqueeze(1).broadcast_to([P, NT, D]), ALU.add) \
                    .then_inc(x_biased, 1)

            g.wait_ge(setup_pool, 10)
            squares(0)
            low_parts(0)
            place_v(0)
            add_bias(0)
            with g.Fori(0, B - 1) as i:
                squares(i + 1)
                low_parts(i + 1)
                place_v(i + 1)
                add_bias(i + 1)

            g.wait_ge(proj_stored, CREDIT + B * 32)
            def squares2(tt):
                g.wait_ge(l_loaded, CREDIT + (tt + 1) * 16)
                g.wait_ge(norms_done, CREDIT + tt * DVE_NORMS)
                g.tensor_tensor(l_sq, mix[:, :, 0:2 * D], mix[:, :, 0:2 * D], ALU.mult).then_inc(l_squared, 1)

            def unit_qk(tt, mlp):
                g.wait_ge(r_ready, CREDIT + tt * len(R.order))
                if mlp is not None:
                    g.wait_ge(t2_ready, CREDIT + T2.filled(f"n1{HC - 1}", mlp))
                g.wait_ge(norms_done, CREDIT + (tt + 1) * DVE_NORMS)
                rr = l_r.rearrange("p (b w h) -> p b w h", b=B, w=2)
                for w in range(2):
                    g.tensor_tensor(perm[:, w, :, :].rearrange("p d (b h) -> p b h d", b=B),
                                    mix[:, :, w * D:(w + 1) * D].rearrange("p b (h d) -> p b h d", d=HD),
                                    rr[:, :, w, :].unsqueeze(3).broadcast_to([P, B, NH, HD]), ALU.mult) \
                        .then_inc(l_perm, 1)

            def scale_rows(tt):
                g.wait_ge(r_act, CREDIT + R.emptied("beta", tt))
                for j, src in enumerate((k_c, v_c)):
                    g.tensor_tensor(wu[:, :, j * HD:(j + 1) * HD], src,
                                    beta.unsqueeze(2).broadcast_to([P, P, HD]), ALU.mult).then_inc(l_kb, 1)

            def normalise_h(tt):
                g.wait_ge(h_done, CREDIT + (tt + 1) * DVE_H)
                g.tensor_tensor(hn, h1, st2[:, 5, :].unsqueeze(2).broadcast_to([P, B, D]), ALU.mult) \
                    .then_inc(hn_ready, 1)

            def add_x2(tt):
                g.wait_ge(h_done, CREDIT + (tt + 1) * DVE_H)
                g.tensor_tensor(x2t, x2t, h1, ALU.add).then_inc(x2_added, 1)

            def multiply_gates(tt):
                for n, f, before in (("u", 0, None), ("u", 1, "fo0"), ("b", 0, "fo1"), ("b", 1, "y0")):
                    g.wait_ge(t2_ready, CREDIT + (T2.filled(before, tt) if before else tt * len(T2.order)))
                    for c in range(HC):
                        g.wait_ge(t2_act, CREDIT + T2.emptied(f"{n}{f}{c}", tt))
                        g.tensor_tensor(hid_a[:, c, :], up[:, c % 2, :], gate[:, c % 2, :], ALU.mult) \
                            .then_inc(gated, 1)

            def tile(i, ahead, after):
                multiply_gates(i)
                if after is not None:
                    squares2(after)
                if after is not None:
                    unit_qk(after, i)
                if ahead is not None:
                    normalise_h(ahead)
                if after is not None:
                    scale_rows(after)
                if ahead is not None:
                    add_x2(ahead)

            squares2(0)
            unit_qk(0, None)
            scale_rows(0)
            squares2(1)
            unit_qk(1, None)
            normalise_h(0)
            scale_rows(1)
            add_x2(0)
            with g.Fori(0, NT - 2) as i:
                tile(i, i + 1, i + 2)
            tile(NT - 2, NT - 1, None)
            tile(NT - 1, None, None)

        @block.tensor
        def _(pe):
            pe.wait_ge(w_final, 1)
            pe.wait_ge(setup_pool, 9)
            for j, job in enumerate(s_jobs):
                if j == 2:
                    pe.wait_ge(w_final, 2)
                if j >= 8:
                    pe.wait_ge(w_taken, j - 7)
                for k, (src, _) in enumerate(job):
                    last = pe.transpose(ps[:, j % 8, k * P:(k + 1) * P], src, ident[:, :])
                last.then_inc(w_ready, 1)
            arena_free(pe)

            def fill(R, use, b):
                R.wait_free(pe, use, b)
                return ps[:, R.bank(use), :]

            def transposes(R, use, b, srcs):
                bank = fill(R, use, b)
                for k, src in enumerate(srcs):
                    last = pe.transpose(bank[0:src.shape[1], k * P:(k + 1) * P], src, ident[:, :])
                last.then_inc(R.ready, 1)

            def transpose_x(b):
                pe.wait_ge(x_loaded, CREDIT + (b + 1) * 16)
                transposes(F, "xT", b, [xb[:, t, :] for t in range(NT)])

            def project_qkv(b):
                pe.wait_ge(f_act, CREDIT + F.emptied("xT", b))
                for t in range(NT):
                    pe.matmul(fill(F, f"qkv{t}", b)[:, 0:3 * D], xT[:, t * P:(t + 1) * P], w_qkv[:, :],
                              start=True, stop=True).then_inc(f_ready, 1)

            def transpose_qk(b):
                pe.wait_ge(qk_normed, CREDIT + b + 1)
                transposes(F, "qT", b, [qk_n[:, t, 0:D] for t in range(NT)])
                transposes(F, "kT", b, [qk_n[:, t, D:2 * D] for t in range(NT)])

            def scores_for_maxima(b, first, end, tail=None):
                if first == 0:
                    pe.wait_ge(rep_loaded, CREDIT + (b + 1) * 32)
                    pe.wait_ge(f_act, CREDIT + F.emptied("kT", b))
                    if tail is not None:
                        pe.wait_ge(g_act, CREDIT + (tail + 1) * len(G.order))
                for k in range(first, end):
                    it, q, gs = s_units[k]
                    pe.wait_ge(s_taken, CREDIT + b * len(s_units) + max(k - 1, 0))
                    w = (it + 1) * P
                    for n, gg in enumerate(gs):
                        rows = slice(32 * q, 32 * q + 32)
                        bank = ps[:, 4 + k % 2, n * w:(n + 1) * w]
                        pe.matmul(bank, qr[rows, gg, it * P:(it + 1) * P], kr[rows, gg, 0:w], start=True, stop=False)
                        last = pe.matmul(bank[:, it * P:w], ident_b[:, :], mask_qk[:, :], start=False, stop=True)
                    last.then_inc(s_ready, 1)

            def transpose_maxima(b):
                pe.wait_ge(s_taken, CREDIT + (b + 1) * len(s_units))
                transposes(F, "nmT", b, [neg_max[:, t, :] for t in range(NT)])

            def scores(b, gg, h4):
                for k in range(gg * PU + 2 * h4, gg * PU + 2 * h4 + 2):
                    _, jt, pr = p_units[k]
                    pe.wait_ge(p_taken, CREDIT + b * len(p_units) + max(k - 1, 0))
                    for n in range(2):
                        rows = slice(32 * (2 * pr + n), 32 * (2 * pr + n) + 32)
                        bank = ps[:, 2 * (k % 2) + n, 0:S - jt * P]
                        pe.matmul(bank, kr[rows, gg, jt * P:(jt + 1) * P], qr[rows, gg, jt * P:S],
                                  start=True, stop=False)
                        last = pe.matmul(bank[:, 0:P], ident_b[:, :], mask_kq[:, :], start=False, stop=True)
                    last.then_inc(p_ready, 1)

            def products(b, gg, h4):
                if h4 == 0:
                    pe.wait_ge(p_taken, CREDIT + b * len(p_units) + PU * (gg + 1))
                    fill(V, f"pvT{gg}", b)
                bank = ps[:, V.bank(f"pvT{gg}"), :]
                for jt in range(NT):
                    last = pe.matmul(bank[32 * h4:32 * h4 + 32, jt * P:S], v_aug[:, jt, 4 * gg + h4, :],
                                     prob[:, gg % 2, h4, p_off[jt]:p_off[jt] + S - jt * P],
                                     start=(jt == 0), stop=(jt == NT - 1))
                if h4 == 3:
                    last.then_inc(pv_ready, 1)

            def turn_products(b, gg):
                pe.wait_ge(pv_act, CREDIT + V.emptied(f"pvT{gg}", b))
                transposes(V, f"pv{gg}", b, [pv_T[:, gg % 2, t * P:(t + 1) * P] for t in range(NT)])

            def transpose_x2(b):
                pe.wait_ge(x2_ready, CREDIT + b + 1)
                transposes(G, "x2T", b, [x2[:, t, :] for t in range(NT)])

            def project(b):
                pe.wait_ge(g_act, CREDIT + G.emptied("x2T", b))
                for t in range(NT):
                    pe.matmul(fill(G, f"c{t}", b)[:, 0:QW], act_T[:, t * P:(t + 1) * P], w_mix[:, :],
                              start=True, stop=True).then_inc(g_ready, 1)

            def batch(i, front, tail):
                pe.wait_ge(t_act, CREDIT + i * T.total["act"])
                pe.wait_ge(t_dve, CREDIT + i * T.total["dve"])
                pe.wait_ge(max_placed, CREDIT + (i + 1) * 64)
                if front is not None:
                    transpose_x(front)
                for gg in range(NG + 1):
                    for h4 in range(4):
                        if gg < NG:
                            scores(i, gg, h4)
                        if (gg, h4) == (0, 0):
                            pe.wait_ge(v_placed, CREDIT + i + 1)
                            if front is not None:
                                project_qkv(front)
                        if gg >= 1:
                            products(i, gg - 1, h4)
                        if gg >= 2 and h4 == 1:
                            turn_products(i, gg - 2)
                        if (gg, h4) == QK_TURNED and front is not None:
                            transpose_qk(front)
                        if tail is not None and (gg, h4) == X2_TURNED:
                            if front is not None:
                                pe.wait_ge(f_act, CREDIT + F.emptied("kT", front))
                            transpose_x2(tail)
                        if tail is not None and (gg, h4) == PROJECTED:
                            project(tail)
                turn_products(i, NG - 1)
                pe.wait_ge(pv_dve, CREDIT + V.emptied(f"pv{NG - 1}", i))
                transposes(T, "aT", i, [att[:, t, :] for t in range(NT)])
                pe.wait_ge(t_act, CREDIT + T.emptied("aT", i))
                bank = fill(T, "ao", i)
                for t in range(NT):
                    last = pe.matmul(bank[:, t * P:(t + 1) * P], act_T[:, t * P:(t + 1) * P], w_out[:, :],
                                     start=True, stop=True)
                last.then_inc(t_ready, 1)
                if front is not None:
                    scores_for_maxima(front, 0, S1, tail)
                pe.wait_ge(xr_ready, CREDIT + i + 1)
                transposes(T, "x1T", i, [xr[:, t, :] for t in range(NT)])
                pe.wait_ge(t_act, CREDIT + T.emptied("x1T", i))
                for t in range(NT):
                    pe.matmul(fill(T, f"L{t}", i), act_T[:, t * P:(t + 1) * P], slot_T[:, :], start=True, stop=True) \
                        .then_inc(t_ready, 1)
                for c in range(4):
                    pe.matmul(fill(T, f"M{c}", i), slot_T[:, c * P:(c + 1) * P], act_T, start=True, stop=True) \
                        .then_inc(t_ready, 1)
                if front is not None:
                    scores_for_maxima(front, S1, S2)
                for t in range(NT):
                    pe.wait_ge(t_act, CREDIT + T.emptied(f"L{t}", i))
                    transposes(T, f"cT{t}", i, [comb[:, t, c * P:(c + 1) * P] for c in range(4)])
                for c in range(4):
                    pe.wait_ge(t_act, CREDIT + T.emptied(f"M{c}", i))
                    transposes(T, f"dT{c}", i, [disp_T[:, c, t * P:(t + 1) * P] for t in range(NT)])
                pe.wait_ge(t_dve, CREDIT + T.emptied("dT3", i))
                bank = fill(T, "sn", i)
                for c in range(4):
                    for t in range(NT):
                        last = pe.matmul(bank[:, c * P:(c + 1) * P], disp[:, t, c * P:(c + 1) * P], xr[:, t, :],
                                         start=(t == 0), stop=(t == NT - 1))
                last.then_inc(t_ready, 1)
                pe.wait_ge(t_act, CREDIT + T.emptied("sn", i))
                transposes(T, "slots", i, [slots_n[:, c, :] for c in range(4)])
                pe.wait_ge(t_act, CREDIT + T.emptied("slots", i))
                for c in range(HC):
                    pe.matmul(fill(T, f"h{c}", i), e_w1[:, c * P:(c + 1) * P], slots, start=True, stop=True) \
                        .then_inc(t_ready, 1)
                if front is not None:
                    scores_for_maxima(front, S2, S3)
                    transpose_maxima(front)
                pe.wait_ge(t_act, CREDIT + T.emptied(f"h{HC - 1}", i))
                bank = fill(T, "pr", i)
                for n in range(4):
                    for c in range(HC):
                        last = pe.matmul(bank[:, n * P:(n + 1) * P], h_T[:, c, n * P:(n + 1) * P], e_w2[:, c, :],
                                         start=(c == 0), stop=(c == HC - 1))
                last.then_inc(t_ready, 1)
                pe.wait_ge(t_act, CREDIT + T.emptied("pr", i))
                bank = fill(T, "mo", i)
                for t in range(NT):
                    for n in range(4):
                        last = pe.matmul(bank[:, t * P:(t + 1) * P], comb_T[:, n, t * P:(t + 1) * P], done_e[:, n, :],
                                         start=(n == 0), stop=(n == 3))
                last.then_inc(t_ready, 1)

            transpose_x(0)
            project_qkv(0)
            transpose_qk(0)
            scores_for_maxima(0, 0, len(s_units))
            transpose_maxima(0)
            batch(0, 1, None)
            with pe.Fori(0, B - 2) as i:
                batch(i + 1, i + 2, i)
            batch(B - 1, None, B - 2)
            transpose_x2(B - 1)
            project(B - 1)

            pe.wait_ge(t_act, CREDIT + B * T.total["act"])
            pe.wait_ge(t_dve, CREDIT + B * T.total["dve"])
            pe.wait_ge(g_act, CREDIT + B * len(G.order))
            def transpose_qkv(tt):
                pe.wait_ge(l_perm, CREDIT + (tt + 1) * 4)
                for w, n in enumerate("qkv"):
                    for j in halves:
                        transposes(R, f"{n}{j}", tt, [perm[:, w, 4 * j + d, :] for d in range(4)])
                R.wait_free(pe, "beta", tt)
                pe.transpose(ps[:, R.bank("beta"), 0:P], beta_p, ident[:, :]).then_inc(r_ready, 1)

            def project_o(tt):
                pe.wait_ge(o_ready, CREDIT + tt + 1)
                for j in halves:
                    transposes(H, f"o{j}", tt, [o_c[:, 4 * j + d, :] for d in range(4)])
                pe.wait_ge(h_act, CREDIT + H.emptied("o1", tt))
                for j in halves:
                    transposes(H, f"oT{j}", tt, [o_tok[:, 4 * j + b, :] for b in range(4)])
                for j in halves:
                    pe.wait_ge(h_act, CREDIT + H.emptied(f"oT{j}", tt))
                    bank = fill(H, f"wo{j}", tt)
                    for b in range(4):
                        last = pe.matmul(bank[:, b * P:(b + 1) * P], o_T[:, 4 * j + b, :], w_o1[:, :],
                                         start=True, stop=True)
                    last.then_inc(h_ready, 1)

            def transpose_h(tt):
                pe.wait_ge(hn_ready, CREDIT + tt + 1)
                for j in halves:
                    transposes(H, f"hT{j}", tt, [hn[:, 4 * j + b, :] for b in range(4)])

            def tile(i, ahead, after):
                def fill2(use):
                    T2.wait_free(pe, use, i)
                    return ps[:, T2.bank(use), :]

                def transposes2(use, srcs):
                    bank = fill2(use)
                    for k, src in enumerate(srcs):
                        last = pe.transpose(bank[:, k * P:(k + 1) * P], src, ident[:, :])
                    last.then_inc(t2_ready, 1)

                def by_token(use, hid, w):
                    bank = fill2(use)
                    for b in range(4):
                        for c in range(HC):
                            last = pe.matmul(bank[:, b * P:(b + 1) * P], hid[:, c, b * P:(b + 1) * P],
                                             w[:, c, :], start=(c == 0), stop=(c == HC - 1))
                    last.then_inc(t2_ready, 1)

                def by_hidden(use, w, src):
                    pe.matmul(fill2(use), w, src, start=True, stop=True).then_inc(t2_ready, 1)

                def square_layer(use, f, w, src):
                    for c in range(HC):
                        bank = fill2(f"{use}{f}{c}")
                        for k in range(HC):
                            last = pe.matmul(bank, w[:, k, c * P:(c + 1) * P], src[:, k, :],
                                             start=(k == 0), stop=(k == HC - 1))
                        last.then_inc(t2_ready, 1)

                def transpose_x3(f):
                    pe.wait_ge(x3_ready, CREDIT + i * 2 + f + 1)
                    transposes2(f"x3T{f}", [x3[:, 4 * f + b, :] for b in range(4)])

                for f in halves:
                    pe.wait_ge(h_act, CREDIT + H.emptied(f"hT{f}", i))
                    src = hn_T[:, 4 * f:4 * f + 4, :]
                    for c in range(HC):
                        by_hidden(f"g{f}{c}", w_g[:, c * P:(c + 1) * P], src)
                        by_hidden(f"u{f}{c}", w_u[:, c * P:(c + 1) * P], src)
                    pe.wait_ge(gated, CREDIT + i * 16 + 4 * (f + 1))
                    by_token(f"fo{f}", hid_a, w_d)
                for f in halves:
                    if f == 0:
                        transpose_x3(0)
                    pe.wait_ge(t2_act, CREDIT + T2.emptied(f"x3T{f}", i))
                    for c in range(HC):
                        by_hidden(f"a{f}{c}", f_w1[:, c * P:(c + 1) * P], x3_T[:, f, :])
                        by_hidden(f"b{f}{c}", f_w2[:, c * P:(c + 1) * P], x3_T[:, f, :])
                    pe.wait_ge(gated, CREDIT + i * 16 + 8 + 4 * (f + 1))
                    square_layer("m", f, f_h1, hid_a)
                    if f == 0:
                        transpose_x3(1)
                    pe.wait_ge(t2_act, CREDIT + T2.emptied(f"m{f}{HC - 1}", i))
                    square_layer("n", f, f_h2, hid_b)
                    pe.wait_ge(t2_act, CREDIT + T2.emptied(f"n{f}{HC - 1}", i))
                    by_token(f"y{f}", hid_a, f_w3)
                if ahead is not None:
                    project_o(ahead)
                if after is not None:
                    transpose_qkv(after)
                if ahead is not None:
                    transpose_h(ahead)

            transpose_qkv(0)
            project_o(0)
            transpose_qkv(1)
            transpose_h(0)
            with pe.Fori(0, NT - 2) as i:
                tile(i, i + 1, i + 2)
            tile(NT - 2, NT - 1, None)
            tile(NT - 1, None, None)

        @block.scalar
        def _(act):
            for j, dst in enumerate(s_dst):
                if dst is not None:
                    act.wait_ge(w_ready, j + 1)
                    act.wait_ge(w_taken, j)
                    src = ps[:, j % 8, :]
                    if len(dst.shape) == 3:
                        src = src.rearrange("p (a b) -> p a b", a=4)
                    act.activation(dst, src, ACT.Copy).then_inc(w_taken, 1)
            arena_free(act)
            act.wait_ge(setup_pool, 10)

            def take(R, use, b, dst, src, func=ACT.Copy, **kw):
                act.wait_ge(R.ready, CREDIT + R.filled(use, b))
                return act.activation(dst, src(ps[:, R.bank(use), :]), func, **kw)

            def take_xT(b):
                act.wait_ge(qk_normed, CREDIT + b)
                take(F, "xT", b, xT, lambda p: p).then_inc(f_act, 1)

            def take_qkv(b):
                act.wait_ge(qk_normed, CREDIT + b)
                act.wait_ge(v_placed, CREDIT + b)
                for t in range(NT):
                    take(F, f"qkv{t}", b, qk[:, t, :], lambda p: p[:, 0:2 * D])
                    act.activation(v_new[:, t, :], ps[:, F.bank(f"qkv{t}"), 2 * D:3 * D], ACT.Copy).then_inc(f_act, 1)

            def take_qk_T(b):
                act.wait_ge(split_done, CREDIT + b)
                act.wait_ge(split_stored, CREDIT + b * 96)
                for j, n in enumerate("qk"):
                    for dst in (qk_T[:, j, :], hilo[:, j, 0, :]):
                        r = take(F, f"{n}T", b, dst, lambda p: p, ACT.Identity, scale=qk_gb[:, 2 * j:2 * j + 1],
                                 bias=qk_gb[:, 2 * j + 1:2 * j + 2])
                    r.then_inc(f_act, 1)

            def exponentials(b, gg, first, end):
                for k in range(gg * PU + first, gg * PU + end):
                    _, jt, pr = p_units[k]
                    act.wait_ge(p_ready, CREDIT + b * len(p_units) + k + 1)
                    if k % PU == 0:
                        if gg >= 2:
                            act.wait_ge(pv_ready, CREDIT + V.filled(f"pvT{gg - 2}", b))
                        else:
                            act.wait_ge(pv_ready, CREDIT + b * len(V.order))
                    w = S - jt * P
                    bank = 2 * (k % 2)
                    act.activation(prob[:, gg % 2, 2 * pr:2 * pr + 2, p_off[jt]:p_off[jt] + w],
                                   ps[:, bank:bank + 2, 0:w], ACT.Exp).then_inc(p_taken, 1)

            def take_products(b, gg):
                if gg >= 2:
                    act.wait_ge(pv_ready, CREDIT + V.filled(f"pv{gg - 2}", b))
                else:
                    act.wait_ge(pv_ready, CREDIT + b * len(V.order))
                take(V, f"pvT{gg}", b, pv_T[:, gg % 2, :], lambda p: p).then_inc(pv_act, 1)

            def take_x2(b):
                act.wait_ge(t_ready, CREDIT + T.filled("mo", b))
                take(G, "x2T", b, act_T, lambda p: p).then_inc(g_act, 1)

            def take_projections(b):
                act.wait_ge(proj_stored, CREDIT + b * 32)
                act.wait_ge(x2_ready, CREDIT + b + 1)
                for t in range(NT):
                    take(G, f"c{t}", b, proj[:, t, 0:3 * D], lambda p: p[:, 0:3 * D], ACT.Silu, scale=st[:, 5, t:t + 1])
                    act.activation(proj[:, t, 3 * D:QW], ps[:, G.bank(f"c{t}"), 3 * D:QW], ACT.Tanh,
                                   scale=st[:, 7, t:t + 1]).then_inc(g_act, 1)

            def batch(i, front, tail):
                if front is not None:
                    take_xT(front)
                for gg in range(NG):
                    for h4 in range(4):
                        exponentials(i, gg, 2 * h4, 2 * h4 + 1)
                        if gg >= 2 and h4 == 0:
                            take_products(i, gg - 2)
                        exponentials(i, gg, 2 * h4 + 1, 2 * h4 + 2)
                        if (gg, h4) == (0, 0) and front is not None:
                            take_qkv(front)
                        if (gg, h4) == QK_TURNED and front is not None:
                            take_qk_T(front)
                        if tail is not None and (gg, h4) == X2_TURNED:
                            take_x2(tail)
                        if tail is not None and (gg, h4) == PROJECTED:
                            take_projections(tail)
                take_products(i, NG - 2)
                take_products(i, NG - 1)
                take(T, "aT", i, act_T, lambda p: p).then_inc(t_act, 1)
                act.wait_ge(t_ready, CREDIT + T.filled("ao", i))
                take(T, "x1T", i, act_T, lambda p: p).then_inc(t_act, 1)
                for j, (n, dst) in enumerate((("L", comb), ("M", disp_T))):
                    for t in range(4):
                        act.wait_ge(top_ready, CREDIT + i * 8 + 4 * j + t + 1)
                        take(T, f"{n}{t}", i, dst[:, t, :], lambda p: p, ACT.Exp, bias=neg_top[:, j, t:t + 1],
                             accum_out=z_sum[:, j, t:t + 1]).then_inc(t_act, 1)
                for t in range(NT):
                    take(T, f"cT{t}", i, comb_T[:, :, t * P:(t + 1) * P],
                         lambda p: p.rearrange("p (c s) -> p c s", c=4)).then_inc(t_act, 1)
                act.wait_ge(inv_ready, CREDIT + i + 1)
                for c in range(4):
                    r = take(T, "sn", i, slots_n[:, c, :], lambda p: p[:, c * P:(c + 1) * P], ACT.Identity,
                             scale=z_inv[:, 1, c:c + 1])
                r.then_inc(t_act, 1)
                take(T, "slots", i, slots, lambda p: p, ACT.Identity, scale=gamma_x[:, 0:1]).then_inc(t_act, 1)
                for c in range(HC):
                    take(T, f"h{c}", i, h_T[:, c, :], lambda p: p, ACT.Gelu).then_inc(t_act, 1)
                take(T, "pr", i, done_e, lambda p: p.rearrange("p (c s) -> p c s", c=4)).then_inc(t_act, 1)

            take_xT(0)
            take_qkv(0)
            take_qk_T(0)
            batch(0, 1, None)
            with act.Fori(0, B - 2) as i:
                batch(i + 1, i + 2, i)
            batch(B - 1, None, B - 2)
            take_x2(B - 1)
            take_projections(B - 1)

            def copy_v(tt, mlp):
                act.wait_ge(l_loaded, CREDIT + (tt + 1) * 16)
                act.wait_ge(r_ready, CREDIT + tt * len(R.order))
                if mlp is not None:
                    act.wait_ge(t2_ready, CREDIT + T2.filled(f"n1{HC - 1}", mlp))
                act.activation(perm[:, 2, :, :].rearrange("p d (b h) -> p b h d", b=B),
                               mix[:, :, 2 * D:3 * D].rearrange("p b (h d) -> p b h d", d=HD), ACT.Copy).then_inc(l_perm, 1)
                act.activation(beta_p.rearrange("p (b h) -> p b h", b=B), mix[:, :, 3 * D:QW], ACT.Copy).then_inc(l_perm, 1)

            def take_qkv2(tt):
                act.wait_ge(o_ready, CREDIT + tt)
                for n, dst in (("q", q_c), ("k", k_c), ("v", v_c)):
                    for j in halves:
                        take(R, f"{n}{j}", tt, dst[:, :, 4 * j:4 * j + 4].rearrange("p t d -> p d t"),
                             lambda b: b.rearrange("p (d t) -> p d t", d=4)).then_inc(r_act, 1)
                take(R, "beta", tt, beta, lambda b: b[:, 0:P]).then_inc(r_act, 1)

            def take_o(tt):
                for j in halves:
                    take(H, f"o{j}", tt, o_tok.rearrange("p b (h d) -> p d (b h)", d=HD)[:, 4 * j:4 * j + 4, :],
                         lambda b: b.rearrange("p (d t) -> p d t", d=4)).then_inc(h_act, 1)
                for j in halves:
                    take(H, f"oT{j}", tt, o_T[:, 4 * j:4 * j + 4, :], lambda b: b.rearrange("p (d t) -> p d t", d=4)) \
                        .then_inc(h_act, 1)

            def take_h(tt):
                for j in halves:
                    take(H, f"hT{j}", tt, hn_T[:, 4 * j:4 * j + 4, :], lambda b: b.rearrange("p (d t) -> p d t", d=4)) \
                        .then_inc(h_act, 1)

            def tile(i, ahead, after):
                def take2(use, dst, src=lambda b: b, func=ACT.Copy, **kw):
                    act.wait_ge(t2_ready, CREDIT + T2.filled(use, i))
                    return act.activation(dst, src(ps[:, T2.bank(use), :]), func, **kw)

                def gates(n, m, f, k0, scales):
                    for c in range(HC):
                        act.wait_ge(gated, CREDIT + i * 16 + max(k0 + c - 1, 0))
                        kw = [{"scale": f_s[:, j, c:c + 1]} if scales else {} for j in (0, 1)]
                        take2(f"{n}{f}{c}", gate[:, c % 2, :], func=ACT.Silu, **kw[0]).then_inc(t2_act, 1)
                        take2(f"{m}{f}{c}", up[:, c % 2, :], func=ACT.Identity, **kw[1]).then_inc(t2_act, 1)

                def gelus(use, f, j, dst):
                    for c in range(HC):
                        take2(f"{use}{f}{c}", dst[:, c, :], func=ACT.Gelu, scale=f_s[:, j, c:c + 1]).then_inc(t2_act, 1)

                for f in halves:
                    gates("g", "u", f, 4 * f, False)
                for f in halves:
                    if f == 0:
                        take2("x3T0", x3_T[:, 0, :]).then_inc(t2_act, 1)
                    gates("a", "b", f, 8 + 4 * f, True)
                    gelus("m", f, 2, hid_b)
                    if f == 0:
                        take2("x3T1", x3_T[:, 1, :]).then_inc(t2_act, 1)
                    gelus("n", f, 3, hid_a)
                if ahead is not None:
                    take_o(ahead)
                if after is not None:
                    copy_v(after, i)
                    take_qkv2(after)
                if ahead is not None:
                    take_h(ahead)

            act.wait_ge(proj_stored, CREDIT + B * 32)
            copy_v(0, None)
            take_qkv2(0)
            take_o(0)
            copy_v(1, None)
            take_qkv2(1)
            take_h(0)
            with act.Fori(0, NT - 2) as i:
                tile(i, i + 1, i + 2)
            tile(NT - 2, NT - 1, None)
            tile(NT - 1, None, None)

        @block.vector
        def _(v):
            def rsqrt_steps(o, y, x, t):
                yield o.mark(v.tensor_scalar(y.bitcast(I32), x.bitcast(I32), -0.5, RSQRT_SEED, ALU.mult, ALU.add))
                yield o.mark(v.tensor_tensor(t, y, y, ALU.mult))
                yield o.mark(v.scalar_tensor_tensor(t, t, -0.5, x, ALU.mult, ALU.mult))
                yield o.mark(v.scalar_tensor_tensor(y, t, 1.5, y, ALU.add, ALU.mult))
                yield o.mark(v.tensor_tensor(t, y, y, ALU.mult))
                yield o.mark(v.tensor_tensor(t, t, x, ALU.mult))
                yield o.mark(v.scalar_tensor_tensor(t, t, -10.0 / 3, t, ALU.add, ALU.mult))
                yield o.mark(v.scalar_tensor_tensor(y, t, 5.0, y, ALU.add, ALU.mult))

            def rsqrt(o, y, x, t):
                for _ in rsqrt_steps(o, y, x, t):
                    o.complete()

            def layer_norm(o, dst, y, stats, s, n):
                for t in range(n):
                    o.mark(v.bn_stats(stats[:, t, :], y[:, t, :]))
                o.complete()
                mean_e, mean_o = stats[:, 0:n, 1], stats[:, 0:n, 4]
                o.mark(v.tensor_tensor(s[:, 0, 0:n], mean_e, mean_o, ALU.add))
                o.mark(v.tensor_tensor(s[:, 1, 0:n], mean_e, mean_o, ALU.subtract))
                o.step(v.tensor_tensor(s[:, 2, 0:n], stats[:, 0:n, 2], stats[:, 0:n, 5], ALU.add))
                o.mark(v.tensor_scalar(s[:, 0, 0:n], s[:, 0, 0:n], 0.5, None, ALU.mult))
                o.mark(v.scalar_tensor_tensor(s[:, 1, 0:n], s[:, 1, 0:n], 0.25 * RSQRT_SCALE, s[:, 1, 0:n],
                                              ALU.mult, ALU.mult))
                o.step(v.tensor_scalar(s[:, 2, 0:n], s[:, 2, 0:n], RSQRT_SCALE / D, RSQRT_SCALE * LN_EPS,
                                       ALU.mult, ALU.add))
                o.step(v.tensor_tensor(s[:, 2, 0:n], s[:, 2, 0:n], s[:, 1, 0:n], ALU.add))
                rsqrt(o, s[:, 3, 0:n], s[:, 2, 0:n], s[:, 4, 0:n])
                for t in range(n):
                    r = v.tensor_scalar(dst[:, t, :], y[:, t, :], s[:, 0, t:t + 1], s[:, 3, t:t + 1],
                                        ALU.subtract, ALU.mult)
                    if t < n - 1:
                        o.mark(r)
                return r

            def scaled(dst, y, s, n):
                return v.tensor_tensor(dst, y, s.unsqueeze(2).broadcast_to([P, n, D]), ALU.mult)

            o = Order(v, setup_dve, 0, 0, 0)
            v.wait_ge(w_first, W_FIRST * 16)
            o.step(v.tensor_tensor(slot_sq, raw_slot, raw_slot, ALU.mult))
            o.step(v.tensor_reduce(slot_n, slot_sq, X, ALU.add))
            o.step(v.tensor_scalar(slot_n, slot_n, 1e-24, RSQRT_SCALE, ALU.max, ALU.mult))
            rsqrt(o, slot_r, slot_n, slot_t)
            o.step(v.tensor_scalar(slot_r, slot_r, float(D) ** 0.5, None, ALU.mult))
            o.step(scaled(raw_slot, raw_slot, slot_r, 4))
            o.step(v.tensor_tensor(gamma_s[:, :], gamma_s[:, :], gamma_x[:, :], ALU.mult))
            v.tensor_scalar(qk_gb[:, :], qk_gb[:, :], float(D) ** -0.25, None, ALU.mult).then_inc(w_final, 1)
            v.wait_ge(w_final, 1)
            v.wait_ge(w_ready, 1)
            o.step(v.tensor_reduce(centre, ps[:, 0, 0:2 * D].rearrange("p (g d) -> p g d", d=HD), X, ALU.add))
            o.step(v.tensor_scalar(centre, centre, -1.0 / HD, None, ALU.mult))
            o.step(v.tensor_tensor(w_qkv[:, 0:2 * D].rearrange("p (g d) -> p g d", d=HD),
                                   ps[:, 0, 0:2 * D].rearrange("p (g d) -> p g d", d=HD),
                                   centre.unsqueeze(2).broadcast_to([P, 2 * NH, HD]), ALU.add))
            o.step(v.tensor_copy(w_qkv[:, 2 * D:3 * D], ps[:, 0, 2 * D:3 * D]))
            v.tensor_copy(w_out[:, :], ps[:, 0, 3 * D:4 * D]).then_inc(w_taken, 1)
            v.wait_ge(w_ready, 2)
            v.tensor_scalar(slot_T[:, :], ps[:, 1, :], gamma_s[:, 0:1], None, ALU.mult).then_inc(w_taken, 1)
            v.wait_ge(w_loaded, W_REST * 16)
            o.mark(v.tensor_scalar(raw_w3, raw_w3, f_s3[:, 0:1], None, ALU.mult))
            o.mark(v.tensor_scalar(w_mix[:, :], w_mix[:, :], ln12[:, 0:1], None, ALU.mult))
            o.step(v.tensor_scalar(w_g[:, :], w_g[:, :], ln12[:, 1:2], None, ALU.mult))
            v.tensor_scalar(w_u[:, :], w_u[:, :], ln12[:, 1:2], None, ALU.mult).then_inc(w_final, 1)
            assert o.n == DVE_SETUP, ('DVE_SETUP', o.n, 0)
            arena_free(v)

            def arrived(R, use, b):
                v.wait_ge(R.ready, CREDIT + R.filled(use, b))
                return ps[:, R.bank(use), :]

            def norms(b):
                o = Order(v, front_done, DVE_FRONT, b, CREDIT)
                v.wait_ge(qk_squared, CREDIT + b + 1)
                o.step(v.tensor_reduce(qk_var, qk_sq.rearrange("p t (g d) -> p (t g) d", d=HD), X, ALU.add))
                o.step(v.tensor_scalar(qk_var, qk_var, RSQRT_SCALE / HD, RSQRT_SCALE * LN_EPS, ALU.mult, ALU.add))
                rsqrt(o, qk_r, qk_var, qk_t)
                v.tensor_tensor(qk_n.rearrange("p t (g d) -> p (t g) d", d=HD),
                                qk.rearrange("p t (g d) -> p (t g) d", d=HD),
                                qk_r.unsqueeze(2).broadcast_to([P, P, HD]), ALU.mult).then_inc(qk_normed, 1)
                o.end('DVE_FRONT')

            def maximum(b, k):
                it, q, gs = s_units[k]
                v.wait_ge(s_ready, CREDIT + b * len(s_units) + k + 1)
                w = (it + 1) * P
                v.tensor_reduce(neg_max[:, it, 4 * gs[0] + q:4 * gs[-1] + q + 1:4],
                                ps[:, 4 + k % 2, 0:len(gs) * w].rearrange("p (n w) -> p n w", w=w),
                                X, ALU.max, negate=True).then_inc(s_taken, 1)

            def take_maxima(b):
                v.wait_ge(max_placed, CREDIT + b * 64)
                v.tensor_copy(nm_T[:, :], arrived(F, "nmT", b)[0:NH, :]).then_inc(f_dve, 1)

            def finish(b):
                o = Order(v, tail_done, DVE_TAIL, b, CREDIT)
                s = st
                v.wait_ge(proj_stored, CREDIT + b * 32)
                o.step(layer_norm(o, x2, y1, bn1, s, NT))
                o.step(v.tensor_tensor(y_sq, x2, x2, ALU.mult))
                o.step(v.tensor_reduce(s[:, 1, :], y_sq, X, ALU.add))
                o.step(v.tensor_scalar(s[:, 2, :], s[:, 1, :], RSQRT_SCALE / D, RSQRT_SCALE * 1e-6, ALU.mult, ALU.add))
                rsqrt(o, s[:, 5, :], s[:, 2, :], s[:, 4, :])
                v.tensor_scalar(s[:, 7, :], s[:, 5, :], 0.5, None, ALU.mult).then_inc(x2_ready, 1)
                o.end('DVE_TAIL')

            def finish_beta(b):
                v.wait_ge(g_act, CREDIT + (b + 1) * len(G.order))
                v.tensor_scalar(proj[:, :, 3 * D:QW], proj[:, :, 3 * D:QW], 0.5, 0.5, ALU.mult, ALU.add) \
                    .then_inc(beta_ready, 1)

            def batch(i, front, tail):
                o = Order(v, dve_done, DVE1, i, CREDIT)
                s = st
                reduced = 0

                def reduce_to(end):
                    nonlocal reduced
                    if front is not None:
                        for k in range(reduced, end):
                            maximum(front, k)
                        reduced = max(end, reduced)

                if tail is not None:
                    finish(tail)
                if front is not None:
                    norms(front)
                for g in range(NG):
                    pv = arrived(V, f"pv{g}", i).rearrange("p (t h d) -> p t h d", t=NT, h=4)
                    o.step(v.reciprocal(rec, pv[:, :, :, HD]))
                    if g == 0:
                        v.wait_ge(t_ready, CREDIT + i * len(T.order))
                    v.tensor_tensor(att[:, :, g * 32:(g + 1) * 32].rearrange("p t (h d) -> p t h d", d=HD),
                                    pv[:, :, :, 0:HD], rec.unsqueeze(3).broadcast_to([P, NT, 4, HD]),
                                    ALU.mult).then_inc(pv_dve, 1)
                    v.wait_ge(pv_dve, CREDIT + V.emptied(f"pv{g}", i))
                if tail is not None:
                    finish_beta(tail)
                v.wait_ge(x_biased, CREDIT + i + 1)
                v.tensor_tensor(y1, arrived(T, "ao", i).rearrange("p (t d) -> p t d", d=D), xbo, ALU.add).then_inc(t_dve, 1)
                v.wait_ge(t_dve, CREDIT + T.emptied("ao", i))
                o.between = lambda: reduce_to(min(reduced + 1, S1))
                layer_norm(o, x1, y1, bn1, s, NT).then_inc(x1_ready, 1)
                v.wait_ge(x1_ready, CREDIT + i + 1)
                o.step(v.tensor_tensor(y_sq, x1, x1, ALU.mult))
                o.step(v.tensor_reduce(s[:, 1, :], y_sq, X, ALU.add))
                o.step(v.tensor_scalar(s[:, 1, :], s[:, 1, :], 1e-24, RSQRT_SCALE, ALU.max, ALU.mult))
                rsqrt(o, s[:, 3, :], s[:, 1, :], s[:, 4, :])
                o.step(v.tensor_scalar(s[:, 6, :], s[:, 3, :], float(D) ** 0.5, None, ALU.mult))
                o.between = None
                reduce_to(S1)
                scaled(xr, x1, s[:, 6, :], NT).then_inc(xr_ready, 1)
                for j, n in enumerate("LM"):
                    for t in range(4):
                        v.tensor_reduce(neg_top[:, j, t:t + 1], arrived(T, f"{n}{t}", i), X, ALU.max, negate=True) \
                            .then_inc(top_ready, 1)
                reduce_to(S2)
                v.wait_ge(t_act, CREDIT + T.emptied("M3", i))
                v.reciprocal(z_inv, z_sum).then_inc(inv_ready, 1)
                for c in range(4):
                    v.tensor_copy(disp[:, :, c * P:(c + 1) * P],
                                  arrived(T, f"dT{c}", i).rearrange("p (t n) -> p t n", t=NT)).then_inc(t_dve, 1)
                if front is not None:
                    reduce_to(S3)
                    take_maxima(front)
                v.wait_ge(inv_ready, CREDIT + i + 1)
                v.tensor_tensor(y1, arrived(T, "mo", i).rearrange("p (t d) -> p t d", d=D),
                                z_inv[:, 0, :].unsqueeze(2).broadcast_to([P, NT, D]), ALU.mult).then_inc(t_dve, 1)
                v.wait_ge(t_dve, CREDIT + T.emptied("mo", i))
                o.step(v.tensor_tensor(y1, y1, x1, ALU.add))
                o.end('DVE1')

            norms(0)
            for k in range(len(s_units)):
                maximum(0, k)
            take_maxima(0)
            batch(0, 1, None)
            with v.Fori(0, B - 2) as i:
                batch(i + 1, i + 2, i)
            batch(B - 1, None, B - 2)
            finish(B - 1)
            finish_beta(B - 1)

            v.wait_ge(proj_stored, CREDIT + B * 32)
            v.memset(k_u[:, 0, :, :, CH], 0.0).then_inc(setup_dve, 1)
            v.wait_ge(setup_dve, DVE_SETUP + 1)
            def norms_qk(tt, o):
                v.wait_ge(l_squared, CREDIT + tt + 1)
                v.wait_ge(l_perm, CREDIT + tt * 4)
                yield o.mark(v.tensor_reduce(l_var, l_sq.rearrange("p b (g d) -> p (b g) d", d=HD), X, ALU.add))
                yield o.mark(v.tensor_scalar(l_var, l_var, 1e-6, RSQRT_SCALE, ALU.add, ALU.mult))
                yield from rsqrt_steps(o, l_r, l_var, l_t)
                o.end('DVE_NORMS')

            def scan(tt, o, last):
                v.wait_ge(r_act, CREDIT + R.emptied("k1", tt))
                kc = k_c.rearrange("p (c j) d -> p c j d", j=CH)
                qc = q_c.rearrange("p (c j) d -> p c j d", j=CH)
                wc = wu.rearrange("p (c j) w -> p c j w", j=CH)
                uc = u_c.rearrange("p (c j) d -> p c j d", j=CH)
                for dst, left, first in ((qkd, qc, 0), (gram, wc[:, :, :, 0:HD], 1)):
                    if first:
                        v.wait_ge(l_kb, CREDIT + (tt + 1) * 2)
                    for lag in range(first, CH):
                        n = CH - lag
                        tv = tmp[:, 0:NC * n * HD].rearrange("p (c j d) -> p c j d", c=NC, j=n)
                        yield o.mark(v.tensor_tensor(tv, left[:, :, lag:CH, :], kc[:, :, 0:n, :], ALU.mult))
                        yield o.mark(v.tensor_reduce(dst[:, :, lag * CH:lag * CH + (n - 1) * (CH + 1) + 1:CH + 1], tv, X, ALU.add))
                for r_ in range(1, CH):
                    tv = tmp[:, 0:NC * 2 * HD * r_].rearrange("p (c w j) -> p c w j", c=NC, j=r_)
                    yield o.mark(v.tensor_tensor(tv, wc[:, :, 0:r_, :].rearrange("p c j w -> p c w j"),
                                           gram[:, :, r_ * CH:r_ * CH + r_].unsqueeze(2).broadcast_to([P, NC, 2 * HD, r_]),
                                           ALU.mult))
                    yield o.mark(v.tensor_reduce(fold, tv, X, ALU.add))
                    yield o.mark(v.tensor_tensor(wc[:, :, r_, :], wc[:, :, r_, :], fold, ALU.subtract))
                def minus_u(c):
                    return o.mark(v.tensor_scalar(w_s[:, c % 2, :, :, HD], wc[:, c, :, HD:2 * HD], -1.0, None, ALU.mult))

                minus_u(0)
                for c in range(NC):
                    now = k_u[:, c % 2, :, :, CH]
                    o.mark(v.tensor_tensor(w_s[:, c % 2, :, :, 0:HD],
                                           wc[:, c, :, 0:HD].unsqueeze(2).broadcast_to([P, CH, HD, HD]),
                                           now.unsqueeze(1).broadcast_to([P, CH, HD, HD]), ALU.mult))
                    yield o.mark(v.tensor_copy(state[:, c, :, :], now))
                    o.mark(v.tensor_reduce(uc[:, c, :, :], w_s[:, c % 2, :, :, :], X, ALU.add, negate=True))
                    yield minus_u(c + 1) if c < NC - 1 else None
                    yield o.mark(v.tensor_tensor(k_u[:, c % 2, :, :, 0:CH],
                                                 uc[:, c, :, :].rearrange("p j v -> p v j").unsqueeze(2)
                                                 .broadcast_to([P, HD, HD, CH]),
                                                 kc[:, c, :, :].rearrange("p j k -> p k j").unsqueeze(1)
                                                 .broadcast_to([P, HD, HD, CH]), ALU.mult))
                    yield o.mark(v.tensor_reduce(k_u[:, (c + 1) % 2, :, :, CH], k_u[:, c % 2, :, :, :], X, ALU.add))
                oc = o_c.rearrange("p v (c j) -> p c j v", j=CH)
                for r_ in range(CH):
                    yield o.mark(v.tensor_tensor(o_m[:, :, :, 0:HD], state,
                                           qc[:, :, r_, :].unsqueeze(2).broadcast_to([P, NC, HD, HD]), ALU.mult))
                    yield o.mark(v.tensor_tensor(o_m[:, :, :, HD:HD + r_ + 1], uc[:, :, 0:r_ + 1, :].rearrange("p c j v -> p c v j"),
                                           qkd[:, :, r_ * CH:r_ * CH + r_ + 1].unsqueeze(2)
                                           .broadcast_to([P, NC, HD, r_ + 1]), ALU.mult))
                    if r_ == 0:
                        if last is not None:
                            v.wait_ge(h_ready, CREDIT + H.filled("o1", last))
                    r = v.tensor_reduce(oc[:, :, r_, :], o_m[:, :, :, 0:HD + r_ + 1], X, ALU.add)
                    if r_ < CH - 1:
                        yield o.mark(r)
                    else:
                        yield r.then_inc(o_ready, 1)
                o.end('DVE_SCAN')

            def advance(o, steps, n):
                for _ in range(n):
                    o.settle()
                    if next(steps, o) is o:
                        return

            def residual_h(tt):
                o = Order(v, h_done, DVE_H, tt, CREDIT)
                s = st2
                v.wait_ge(x2_loaded, CREDIT + (tt + 1) * 16)
                for j in halves:
                    v.tensor_tensor(h1[:, 4 * j:4 * j + 4, :], arrived(H, f"wo{j}", tt).rearrange("p (b d) -> p b d", d=D),
                                    x2t[:, 4 * j:4 * j + 4, :], ALU.add).then_inc(h_dve, 1)
                v.wait_ge(h_dve, CREDIT + H.emptied("wo1", tt))
                o.step(v.tensor_tensor(hn, h1, h1, ALU.mult))
                o.step(v.tensor_reduce(s[:, 1, :], hn, X, ALU.add))
                o.step(v.tensor_scalar(s[:, 2, :], s[:, 1, :], RSQRT_SCALE / D, RSQRT_SCALE * 1e-6, ALU.mult, ALU.add))
                rsqrt(o, s[:, 5, :], s[:, 2, :], s[:, 4, :])
                o.end('DVE_H')

            def tile(i, ahead, after):
                o = Order(v, dve2_done, DVE2, i, CREDIT)
                s = st2
                if ahead is not None:
                    o_scan = Order(v, scan_done, DVE_SCAN, ahead, CREDIT)
                    steps = scan(ahead, o_scan, i)

                def further(n):
                    if ahead is not None:
                        advance(o_scan, steps, n)

                def arrived2(use):
                    return arrived(T2, use, i)

                further(W_G)
                o.between = None
                for f in halves:
                    v.wait_ge(x2_added, CREDIT + i + 1)
                    v.tensor_tensor(y3, arrived2(f"fo{f}").rearrange("p (b d) -> p b d", d=D),
                                    x2t[:, 4 * f:4 * f + 4, :], ALU.add).then_inc(t2_dve, 1)
                    v.wait_ge(t2_dve, CREDIT + T2.emptied(f"fo{f}", i))
                    layer_norm(o, x3[:, 4 * f:4 * f + 4, :], y3, bn2, s, 4).then_inc(x3_ready, 1)
                    v.wait_ge(x3_ready, CREDIT + i * 2 + f + 1)
                    if f == 0:
                        further(W_F)
                    o.between = lambda: further(1)
                for f in halves:
                    further(W_H if f == 0 else DVE_SCAN)
                    if f == 1:
                        o.between = None
                        if after is not None:
                            o_norms = Order(v, norms_done, DVE_NORMS, after, CREDIT)
                            norm_steps = norms_qk(after, o_norms)
                            o.between = lambda: advance(o_norms, norm_steps, 1)
                    v.tensor_tensor(y4, arrived2(f"y{f}").rearrange("p (b d) -> p b d", d=D),
                                    x3[:, 4 * f:4 * f + 4, :], ALU.add).then_inc(t2_dve, 1)
                    v.wait_ge(t2_dve, CREDIT + T2.emptied(f"y{f}", i))
                    v.wait_ge(stored, CREDIT + i * 32 + f * 16)
                    layer_norm(o, x4, y4, bn2, s, 4).then_inc(x4_ready, 1)
                    v.wait_ge(x4_ready, CREDIT + i * 2 + f + 1)
                if after is not None:
                    advance(o_norms, norm_steps, DVE_NORMS + 1)
                if ahead is not None:
                    residual_h(ahead)
                o.end('DVE2')

            o = Order(v, scan_done, DVE_SCAN, 0, CREDIT)
            o_norms = Order(v, norms_done, DVE_NORMS, 0, CREDIT)
            advance(o_norms, norms_qk(0, o_norms), DVE_NORMS + 1)
            advance(o, scan(0, o, None), DVE_SCAN + 10)
            o_norms = Order(v, norms_done, DVE_NORMS, 1, CREDIT)
            advance(o_norms, norms_qk(1, o_norms), DVE_NORMS + 1)
            residual_h(0)
            with v.Fori(0, NT - 2) as i:
                tile(i, i + 1, i + 2)
            tile(NT - 2, NT - 1, None)
            tile(NT - 1, None, None)


QK_TURNED = (1, 3)
X2_TURNED, PROJECTED = (2, 1), (3, 0)
W_G, W_F, W_H = 20, 8, 80
W_FIRST = 4 + 4 + 1 + 2 + 1 + 1
W_REST = 2 + 2 + 2 + 4 + 2 + 2 + 2 + 2 + 4
DVE_SETUP = 21
DVE_FRONT = 10
DVE_TAIL = 34
DVE1 = 39
DVE_SCAN = 226
DVE_NORMS = 10
DVE2 = 88
DVE_H = 11

_OUTS = [((B, S, D), "float32")]


def kernel(**inputs):
    import concourse.bacc as bacc
    from concourse.bass_utils import run_bass_kernel_spmd

    nc = bacc.Bacc("TRN2", target_bir_lowering=False, num_devices=1)
    arrays, args = {}, {}
    for name, value in inputs.items():
        a = np.ascontiguousarray(value)
        arrays[f"in_{name}"] = a
        args[name] = nc.dram_tensor(f"in_{name}", a.shape, mybir.dt.from_np(a.dtype), kind="ExternalInput").ap()
    shape, dtype = _OUTS[0]
    out = nc.dram_tensor("out_0", shape, mybir.dt.from_np(np.dtype(dtype)), kind="ExternalOutput").ap()
    build(nc, args, out)
    r = run_bass_kernel_spmd(nc, [arrays], core_ids=[0])
    return r.results[0]["out_0"]
```
